# Optimizing a Trainium2 kernel written in Bass

```python
import numpy as np
import jax
import jax.numpy as jnp

def _softmax(x, axis=-1):
    return jax.nn.softmax(x, axis=axis)

def _gelu(x):
    return jax.nn.gelu(x, approximate=True)

def _silu(x):
    return jax.nn.silu(x)

def _sigmoid(x):
    return jax.nn.sigmoid(x)

def _layernorm(x, axis=-1, eps=1e-05):
    m = jnp.mean(x, axis=axis, keepdims=True)
    v = jnp.var(x, axis=axis, keepdims=True)
    return (x - m) / jnp.sqrt(v + eps)

def _scatter_add(tgt, idx, src, axis=0):
    return tgt.at[idx].add(src)

def _segment_sum(src, seg, n):
    return jax.ops.segment_sum(src, seg, n)
kernel_name = 'mk_perceiver_d2_seqx_r4_59e694'

def setup_inputs(seed: int=0):
    np.random.seed(seed)
    _w = jnp.asarray

    def _rec_inputs():
        import jax
        import jax.numpy as jnp
        _rk = jax.random.key(seed)
        x = -0.0002928 + 1 * jax.random.normal(jax.random.fold_in(_rk, 1), (1, 128, 256), jnp.float32)
        _lenS = 128 - jax.random.randint(jax.random.fold_in(_rk, 7), (1,), 0, max(1, 128 // 4) + 1, jnp.int32)
        _lenS2 = 12544 - jax.random.randint(jax.random.fold_in(_rk, 8), (1,), 0, max(1, 12544 // 4) + 1, jnp.int32)
        _ctx_1024P = jax.random.normal(jax.random.fold_in(_rk, 11), (1, 16, 256), jnp.float32)
        _ctx_1024c = jax.random.dirichlet(jax.random.fold_in(_rk, 511), 0.3 * jnp.ones((16,), jnp.float32), (1, 12544))
        _ctx_1024t = jnp.einsum('bsk,bkd->bsd', _ctx_1024c, _ctx_1024P)
        _ctx_1024t = _ctx_1024t * jax.lax.rsqrt(jnp.mean(jnp.square(_ctx_1024t)) + 1e-12) * 0.953939
        ctx_1024 = -1.39393e-06 + 0.999914 * (_ctx_1024t + 0.3 * jax.random.normal(jax.random.fold_in(_rk, 611), (1, 12544, 256), jnp.float32))
        _validS = jnp.arange(128)[None, :] < _lenS[:, None]
        _validS2 = jnp.arange(12544)[None, :] < _lenS2[:, None]
        _causal = jnp.tril(jnp.ones((128, 128), dtype=bool))
        mask_Bx1xSxS2_ik1 = jnp.where(jnp.broadcast_to(_validS2[:, None, None, :], (1, 1, 128, 12544)), 1, 0).astype(jnp.int32)
        return (x, ctx_1024, mask_Bx1xSxS2_ik1)
    x, ctx_1024, mask_Bx1xSxS2_ik1 = _rec_inputs()

    def _L0_xattn_setup():
        import jax, jax.numpy as jnp
        import numpy as np
        D_MODEL = 256
        NHEADS = 16
        D_K = D_MODEL // NHEADS

        def _split_heads(x):
            B, S, _ = x.shape
            return x.reshape(B, S, NHEADS, D_K).transpose(0, 2, 1, 3)
        key = jax.random.key(seed)
        ks = jax.random.split(key, 12)
        B, S = (2, 512)
        scale = 1.0 / np.sqrt(D_MODEL)
        inp = {'query': jax.random.normal(ks[0], (B, S, D_MODEL), dtype=jnp.float32), 'key': jax.random.normal(ks[1], (B, S, D_MODEL), dtype=jnp.float32), 'value': jax.random.normal(ks[2], (B, S, D_MODEL), dtype=jnp.float32), 'mask': jax.random.randint(ks[3], (B, 1, S, S), 0, 2, dtype=jnp.int32), 'Wq': jax.random.normal(ks[4], (D_MODEL, D_MODEL), dtype=jnp.float32) * scale, 'bq': jnp.zeros((D_MODEL,), dtype=jnp.float32), 'Wk': jax.random.normal(ks[5], (D_MODEL, D_MODEL), dtype=jnp.float32) * scale, 'bk': jnp.zeros((D_MODEL,), dtype=jnp.float32), 'Wv': jax.random.normal(ks[6], (D_MODEL, D_MODEL), dtype=jnp.float32) * scale, 'bv': jnp.zeros((D_MODEL,), dtype=jnp.float32), 'Wo': jax.random.normal(ks[7], (D_MODEL, D_MODEL), dtype=jnp.float32) * scale, 'bo': jnp.zeros((D_MODEL,), dtype=jnp.float32)}
        return inp
    _L0_xattn_all = _L0_xattn_setup()
    _L0_xattn_in = {k: v for k, v in _L0_xattn_all.items() if k in ('Wq', 'bq', 'Wk', 'bk', 'Wv', 'bv', 'Wo', 'bo')}
    del _L0_xattn_all

    def _L0_attn_setup():
        import jax, jax.numpy as jnp
        import numpy as np
        D_MODEL = 256
        N_HEADS = 16
        LATENT_HEADS = 8
        LATENT_DIM = 128
        N_LATENTS = 64
        WINDOW = 64
        HEAD_DIM = D_MODEL // N_HEADS
        LAT_HD = LATENT_DIM // LATENT_HEADS
        B, S = (2, 1024)

        def _pool_to_latents(x):
            Bx, Sx, C = x.shape
            chunk = max(1, Sx // N_LATENTS)
            return x.reshape(Bx, N_LATENTS, chunk, C).mean(axis=2)

        def _local_window_attn(Q, K, V):
            Bx, H, Sx, D = Q.shape
            W = WINDOW
            nb = Sx // W
            Qb = Q.reshape(Bx, H, nb, W, D)
            Kp = jnp.pad(K, ((0, 0), (0, 0), (W, 0), (0, 0))).reshape(Bx, H, nb + 1, W, D)
            Vp = jnp.pad(V, ((0, 0), (0, 0), (W, 0), (0, 0))).reshape(Bx, H, nb + 1, W, D)
            Kw = jnp.concatenate([Kp[:, :, :-1], Kp[:, :, 1:]], axis=3)
            Vw = jnp.concatenate([Vp[:, :, :-1], Vp[:, :, 1:]], axis=3)
            i = jnp.arange(W)[:, None]
            j = jnp.arange(2 * W)[None, :]
            base = (j > i) & (j <= i + W)
            blk0 = (jnp.arange(nb) > 0)[:, None, None] | (j >= W)[None, :, :]
            mask = base[None, :, :] & blk0
            sc = jnp.einsum('bhnid,bhnjd->bhnij', Qb, Kw) / np.sqrt(D).astype(np.float32)
            sc = jnp.where(mask[None, None], sc, -jnp.inf)
            p = jax.nn.softmax(sc, axis=-1)
            out = jnp.einsum('bhnij,bhnjd->bhnid', p, Vw)
            return out.reshape(Bx, H, Sx, D)
        key = jax.random.key(seed)
        ks = jax.random.split(key, 11)
        std = 0.02
        w = lambda k, shp: jax.random.normal(k, shp, jnp.float32) * std
        return {'x': jax.random.normal(ks[0], (B, S, D_MODEL), jnp.float32), 'wq': w(ks[1], (D_MODEL, D_MODEL)), 'wk': w(ks[2], (D_MODEL, D_MODEL)), 'wv': w(ks[3], (D_MODEL, D_MODEL)), 'wgq': w(ks[4], (D_MODEL, LATENT_DIM)), 'wgk': w(ks[5], (D_MODEL, LATENT_DIM)), 'wgv': w(ks[6], (D_MODEL, LATENT_DIM)), 'r_out_w': w(ks[7], (LATENT_DIM, D_MODEL)), 'gate_local_w': w(ks[8], (N_HEADS, HEAD_DIM)), 'gate_remote_w': w(ks[9], (N_HEADS, HEAD_DIM)), 'w_out': w(ks[10], (D_MODEL, D_MODEL))}
    _L0_attn_all = _L0_attn_setup()
    _L0_attn_in = {k: v for k, v in _L0_attn_all.items() if k in ('wq', 'wk', 'wv', 'wgq', 'wgk', 'wgv', 'r_out_w', 'gate_local_w', 'gate_remote_w', 'w_out')}
    del _L0_attn_all

    def _L0_ffn_setup():
        import jax, jax.numpy as jnp
        import numpy as np
        B, P, D, D_MLP, E, K = (2, 512, 256, 1024, 8, 2)
        key = jax.random.key(seed)
        k_x, k_g, k_in, k_out = jax.random.split(key, 4)
        s_in = 1.0 / np.sqrt(D).astype(np.float32)
        s_out = 1.0 / np.sqrt(D_MLP).astype(np.float32)
        return {'x': jax.random.normal(k_x, (B, P, D), dtype=jnp.float32), 'W_gate': jax.random.normal(k_g, (D, E), dtype=jnp.float32) * s_in, 'W_in': jax.random.normal(k_in, (E, D, D_MLP), dtype=jnp.float32) * s_in, 'b_in': jnp.zeros((E, D_MLP), dtype=jnp.float32), 'W_out': jax.random.normal(k_out, (E, D_MLP, D), dtype=jnp.float32) * s_out, 'b_out': jnp.zeros((E, D), dtype=jnp.float32)}
    _L0_ffn_all = _L0_ffn_setup()
    _L0_ffn_in = {k: v for k, v in _L0_ffn_all.items() if k in ('W_gate', 'W_in', 'b_in', 'W_out', 'b_out')}
    del _L0_ffn_all

    def _L1_xattn_setup():
        import jax, jax.numpy as jnp
        import numpy as np
        DIM = 256
        HEADS = 16
        DIM_HEAD = 64
        INNER = HEADS * DIM_HEAD
        EPS = 1e-05

        def _split_heads(t):
            b, n, _ = t.shape
            return t.reshape(b, n, HEADS, DIM_HEAD).transpose(0, 2, 1, 3)
        key = jax.random.key(seed)
        ks = jax.random.split(key, 9)
        b, n, m = (2, 512, 64)
        s = DIM ** (-0.5)
        return {'x': jax.random.normal(ks[0], (b, n, DIM), jnp.float32), 'memories': jax.random.normal(ks[1], (b, m, DIM), jnp.float32), 'ln_g': jnp.ones((DIM,), jnp.float32), 'ln_b': jnp.zeros((DIM,), jnp.float32), 'Wq': jax.random.normal(ks[2], (DIM, INNER), jnp.float32) * s, 'Wkv': jax.random.normal(ks[3], (DIM, 2 * INNER), jnp.float32) * s, 'Wm': jax.random.normal(ks[4], (DIM, INNER), jnp.float32) * s, 'Wo': jax.random.normal(ks[5], (INNER, DIM), jnp.float32) * s, 'bo': jnp.zeros((DIM,), jnp.float32)}
    _L1_xattn_all = _L1_xattn_setup()
    _L1_xattn_in = {k: v for k, v in _L1_xattn_all.items() if k in ('ln_g', 'ln_b', 'Wq', 'Wkv', 'Wm', 'Wo', 'bo')}
    del _L1_xattn_all

    def _L1_attn_setup():
        import jax, jax.numpy as jnp
        import numpy as np
        N_HEADS = 16
        EPS = 1e-06

        def _phi(x):
            return jax.nn.softplus(x) + EPS

        def _reference_tuple_inner(x, Wq, Wk, Wv, Wo):
            B, T, D = x.shape
            H = N_HEADS
            dh = D // H

            def proj(W):
                y = jnp.einsum('btd,ed->bte', x, W)
                return y.reshape(B, T, H, dh).transpose(1, 0, 2, 3)
            q = proj(Wq)
            k = proj(Wk)
            v = proj(Wv)
            qf = _phi(q)
            kf = _phi(k)
            kv0 = jnp.zeros((B, H, dh, dh), dtype=x.dtype)
            z0 = jnp.zeros((B, H, dh), dtype=x.dtype)

            def step(carry, inp):
                kv, z = carry
                qt, kt, vt = inp
                kv = kv + jnp.einsum('bhd,bhe->bhde', kt, vt)
                z = z + kt
                num = jnp.einsum('bhd,bhde->bhe', qt, kv)
                den = jnp.einsum('bhd,bhd->bh', qt, z) + EPS
                return ((kv, z), num / den[..., None])
            (kv_acc, z_acc), out_t = jax.lax.scan(step, (kv0, z0), (qf, kf, v))
            out = out_t.transpose(1, 0, 2, 3).reshape(B, T, D)
            out = jnp.einsum('btd,ed->bte', out, Wo)
            return (out, kv_acc, z_acc)
        key = jax.random.key(seed)
        ks = jax.random.split(key, 5)
        D = 256
        s = 1.0 / np.sqrt(D)
        x = jax.random.normal(ks[0], (4, 1024, D), dtype=jnp.float32)
        Wq = jax.random.normal(ks[1], (D, D), dtype=jnp.float32) * s
        Wk = jax.random.normal(ks[2], (D, D), dtype=jnp.float32) * s
        Wv = jax.random.normal(ks[3], (D, D), dtype=jnp.float32) * s
        Wo = jax.random.normal(ks[4], (D, D), dtype=jnp.float32) * s
        return {'x': x, 'Wq': Wq, 'Wk': Wk, 'Wv': Wv, 'Wo': Wo}
    _L1_attn_all = _L1_attn_setup()
    _L1_attn_in = {k: v for k, v in _L1_attn_all.items() if k in ('Wq', 'Wk', 'Wv', 'Wo')}
    del _L1_attn_all

    def _L1_ffn_setup():
        import jax, jax.numpy as jnp
        import numpy as np
        D_MODEL = 256
        D_HIDDEN = 1024
        NUM_BANKS = 16
        NUM_SELECTED = 2
        key = jax.random.key(seed)
        ks = jax.random.split(key, 7)
        s = 0.02
        return {'tensor': jax.random.normal(ks[0], (4, 256, D_MODEL), dtype=jnp.float32), 'Wr': jax.random.normal(ks[1], (D_MODEL, NUM_BANKS), dtype=jnp.float32) * s, 'br': jnp.zeros((NUM_BANKS,), dtype=jnp.float32), 'W1': jax.random.normal(ks[2], (NUM_BANKS, D_MODEL, D_HIDDEN), dtype=jnp.float32) * s, 'b1': jnp.zeros((NUM_BANKS, D_HIDDEN), dtype=jnp.float32), 'W2': jax.random.normal(ks[3], (NUM_BANKS, D_HIDDEN, D_MODEL), dtype=jnp.float32) * s, 'b2': jnp.zeros((NUM_BANKS, D_MODEL), dtype=jnp.float32)}
    _L1_ffn_all = _L1_ffn_setup()
    _L1_ffn_in = {k: v for k, v in _L1_ffn_all.items() if k in ('Wr', 'br', 'W1', 'b1', 'W2', 'b2')}
    del _L1_ffn_all
    return {'x': x, 'ctx_1024': ctx_1024, 'mask_Bx1xSxS2_ik1': mask_Bx1xSxS2_ik1, 'L0_xattn_Wq': _L0_xattn_in['Wq'], 'L0_xattn_bq': _L0_xattn_in['bq'], 'L0_xattn_Wk': _L0_xattn_in['Wk'], 'L0_xattn_bk': _L0_xattn_in['bk'], 'L0_xattn_Wv': _L0_xattn_in['Wv'], 'L0_xattn_bv': _L0_xattn_in['bv'], 'L0_xattn_Wo': _L0_xattn_in['Wo'], 'L0_xattn_bo': _L0_xattn_in['bo'], 'L0_attn_wq': _L0_attn_in['wq'], 'L0_attn_wk': _L0_attn_in['wk'], 'L0_attn_wv': _L0_attn_in['wv'], 'L0_attn_wgq': _L0_attn_in['wgq'], 'L0_attn_wgk': _L0_attn_in['wgk'], 'L0_attn_wgv': _L0_attn_in['wgv'], 'L0_attn_r_out_w': _L0_attn_in['r_out_w'], 'L0_attn_gate_local_w': _L0_attn_in['gate_local_w'], 'L0_attn_gate_remote_w': _L0_attn_in['gate_remote_w'], 'L0_attn_w_out': _L0_attn_in['w_out'], 'L0_ffn_W_gate': _L0_ffn_in['W_gate'], 'L0_ffn_W_in': _L0_ffn_in['W_in'], 'L0_ffn_b_in': _L0_ffn_in['b_in'], 'L0_ffn_W_out': _L0_ffn_in['W_out'], 'L0_ffn_b_out': _L0_ffn_in['b_out'], 'L1_xattn_ln_g': _L1_xattn_in['ln_g'], 'L1_xattn_ln_b': _L1_xattn_in['ln_b'], 'L1_xattn_Wq': _L1_xattn_in['Wq'], 'L1_xattn_Wkv': _L1_xattn_in['Wkv'], 'L1_xattn_Wm': _L1_xattn_in['Wm'], 'L1_xattn_Wo': _L1_xattn_in['Wo'], 'L1_xattn_bo': _L1_xattn_in['bo'], 'L1_attn_Wq': _L1_attn_in['Wq'], 'L1_attn_Wk': _L1_attn_in['Wk'], 'L1_attn_Wv': _L1_attn_in['Wv'], 'L1_attn_Wo': _L1_attn_in['Wo'], 'L1_ffn_Wr': _L1_ffn_in['Wr'], 'L1_ffn_br': _L1_ffn_in['br'], 'L1_ffn_W1': _L1_ffn_in['W1'], 'L1_ffn_b1': _L1_ffn_in['b1'], 'L1_ffn_W2': _L1_ffn_in['W2'], 'L1_ffn_b2': _L1_ffn_in['b2']}

def reference(x, ctx_1024, mask_Bx1xSxS2_ik1, L0_xattn_Wq, L0_xattn_bq, L0_xattn_Wk, L0_xattn_bk, L0_xattn_Wv, L0_xattn_bv, L0_xattn_Wo, L0_xattn_bo, L0_attn_wq, L0_attn_wk, L0_attn_wv, L0_attn_wgq, L0_attn_wgk, L0_attn_wgv, L0_attn_r_out_w, L0_attn_gate_local_w, L0_attn_gate_remote_w, L0_attn_w_out, L0_ffn_W_gate, L0_ffn_W_in, L0_ffn_b_in, L0_ffn_W_out, L0_ffn_b_out, L1_xattn_ln_g, L1_xattn_ln_b, L1_xattn_Wq, L1_xattn_Wkv, L1_xattn_Wm, L1_xattn_Wo, L1_xattn_bo, L1_attn_Wq, L1_attn_Wk, L1_attn_Wv, L1_attn_Wo, L1_ffn_Wr, L1_ffn_br, L1_ffn_W1, L1_ffn_b1, L1_ffn_W2, L1_ffn_b2):
    import jax
    import jax.numpy as jnp

    def _L0_xattn_ref(query, key, value, mask, Wq, bq, Wk, bk, Wv, bv, Wo, bo):
        import jax, jax.numpy as jnp
        import numpy as np
        D_MODEL = 256
        NHEADS = 16
        D_K = D_MODEL // NHEADS

        def _split_heads(x):
            B, S, _ = x.shape
            return x.reshape(B, S, NHEADS, D_K).transpose(0, 2, 1, 3)
        B, Sq, _ = query.shape
        q = _split_heads(query @ Wq + bq)
        k = _split_heads(key @ Wk + bk)
        v = _split_heads(value @ Wv + bv)
        scores = jnp.einsum('bhqd,bhkd->bhqk', q, k) / np.sqrt(D_K).astype(np.float32)
        scores = jnp.where(mask == 0, jnp.float32(-1000000000000.0), scores)
        weights = jax.nn.softmax(scores, axis=-1)
        out = jnp.einsum('bhqk,bhkd->bhqd', weights, v)
        out = out.transpose(0, 2, 1, 3).reshape(B, Sq, D_MODEL)
        return out @ Wo + bo

    def _L0_attn_ref(x, wq, wk, wv, wgq, wgk, wgv, r_out_w, gate_local_w, gate_remote_w, w_out):
        import jax, jax.numpy as jnp
        import numpy as np
        D_MODEL = 256
        N_HEADS = 16
        LATENT_HEADS = 8
        LATENT_DIM = 128
        N_LATENTS = 64
        WINDOW = 64
        HEAD_DIM = D_MODEL // N_HEADS
        LAT_HD = LATENT_DIM // LATENT_HEADS
        B, S = (2, 1024)

        def _pool_to_latents(x):
            Bx, Sx, C = x.shape
            chunk = max(1, Sx // N_LATENTS)
            return x.reshape(Bx, N_LATENTS, chunk, C).mean(axis=2)

        def _local_window_attn(Q, K, V):
            Bx, H, Sx, D = Q.shape
            W = WINDOW
            nb = Sx // W
            Qb = Q.reshape(Bx, H, nb, W, D)
            Kp = jnp.pad(K, ((0, 0), (0, 0), (W, 0), (0, 0))).reshape(Bx, H, nb + 1, W, D)
            Vp = jnp.pad(V, ((0, 0), (0, 0), (W, 0), (0, 0))).reshape(Bx, H, nb + 1, W, D)
            Kw = jnp.concatenate([Kp[:, :, :-1], Kp[:, :, 1:]], axis=3)
            Vw = jnp.concatenate([Vp[:, :, :-1], Vp[:, :, 1:]], axis=3)
            i = jnp.arange(W)[:, None]
            j = jnp.arange(2 * W)[None, :]
            base = (j > i) & (j <= i + W)
            blk0 = (jnp.arange(nb) > 0)[:, None, None] | (j >= W)[None, :, :]
            mask = base[None, :, :] & blk0
            sc = jnp.einsum('bhnid,bhnjd->bhnij', Qb, Kw) / np.sqrt(D).astype(np.float32)
            sc = jnp.where(mask[None, None], sc, -jnp.inf)
            p = jax.nn.softmax(sc, axis=-1)
            out = jnp.einsum('bhnij,bhnjd->bhnid', p, Vw)
            return out.reshape(Bx, H, Sx, D)
        Bx, Sx, _ = x.shape
        chunk = max(1, Sx // N_LATENTS)
        Q = (x @ wq).reshape(Bx, Sx, N_HEADS, HEAD_DIM).transpose(0, 2, 1, 3)
        K = (x @ wk).reshape(Bx, Sx, N_HEADS, HEAD_DIM).transpose(0, 2, 1, 3)
        V = (x @ wv).reshape(Bx, Sx, N_HEADS, HEAD_DIM).transpose(0, 2, 1, 3)
        local = _local_window_attn(Q, K, V)
        GQ = (x @ wgq).reshape(Bx, Sx, LATENT_HEADS, LAT_HD).transpose(0, 2, 1, 3)
        GK = _pool_to_latents(x @ wgk).reshape(Bx, N_LATENTS, LATENT_HEADS, LAT_HD).transpose(0, 2, 1, 3)
        GV = _pool_to_latents(x @ wgv).reshape(Bx, N_LATENTS, LATENT_HEADS, LAT_HD).transpose(0, 2, 1, 3)
        lsc = jnp.einsum('bhsd,bhnd->bhsn', GQ, GK) / np.sqrt(LAT_HD).astype(np.float32)
        lmask = jnp.arange(N_LATENTS)[None, :] <= (jnp.arange(Sx) // chunk)[:, None]
        lsc = jnp.where(lmask[None, None], lsc, -jnp.inf)
        lp = jax.nn.softmax(lsc, axis=-1)
        rem = jnp.einsum('bhsn,bhnd->bhsd', lp, GV)
        rem = rem.transpose(0, 2, 1, 3).reshape(Bx, Sx, LATENT_DIM) @ r_out_w
        rem = rem.reshape(Bx, Sx, N_HEADS, HEAD_DIM).transpose(0, 2, 1, 3)
        gl = jax.nn.sigmoid(jnp.einsum('bhsd,hd->bhs', Q, gate_local_w))[..., None]
        gr = jax.nn.sigmoid(jnp.einsum('bhsd,hd->bhs', Q, gate_remote_w))[..., None]
        out = gl * local + gr * rem
        out = out.transpose(0, 2, 1, 3).reshape(Bx, Sx, D_MODEL)
        return out @ w_out

    def _L0_ffn_ref(x, W_gate, W_in, b_in, W_out, b_out):
        import jax, jax.numpy as jnp
        import numpy as np
        B, P, D, D_MLP, E, K = (2, 512, 256, 1024, 8, 2)
        gate_logits = jnp.einsum('bpd,de->bpe', x, W_gate)
        top_w, top_idx = jax.lax.top_k(gate_logits, K)
        top_w = jax.nn.softmax(top_w, axis=-1)
        combine = jnp.einsum('bpke,bpk->bpe', jax.nn.one_hot(top_idx, E, dtype=x.dtype), top_w)
        out = jnp.zeros_like(x)
        for e in range(E):
            h = jax.nn.gelu(jnp.einsum('bpd,dm->bpm', x, W_in[e]) + b_in[e], approximate=False)
            y = jnp.einsum('bpm,md->bpd', h, W_out[e]) + b_out[e]
            out = out + combine[..., e, None] * y
        return out

    def _L1_xattn_ref(x, memories, ln_g, ln_b, Wq, Wkv, Wm, Wo, bo):
        import jax, jax.numpy as jnp
        import numpy as np
        DIM = 256
        HEADS = 16
        DIM_HEAD = 64
        INNER = HEADS * DIM_HEAD
        EPS = 1e-05

        def _split_heads(t):
            b, n, _ = t.shape
            return t.reshape(b, n, HEADS, DIM_HEAD).transpose(0, 2, 1, 3)
        mu = jnp.mean(x, axis=-1, keepdims=True)
        var = jnp.mean(jnp.square(x - mu), axis=-1, keepdims=True)
        xn = (x - mu) * jax.lax.rsqrt(var + EPS) * ln_g + ln_b
        q = _split_heads(xn @ Wq)
        kv = xn @ Wkv
        k = _split_heads(kv[..., :INNER])
        v = _split_heads(kv[..., INNER:])
        mem = _split_heads(memories @ Wm)
        k = jnp.concatenate([k, mem], axis=2)
        v = jnp.concatenate([v, mem], axis=2)
        scale = DIM_HEAD ** (-0.5)
        dots = jnp.einsum('bhid,bhjd->bhij', q, k) * scale
        attn = jax.nn.softmax(dots, axis=-1)
        out = jnp.einsum('bhij,bhjd->bhid', attn, v)
        b, h, n, d = out.shape
        out = out.transpose(0, 2, 1, 3).reshape(b, n, h * d)
        return out @ Wo + bo

    def _L1_attn_ref(x, Wq, Wk, Wv, Wo):
        import jax, jax.numpy as jnp
        import numpy as np
        N_HEADS = 16
        EPS = 1e-06

        def _phi(x):
            return jax.nn.softplus(x) + EPS

        def _reference_tuple_inner(x, Wq, Wk, Wv, Wo):
            B, T, D = x.shape
            H = N_HEADS
            dh = D // H

            def proj(W):
                y = jnp.einsum('btd,ed->bte', x, W)
                return y.reshape(B, T, H, dh).transpose(1, 0, 2, 3)
            q = proj(Wq)
            k = proj(Wk)
            v = proj(Wv)
            qf = _phi(q)
            kf = _phi(k)
            kv0 = jnp.zeros((B, H, dh, dh), dtype=x.dtype)
            z0 = jnp.zeros((B, H, dh), dtype=x.dtype)

            def step(carry, inp):
                kv, z = carry
                qt, kt, vt = inp
                kv = kv + jnp.einsum('bhd,bhe->bhde', kt, vt)
                z = z + kt
                num = jnp.einsum('bhd,bhde->bhe', qt, kv)
                den = jnp.einsum('bhd,bhd->bh', qt, z) + EPS
                return ((kv, z), num / den[..., None])
            (kv_acc, z_acc), out_t = jax.lax.scan(step, (kv0, z0), (qf, kf, v))
            out = out_t.transpose(1, 0, 2, 3).reshape(B, T, D)
            out = jnp.einsum('btd,ed->bte', out, Wo)
            return (out, kv_acc, z_acc)
        return _reference_tuple_inner(x, Wq, Wk, Wv, Wo)[0]

    def _L1_ffn_ref(tensor, Wr, br, W1, b1, W2, b2):
        import jax, jax.numpy as jnp
        import numpy as np
        D_MODEL = 256
        D_HIDDEN = 1024
        NUM_BANKS = 16
        NUM_SELECTED = 2
        logits = jnp.einsum('bsd,de->bse', tensor, Wr) + br
        probs = jax.nn.softmax(logits, axis=-1)
        topv, topi = jax.lax.top_k(probs, NUM_SELECTED)
        gate = jnp.sum(jax.nn.one_hot(topi, NUM_BANKS, dtype=tensor.dtype) * topv[..., None], axis=-2)
        h = jax.nn.relu(jnp.einsum('bsd,edh->bseh', tensor, W1) + b1)
        y = jnp.einsum('bseh,ehm->bsem', h, W2) + b2
        out = jnp.einsum('bse,bsem->bsm', gate, y)
        return out
    x = x + _L0_xattn_ref(_layernorm(x, axis=-1), ctx_1024, ctx_1024, mask_Bx1xSxS2_ik1, L0_xattn_Wq, L0_xattn_bq, L0_xattn_Wk, L0_xattn_bk, L0_xattn_Wv, L0_xattn_bv, L0_xattn_Wo, L0_xattn_bo)
    x = x + _L0_attn_ref(_layernorm(x, axis=-1), L0_attn_wq, L0_attn_wk, L0_attn_wv, L0_attn_wgq, L0_attn_wgk, L0_attn_wgv, L0_attn_r_out_w, L0_attn_gate_local_w, L0_attn_gate_remote_w, L0_attn_w_out)
    x = x + _L0_ffn_ref(_layernorm(x, axis=-1), L0_ffn_W_gate, L0_ffn_W_in, L0_ffn_b_in, L0_ffn_W_out, L0_ffn_b_out)
    x = x + _L1_xattn_ref(_layernorm(x, axis=-1), ctx_1024, L1_xattn_ln_g, L1_xattn_ln_b, L1_xattn_Wq, L1_xattn_Wkv, L1_xattn_Wm, L1_xattn_Wo, L1_xattn_bo)
    x = x + _L1_attn_ref(_layernorm(x, axis=-1), L1_attn_Wq, L1_attn_Wk, L1_attn_Wv, L1_attn_Wo)
    x = x + _L1_ffn_ref(_layernorm(x, axis=-1), L1_ffn_Wr, L1_ffn_br, L1_ffn_W1, L1_ffn_b1, L1_ffn_W2, L1_ffn_b2)
    return x

_drawn_inputs = setup_inputs


def setup_inputs(seed=0):
    import zlib

    import numpy as np

    out = dict(_drawn_inputs(seed))
    spreads = {'L0_xattn_bq': (0.0, 0.1),
     'L0_xattn_bk': (0.0, 2.0),
     'L0_xattn_bv': (0.0, 0.1),
     'L0_xattn_bo': (0.0, 0.1),
     'L0_ffn_b_in': (0.0, 0.1),
     'L0_ffn_b_out': (0.0, 0.1),
     'L1_xattn_ln_g': (1.0, 0.2),
     'L1_xattn_ln_b': (0.0, 0.1),
     'L1_xattn_bo': (0.0, 0.352),
     'L1_ffn_br': (0.0, 0.8),
     'L1_ffn_b1': (0.0, 0.8),
     'L1_ffn_b2': (0.0, 0.8)}
    factors = {'L0_attn_wq': 3.593,
     'L0_attn_wk': 3.593,
     'L0_attn_wgq': 8.0,
     'L0_attn_wgk': 8.0,
     'L0_attn_wgv': 4.845,
     'L0_attn_r_out_w': 8.0,
     'L0_attn_gate_local_w': 8.0,
     'L0_attn_gate_remote_w': 8.0,
     'L1_xattn_Wkv': 5.148,
     'L1_attn_Wq': 48.045,
     'L1_attn_Wk': 22.758,
     'L1_ffn_Wr': 4.383,
     'L1_ffn_W1': 5.968,
     'L1_ffn_W2': 4.759}
    for name, (base, spread) in spreads.items():
        noise = np.random.default_rng([zlib.crc32(name.encode()), seed]).standard_normal(out[name].shape)
        drawn = base * np.exp(spread * noise) if base else spread * noise
        out[name] = jnp.asarray(drawn.astype(out[name].dtype))
    for name, factor in factors.items():
        out[name] = (out[name] * factor).astype(out[name].dtype)
    return out
```

```python
import numpy as np
import concourse.bass as bass
from concourse import mybir
from concourse.alu_op_type import AluOpType as ALU
from contextlib import ExitStack

ACT = mybir.ActivationFunctionType
AX = mybir.AxisListType
FP32 = mybir.dt.float32
INT32 = mybir.dt.int32

P = 128
D = 256
DC = D // P
KEYS = 12544
TILES = 7
BLK = TILES * P
NBLK = KEYS // BLK
HEADS = 16
SPLIT = 4
MASKED = -1.0e12
HUGE = 3.0e38
HID = 1024
HT = HID // P
SLOTS = 2


class Cross:

    def __init__(self, name, k_tiles, head_dim, masked, value_groups, sem):
        self.name = name
        self.k_tiles = k_tiles
        self.dv = head_dim
        self.masked = masked
        self.vgroups = value_groups
        self.kgroups = 2 * DC + 2 * k_tiles
        self.groups = value_groups + 2 * HEADS + self.kgroups
        self.ctx_in = sem(name + "_ctx_in")
        self.ring_full = [sem(name + "_ring_full_even"), sem(name + "_ring_full_odd")]
        self.ring_free = [sem(name + "_ring_free_even"), sem(name + "_ring_free_odd")]
        self.scores = sem(name + "_scores")
        self.blkmax = sem(name + "_blkmax")
        self.negmax = sem(name + "_negmax")
        self.probs = sem(name + "_probs")
        self.shift = sem(name + "_shift")
        self.corr = sem(name + "_corr")
        self.sums = sem(name + "_sums")
        self.pv = sem(name + "_pv")
        self.scaled = sem(name + "_scaled")
        self.acc = sem(name + "_acc")

    def seq(self, b, j):
        return b * (self.groups // 2) + (self.kgroups + j - j % 2) // 2 + 1

    def j_probs(self, h, more):
        return self.vgroups + 2 * h + (self.kgroups if more and h == HEADS - 1 else 0)

    def j_keys(self):
        return self.vgroups + 2 * (HEADS - 1)


def perceiver(nc, a, out):
    ctx = ExitStack()
    with ctx:
        def sb(name, shape, dt=FP32):
            return ctx.enter_context(nc.sbuf_tensor(name, shape, dt))

        def sem(name):
            return ctx.enter_context(nc.semaphore(name))

        norms = ["x0", "la", "f0", "x1", "xm", "l1", "f1"]
        turned_norms = ["x0", "la", "f0", "xm", "l1", "f1"]
        attentions = ["x0", "la", "x1", "l1"]
        routed = ["f0", "f1"]
        shared = {"var": norms, "sd": norms, "xn": norms, "xT": turned_norms, "xT.sb": turned_norms,
                  "attn": attentions, "attnT": attentions, "attnT.sb": attentions,
                  "bias": routed, "bias.sb": routed, "logits": routed, "top": routed, "exp": routed, "comb": routed,
                  "combT": routed, "combT.sb": routed, "bias_ps": routed, "bias_used": routed}
        stages = {}

        def place(name):
            phase, _, step = name.partition(".")
            return (step, shared[step].index(phase) + 1) if step in shared else (name, 1)

        def stage(name):
            key = place(name)[0]
            if key not in stages:
                stages[key] = sem("step_" + key.replace(".", "_"))
            return stages[key]

        X = sb("X", [P, D])
        xn = sb("xn", [P, D])
        xm = sb("xm", [P, D])
        xT = sb("xT", [P, DC, P])
        ident = sb("ident", [P, P])
        headmask = sb("headmask", [P, 8])
        window = sb("window", [P, P])
        latmask = sb("latmask", [P, 64])
        causal = sb("causal", [P, P])
        rev8 = sb("rev8", [P, 8])
        rev16 = sb("rev16", [P, 16])
        stats = sb("stats", [P, 6])
        meanvar = sb("meanvar", [P, 2])
        sd = sb("sd", [P, 2])
        qT = sb("qT", [P, 8, P])
        qz = sb("qz", [P, 2, 8, P])
        ctx_nat = sb("ctx_nat", [P, TILES, D])
        ctxT = sb("ctxT", [P, DC, BLK])
        kT = sb("kT", [P, 8, BLK])
        vals = sb("vals", [P, TILES, 1024])
        probs = sb("probs", [P, 2, 1024])
        probsT = sb("probsT", [P, 2, 1024])
        masked_s = sb("masked_s", [P, 2, BLK])
        mask_raw = sb("mask_raw", [P, BLK], INT32)
        mask_add = sb("mask_add", [P, BLK])
        O = sb("O", [P, 1024])
        den = sb("den", [P, HEADS])
        negcur = sb("negcur", [P, HEADS])
        negprev = sb("negprev", [P, HEADS])
        blkmax = sb("blkmax", [P, HEADS])
        rowsum = sb("rowsum", [P, HEADS])
        shift = sb("shift", [P, HEADS])
        corr = sb("corr", [P, HEADS])
        v_self = sb("v_self", [P, 1024])
        wq0 = sb("wq0", [P, DC, D])
        wk0 = sb("wk0", [P, DC, D])
        wv0 = sb("wv0", [P, DC, D])
        wo0 = sb("wo0", [P, DC, D])
        la_wq = sb("la_wq", [P, DC, D])
        la_wk = sb("la_wk", [P, DC, D])
        la_wv = sb("la_wv", [P, DC, D])
        la_wgq = sb("la_wgq", [P, DC, P])
        la_wgk = sb("la_wgk", [P, DC, P])
        la_wgv = sb("la_wgv", [P, DC, P])
        la_rout = sb("la_rout", [P, D])
        la_wout = sb("la_wout", [P, DC, D])
        wm1 = sb("wm1", [P, DC, 1024])
        wo1 = sb("wo1", [P, 8, D])
        rows = sb("rows", [P, 8, D])
        BV0, BO0, GL, GR, LNG, LNB, BO1 = range(7)
        cols = sb("cols", [P, 4])
        wgate0 = sb("wgate0", [P, DC, 8])
        wr1 = sb("wr1", [P, DC, 16])
        br1 = sb("br1", [P, 16])
        bout0 = sb("bout0", [8, D])
        b2_1 = sb("b2_1", [16, D])
        bin_rows = sb("bin_rows", [P, P])
        b1_rows = sb("b1_rows", [P, P])
        bin_cols = sb("bin_cols", [P, 8 * HT])
        b1_cols = sb("b1_cols", [P, 16 * HT])
        win = sb("win", [P, SLOTS, DC, HID])
        wout = sb("wout", [P, SLOTS, HT, D])
        gate = sb("gate", [P, 8, 16])
        comb = sb("comb", [P, 16])
        combT = sb("combT", [16, P])
        pad = sb("pad", [P, 2])
        gatecol = sb("gatecol", [P, 8])
        gates = sb("gates", [P, 32])
        kflat = kT[:, :, :].rearrange("p a b -> p (a b)")
        vflat = vals[:, :, :].rearrange("p a b -> p (a b)")
        wide_a = probs[:, :, :].rearrange("p a b -> p (a b)")
        wide_b = probsT[:, :, :].rearrange("p a b -> p (a b)")
        hT = vflat[:, 4096:4096 + 2 * HID].rearrange("p (s t n) -> p s t n", s=2, t=HT)
        attn = ctxT[:, 0, 0:D]
        attnT = O[:, 0:1024].rearrange("p (t n) -> p t n", t=8)

        kz = kflat[:, 0:2048].rearrange("p (e h k) -> p e h k", e=2, h=8)
        gkz = kflat[:, 2048:2560].rearrange("p (h k) -> p h k", h=8)
        lat_s = kflat[:, 2560:3072]
        q_nat = kflat[:, 3072:3328]
        v_nat = kflat[:, 3328:3584]
        gv_nat = kflat[0:64, 3584:3712]
        rem = kflat[:, 3712:3840]
        xpool = kflat[:, 3840:3968].rearrange("p (c n) -> p c n", c=DC)
        k_self = kflat[:, 6144:7168].rearrange("p (t n) -> p t n", t=8)
        v_ext = kflat[:, 2048:2048 + HEADS * 17].rearrange("p (h d) -> p h d", h=HEADS)
        sp_z, sp_a, sp_w, sp_u = (kflat[:, 4096 + 512 * i:4096 + 512 * (i + 1)] for i in range(4))
        v0 = vflat[:, 0:TILES * D]
        wT = wide_b.rearrange("p (w c n) -> p w c n", w=4, c=DC)

        ps_s = ctx.enter_context(nc.psum_tensor("ps_s", [P, 4 * 512], FP32))
        ps_ring = ctx.enter_context(nc.psum_tensor("ps_ring", [P, 2 * 512], FP32))
        ps_o = ctx.enter_context(nc.psum_tensor("ps_o", [P, 2 * 512], FP32))

        L0 = Cross("x0", 2, 16, True, 4, sem)
        L1 = Cross("x1", 8, 64, False, 14, sem)
        mask_in = sem("mask_in")
        mask_ready = sem("mask_ready")
        expert_in = [sem(f"expert_in{s}") for s in range(SLOTS)]
        hid_full = sem("hid_full")
        hid_ready = sem("hid_ready")
        y_full = sem("y_full")
        y_added = sem("y_added")
        loads = {k: sem("load_" + k) for k in ("x", "x0", "x0b", "la", "f0", "x1", "x1big", "la1", "f1")}
        stored = sem("stored")
        act_step = sem("act_step")
        dve_step = sem("dve_step")
        pool_step = sem("pool_step")

        def chunked(w):
            return w.rearrange("(c p) n -> p c n", p=P)

        def row(v, n=D):
            return v.rearrange("(a n) -> a n", a=1).broadcast_to([P, n])

        LOADS = {
            "x": [(X[:, :], a["x"].rearrange("a s d -> (a s) d"))],
            "x0": [(wq0[:, :, :], chunked(a["L0_xattn_Wq"])), (wk0[:, :, :], chunked(a["L0_xattn_Wk"])),
                   (wv0[:, :, :], chunked(a["L0_xattn_Wv"])),
                   (cols[:, 0:2], a["L0_xattn_bq"].rearrange("(c p) -> p c", p=P)),
                   (cols[:, 2:4], a["L0_xattn_bk"].rearrange("(c p) -> p c", p=P))],
            "x0b": [(wo0[:, :, :], chunked(a["L0_xattn_Wo"])), (rows[:, BV0, :], row(a["L0_xattn_bv"])),
                    (rows[:, BO0, :], row(a["L0_xattn_bo"]))],
            "la": [(la_wq[:, :, :], chunked(a["L0_attn_wq"])), (la_wk[:, :, :], chunked(a["L0_attn_wk"])),
                   (la_wv[:, :, :], chunked(a["L0_attn_wv"])), (la_wgq[:, :, :], chunked(a["L0_attn_wgq"])),
                   (la_wgk[:, :, :], chunked(a["L0_attn_wgk"])), (la_wgv[:, :, :], chunked(a["L0_attn_wgv"])),
                   (la_rout[:, :], a["L0_attn_r_out_w"]), (la_wout[:, :, :], chunked(a["L0_attn_w_out"])),
                   (rows[:, GL, :], row(a["L0_attn_gate_local_w"].rearrange("h d -> (h d)"))),
                   (rows[:, GR, :], row(a["L0_attn_gate_remote_w"].rearrange("h d -> (h d)")))],
            "f0": [(wgate0[:, :, :], chunked(a["L0_ffn_W_gate"])), (bout0[:, :], a["L0_ffn_b_out"]),
                   (bin_rows[0:8 * HT, :], a["L0_ffn_b_in"].rearrange("e (t p) -> (e t) p", p=P))],
            "x1": [(wm1[:, :, :], chunked(a["L1_xattn_Wm"])), (wo1[:, :, :], chunked(a["L1_xattn_Wo"])),
                   (rows[:, LNG, :], row(a["L1_xattn_ln_g"])), (rows[:, LNB, :], row(a["L1_xattn_ln_b"])),
                   (rows[:, BO1, :], row(a["L1_xattn_bo"]))],
            "x1big": [(kflat[:, 4096:6144].rearrange("p (c n) -> p c n", c=DC), chunked(a["L1_xattn_Wq"])),
                      (vflat[:, 0:4096].rearrange("p (c n) -> p c n", c=DC), chunked(a["L1_xattn_Wkv"]))],
            "la1": [(wq0[:, :, :], chunked(a["L1_attn_Wq"])), (wk0[:, :, :], chunked(a["L1_attn_Wk"])),
                    (wv0[:, :, :], chunked(a["L1_attn_Wv"])), (wo0[:, :, :], chunked(a["L1_attn_Wo"]))],
            "f1": [(wr1[:, :, :], chunked(a["L1_ffn_Wr"])), (br1[:, :], row(a["L1_ffn_br"], 16)),
                   (b2_1[:, :], a["L1_ffn_b2"]), (b1_rows[:, :], a["L1_ffn_b1"].rearrange("e (t p) -> (e t) p", p=P))],
        }
        WQ1 = LOADS["x1big"][0][0]
        WKV1 = LOADS["x1big"][1][0]
        ctx_blocks = a["ctx_1024"].rearrange("a (b p t) d -> (a b) p t d", p=P, t=TILES)
        mask_blocks = a["mask_Bx1xSxS2_ik1"].rearrange("a c q (b n) -> (a c b) q n", n=BLK)

        def arrived(eng, key):
            eng.wait_ge(loads[key], 16 * len(LOADS[key]))

        def after(eng, name):
            eng.wait_ge(stage(name), place(name)[1])

        def expert_rounds(eng, E, body):
            body(0)
            with eng.Fori(0, E // SLOTS - 1) as i:
                body(i + 1)

        block = ctx.enter_context(nc.Block())

        @block.sync
        def _(sp):
            def load(key):
                for dst, src in LOADS[key]:
                    with nc.allow_non_contiguous_dma(reason="two bias vectors of 256 values as columns"):
                        sp.dma_start(dst, src).then_inc(loads[key], 16)

            def ctx_load(L, b):
                sp.dma_start(ctx_nat[:, :, :], ctx_blocks[b]).then_inc(L.ctx_in, 16)

            def mask_load(b):
                sp.dma_start(mask_raw[:, :], mask_blocks[b]).then_inc(mask_in, 16)

            def expert_load(w1, w2, e, slot):
                sp.dma_start(win[:, slot, :, :], w1[e].rearrange("(c p) n -> p c n", p=P)).then_inc(expert_in[slot], 16)
                sp.dma_start(wout[:, slot, :, :], w2[e].rearrange("(t p) n -> p t n", p=P)).then_inc(expert_in[slot], 16)

            def ctx_stream(L):
                sp.wait_ge(L.ring_full[0], L.seq(0, -L.kgroups + 2))
                sp.wait_ge(L.ring_full[1], L.seq(0, -L.kgroups + 3))
                ctx_load(L, 1)
                if L.masked:
                    sp.wait_ge(mask_ready, 1)
                    mask_load(1)
                with sp.Fori(0, NBLK - 2) as i:
                    sp.wait_ge(L.ring_full[0], L.seq(i, L.j_keys() + 2))
                    sp.wait_ge(L.ring_full[1], L.seq(i, L.j_keys() + 3))
                    ctx_load(L, i + 2)
                    if L.masked:
                        sp.wait_ge(mask_ready, i + 2)
                        mask_load(i + 2)

            w0 = (a["L0_ffn_W_in"], a["L0_ffn_W_out"])
            w1 = (a["L1_ffn_W1"], a["L1_ffn_W2"])
            load("x")
            ctx_load(L0, 0)
            mask_load(0)
            load("x0")
            load("x0b")
            load("la")
            load("f0")
            load("x1")
            load("f1")
            for s in range(SLOTS):
                expert_load(*w0, s, s)
            ctx_stream(L0)
            after(sp, "la.out_ps")
            ctx_load(L1, 0)
            load("x1big")
            load("la1")
            with sp.Fori(0, 8 // SLOTS - 1) as i:
                for s in range(SLOTS):
                    sp.wait_ge(y_full, i * SLOTS + (s + 1))
                    expert_load(*w0, i * SLOTS + (SLOTS + s), s)
            for s in range(SLOTS):
                sp.wait_ge(y_full, 8 - SLOTS + s + 1)
                expert_load(*w1, s, s)
            ctx_stream(L1)
            with sp.Fori(0, 16 // SLOTS - 1) as i:
                for s in range(SLOTS):
                    sp.wait_ge(y_full, i * SLOTS + (8 + s + 1))
                    expert_load(*w1, i * SLOTS + (SLOTS + s), s)
            after(sp, "f1.done")
            sp.dma_start(out.rearrange("a s d -> (a s) d"), X[:, :]).then_inc(stored, 16)
            sp.wait_ge(stored, 16)

        @block.gpsimd
        def _(pool):
            count = [0]

            def link(ins):
                count[0] += 1
                ins.then_inc(pool_step, 1)
                pool.wait_ge(pool_step, count[0])

            link(pool.memset(ident[:, :], 0.0))
            pool.affine_select(out=ident[:, :], in_=ident[:, :], compare_op=ALU.not_equal, fill=1.0, base=0,
                               pattern=[[-1, P]], channel_multiplier=1).then_inc(stage("ident"), 1)
            link(pool.memset(headmask[:, :], 1.0))
            link(pool.affine_select(out=headmask[:, :], in_=headmask[:, :], compare_op=ALU.is_ge, fill=0.0, base=0,
                                    pattern=[[-16, 8]], channel_multiplier=1))
            pool.affine_select(out=headmask[:, :], in_=headmask[:, :], compare_op=ALU.is_ge, fill=0.0, base=15,
                               pattern=[[16, 8]], channel_multiplier=-1).then_inc(stage("headmask"), 1)

            def mask_convert(b):
                pool.wait_ge(mask_in, (b + 1) * 16)
                if not (isinstance(b, int) and b == 0):
                    pool.wait_ge(L0.blkmax, b * HEADS)
                pool.tensor_tensor(pad[:, 1:2], headmask[:, 0:1], headmask[:, 1:2], ALU.add)
                pool.tensor_scalar(mask_add[:, :].rearrange("q (t p) -> q t p", p=P),
                                   mask_raw[:, :].rearrange("q (p t) -> q t p", t=TILES),
                                   0.0, MASKED, ALU.is_equal, ALU.mult).then_inc(mask_ready, 1)

            after(pool, "headmask")
            mask_convert(0)
            link(pool.memset(window[:, :], 0.0))
            link(pool.affine_select(out=window[:, :], in_=window[:, :], compare_op=ALU.is_ge, fill=-HUGE, base=0,
                                    pattern=[[-1, P]], channel_multiplier=1))
            link(pool.affine_select(out=window[:, :], in_=window[:, :], compare_op=ALU.is_ge, fill=-HUGE, base=63,
                                    pattern=[[1, P]], channel_multiplier=-1))
            link(pool.memset(latmask[:, :], 0.0))
            link(pool.affine_select(out=latmask[:, :], in_=latmask[:, :], compare_op=ALU.is_ge, fill=-HUGE, base=0,
                                    pattern=[[-2, 64]], channel_multiplier=1))
            link(pool.memset(causal[:, :], 1.0))
            link(pool.affine_select(out=causal[:, :], in_=causal[:, :], compare_op=ALU.is_ge, fill=0.0, base=0,
                                    pattern=[[1, P]], channel_multiplier=-1))
            for e in range(16):
                if e < 8:
                    link(pool.memset(rev8[:, e:e + 1], float(8 - e)))
                link(pool.memset(rev16[:, e:e + 1], float(16 - e)))
            pool.memset(rev16[:, 0:1], 16.0).then_inc(stage("consts"), 1)
            with pool.Fori(0, NBLK - 1) as i:
                mask_convert(i + 1)

        @block.scalar
        def _(act):
            count = [0]

            def link(ins):
                count[0] += 1
                ins.then_inc(act_step, 1)
                act.wait_ge(act_step, count[0])

            def ln_root(tag):
                after(act, tag + ".var")
                act.activation(sd[:, 0:1], sd[:, 1:2], ACT.Sqrt).then_inc(stage(tag + ".sd"), 1)

            def evacuate(L, b, j, dst, bias=None):
                act.wait_ge(L.ring_full[0], L.seq(b, j))
                n = 512
                src = ps_ring[:, 0:n]
                if bias is None:
                    ins = act.activation(dst, src, ACT.Copy)
                else:
                    ins = act.activation(dst, src, ACT.Identity, bias=bias)
                ins.then_inc(L.ring_free[0], 1)

            def next_keys(L, b, j):
                for c in range(DC):
                    evacuate(L, b, j + 2 * c, ctxT[:, c, 0:512])
                for f in range(L.k_tiles):
                    evacuate(L, b, j + 2 * DC + 2 * f, kT[:, f, 0:512],
                             cols[:, 2 + f:3 + f] if L is L0 else None)

            def cross_block(L, b, more):
                def exps(h):
                    n = h % 2
                    act.wait_ge(L.negmax, b * HEADS + h + 1)
                    if h >= 2:
                        act.wait_ge(L.ring_full[1], L.seq(b, L.j_probs(h - 2, more) + 1))
                    elif not (isinstance(b, int) and b == 0):
                        act.wait_ge(L.ring_full[1], L.seq(b, -1 - 2 * (1 - h) - (L.kgroups if h == 0 else 0)))
                    src = masked_s[:, n, :] if L.masked else ps_s[:, 1024 * n:1024 * n + BLK]
                    act.activation(probs[:, n, 0:BLK], src, ACT.Exp, bias=negcur[:, h:h + 1],
                                   accum_out=rowsum[:, h:h + 1]).then_inc(L.probs, 1)

                def turned(h):
                    evacuate(L, b, L.j_probs(h, more), probsT[:, h % 2, 0:512])

                if not (isinstance(b, int) and b == 0):
                    act.wait_ge(L.sums, b)
                exps(0)
                exps(1)
                for j in range(0, L.vgroups, 2):
                    values_even(L, b, j)
                turned(0)
                for h in range(2, HEADS):
                    exps(h)
                    turned(h - 1)
                act.wait_ge(L.shift, b + 1)
                act.activation(corr[:, :], shift[:, :], ACT.Exp).then_inc(L.corr, 1)
                if more:
                    next_keys(L, b, L.j_keys())
                turned(HEADS - 1)

            def values_even(L, b, j):
                if L is L0:
                    evacuate(L, b, j, v0[:, j * 512:(j + 1) * 512])
                else:
                    evacuate(L, b, j, vals[:, j // 2, 0:512])

            def cross(L):
                if L is L0:
                    arrived(act, "x0")
                next_keys(L, 0, -L.kgroups)
                cross_block(L, 0, True)
                with act.Fori(0, NBLK - 2) as i:
                    cross_block(L, i + 1, True)
                cross_block(L, NBLK - 1, False)

            def softmax_exps(tag, src):
                after(act, tag + ".shifted")
                act.activation(src, src, ACT.Exp).then_inc(stage(tag + ".exps"), 1)

            def experts(E, func, bias_cols, base):
                def round_of_experts(i):
                    for j in range(SLOTS):
                        for half in range(2):
                            act.wait_ge(hid_full, i * (2 * SLOTS) + ((base + j) * 2 + half + 1))
                            bank = (j % 2) * 2 + half
                            for t in range(4):
                                m = half * 4 + t
                                ins = act.activation(
                                    hT[:, j % 2, m, :], ps_s[:, bank * 512 + t * P:bank * 512 + (t + 1) * P], func,
                                    bias=bias_cols[:, bass.ds(i * (SLOTS * HT) + (j * HT + m), 1)])
                            ins.then_inc(hid_ready, 1)

                expert_rounds(act, E, round_of_experts)

            ln_root("x0")
            cross(L0)
            ln_root("la")
            softmax_exps("la.local", wide_a)
            softmax_exps("la.lat", lat_s)
            after(act, "la.gates")
            act.activation(gates[:, :], gates[:, :], ACT.Exp, scale=-1.0).then_inc(stage("la.gexp"), 1)
            ln_root("f0")
            after(act, "f0.top")
            act.activation(gate[:, 6, 0:8], gate[:, 5, 0:8], ACT.Exp).then_inc(stage("f0.exp"), 1)
            experts(8, ACT.Gelu, bin_cols, 0)
            ln_root("x1")
            ln_root("xm")
            softmax_exps("x1.self", wide_a)
            cross(L1)
            ln_root("l1")
            after(act, "l1.abs")
            act.activation(sp_u, sp_a, ACT.Exp, scale=-1.0).then_inc(stage("l1.u"), 1)
            after(act, "l1.w")
            act.activation(sp_a, sp_w, ACT.Ln).then_inc(stage("l1.ln"), 1)
            ln_root("f1")
            after(act, "f1.top")
            act.activation(gate[:, 6, 0:16], gate[:, 5, 0:16], ACT.Exp).then_inc(stage("f1.exp"), 1)
            experts(16, ACT.Relu, b1_cols, 8)

        @block.vector
        def _(dve):
            count = [0]

            def link(ins):
                count[0] += 1
                ins.then_inc(dve_step, 1)
                dve.wait_ge(dve_step, count[0])

            def layernorm(tag, src, dst, eps=1e-5):
                link(dve.bn_stats(stats[:, :], src))
                link(dve.bn_aggr(meanvar[:, :], stats[:, :]))
                dve.tensor_scalar(sd[:, 1:2], meanvar[:, 1:2], eps, None, ALU.add).then_inc(stage(tag + ".var"), 1)
                after(dve, tag + ".sd")
                link(dve.reciprocal(sd[:, 1:2], sd[:, 0:1]))
                dve.tensor_scalar(dst, src, meanvar[:, 0:1], sd[:, 1:2], ALU.subtract,
                                  ALU.mult).then_inc(stage(tag + ".xn"), 1)

            def take(tag, dst, src):
                after(dve, tag)
                dve.tensor_copy(dst, src).then_inc(stage(tag + ".sb"), 1)

            def evacuate(L, b, j, dst, n=384, bias=None):
                dve.wait_ge(L.ring_full[1], L.seq(b, j))
                src = ps_ring[:, 512:512 + n]
                if bias is None:
                    ins = dve.tensor_copy(dst, src)
                else:
                    ins = dve.tensor_scalar(dst, src, bias, None, ALU.add)
                ins.then_inc(L.ring_free[1], 1)

            def next_keys(L, b, j):
                for c in range(DC):
                    evacuate(L, b, j + 2 * c + 1, ctxT[:, c, 512:BLK])
                for f in range(L.k_tiles):
                    evacuate(L, b, j + 2 * DC + 2 * f + 1, kT[:, f, 512:BLK],
                             bias=cols[:, 2 + f:3 + f] if L is L0 else None)

            def cross_block(L, b, more):
                hd = HEADS * L.dv

                def maximum(h):
                    n = h % 2
                    dve.wait_ge(L.scores, b * HEADS + h + 1)
                    s = ps_s[:, 1024 * n:1024 * n + BLK]
                    if L.masked:
                        if h >= 2:
                            dve.wait_ge(L.probs, b * HEADS + h - 1)
                        elif not (isinstance(b, int) and b == 0):
                            dve.wait_ge(L.probs, b * HEADS + h - 1)
                        if h == 0:
                            dve.wait_ge(mask_ready, b + 1)
                        dve.memset(pad[:, 0:1], 0.0)
                        dve.tensor_tensor_reduce(masked_s[:, n, :], s, mask_add[:, :], 1.0, -HUGE, ALU.add, ALU.max,
                                                 blkmax[:, h:h + 1]).then_inc(L.blkmax, 1)
                    else:
                        dve.tensor_reduce(blkmax[:, h:h + 1], s, AX.X, ALU.max).then_inc(L.blkmax, 1)
                    dve.wait_ge(L.blkmax, b * HEADS + h + 1)
                    dve.scalar_tensor_tensor(out=negcur[:, h:h + 1], in0=blkmax[:, h:h + 1], scalar=-1.0,
                                             in1=negprev[:, h:h + 1], op0=ALU.mult,
                                             op1=ALU.min).then_inc(L.negmax, 1)

                def turned(h):
                    evacuate(L, b, L.j_probs(h, more) + 1, probsT[:, h % 2, 512:BLK])

                maximum(0)
                maximum(1)
                for j in range(1, L.vgroups, 2):
                    if L is L0:
                        last = j == L.vgroups - 1
                        evacuate(L, b, j, v0[:, j * 512:j * 512 + (256 if last else 512)], 256 if last else 512)
                    else:
                        evacuate(L, b, j, vals[:, j // 2, 512:1024], 512)
                turned(0)
                for h in range(2, HEADS):
                    maximum(h)
                    turned(h - 1)
                dve.wait_ge(L.negmax, b * HEADS + HEADS)
                dve.tensor_tensor(shift[:, :], negcur[:, :], negprev[:, :], ALU.subtract).then_inc(L.shift, 1)
                if more:
                    next_keys(L, b, L.j_keys())
                dve.wait_ge(L.corr, b + 1)
                dve.wait_ge(L.probs, b * HEADS + HEADS)
                dve.tensor_copy(negprev[:, :], negcur[:, :])
                dve.tensor_tensor(den[:, :], den[:, :], corr[:, :], ALU.mult).then_inc(L.scaled, 1)
                turned(HEADS - 1)
                dve.wait_ge(L.scaled, 2 * b + 1)
                dve.tensor_tensor(den[:, :], den[:, :], rowsum[:, :], ALU.add).then_inc(L.sums, 1)
                o = O[:, 0:hd].rearrange("p (h d) -> p h d", h=HEADS)
                dve.tensor_tensor(o, o, corr[:, :].unsqueeze(2).broadcast_to([P, HEADS, L.dv]),
                                  ALU.mult).then_inc(L.scaled, 1)
                dve.wait_ge(L.scaled, 2 * b + 2)
                dve.wait_ge(L.sums, b + 1)
                dve.wait_ge(L.pv, b + 1)
                dve.tensor_tensor(O[:, 0:hd], O[:, 0:hd], ps_o[:, 0:hd], ALU.add).then_inc(L.acc, 1)
                dve.wait_ge(L.acc, b + 1)

            def cross(L):
                if L is L0:
                    arrived(dve, "x0")
                next_keys(L, 0, -L.kgroups)
                cross_block(L, 0, True)
                with dve.Fori(0, NBLK - 2) as i:
                    cross_block(L, i + 1, True)
                cross_block(L, NBLK - 1, False)

            def head_queries(src, e, dst):
                return dve.tensor_tensor(dst, src.unsqueeze(1).broadcast_to([P, 8, P]),
                                         headmask[:, :].unsqueeze(2).broadcast_to([P, 8, P]), ALU.mult)

            def softmax_head(tag, s, heads, keys, negmax, sums):
                s3 = s.rearrange("p (h k) -> p h k", h=heads)
                link(dve.tensor_reduce(negmax, s3, AX.X, ALU.max, negate=True))
                dve.tensor_tensor(s3, s3, negmax.unsqueeze(2).broadcast_to([P, heads, keys]),
                                  ALU.add).then_inc(stage(tag + ".shifted"), 1)
                after(dve, tag + ".exps")
                link(dve.tensor_reduce(sums, s3, AX.X, ALU.add))

            def route(tag, E, logits, rev, renormalise):
                g = [gate[:, i, 0:E] for i in range(8)]
                m = gatecol
                link(dve.tensor_reduce(m[:, 0:1], logits, AX.X, ALU.max))
                dve.tensor_scalar(g[5], logits, m[:, 0:1], None, ALU.subtract).then_inc(stage(tag + ".top"), 1)
                after(dve, tag + ".exp")
                if renormalise:
                    score = logits
                else:
                    link(dve.tensor_reduce(m[:, 1:2], g[6], AX.X, ALU.add))
                    link(dve.reciprocal(m[:, 2:3], m[:, 1:2]))
                    link(dve.tensor_scalar(g[6], g[6], m[:, 2:3], None, ALU.mult))
                    score = g[6]
                    link(dve.tensor_reduce(m[:, 0:1], score, AX.X, ALU.max))
                link(dve.scalar_tensor_tensor(out=g[0], in0=score, scalar=m[:, 0:1], in1=rev[:, :],
                                              op0=ALU.is_equal, op1=ALU.mult))
                link(dve.tensor_reduce(m[:, 3:4], g[0], AX.X, ALU.max))
                link(dve.tensor_scalar(g[1], g[0], m[:, 3:4], None, ALU.is_equal))
                link(dve.scalar_tensor_tensor(out=g[2], in0=g[1], scalar=-HUGE, in1=score,
                                              op0=ALU.mult, op1=ALU.add))
                link(dve.tensor_reduce(m[:, 4:5], g[2], AX.X, ALU.max))
                link(dve.scalar_tensor_tensor(out=g[0], in0=g[2], scalar=m[:, 4:5], in1=rev[:, :],
                                              op0=ALU.is_equal, op1=ALU.mult))
                link(dve.tensor_reduce(m[:, 5:6], g[0], AX.X, ALU.max))
                link(dve.tensor_scalar(g[3], g[0], m[:, 5:6], None, ALU.is_equal))
                link(dve.tensor_tensor(g[1], g[1], g[3], ALU.add))
                if renormalise:
                    link(dve.tensor_tensor(g[2], g[1], g[6], ALU.mult))
                    link(dve.tensor_reduce(m[:, 1:2], g[2], AX.X, ALU.add))
                    link(dve.reciprocal(m[:, 2:3], m[:, 1:2]))
                    dve.tensor_scalar(comb[:, 0:E], g[2], m[:, 2:3], None, ALU.mult).then_inc(stage(tag + ".comb"), 1)
                else:
                    dve.tensor_tensor(comb[:, 0:E], g[1], g[6], ALU.mult).then_inc(stage(tag + ".comb"), 1)

            def experts(tag, E, base):
                take(tag + ".combT", combT[0:E, :], ps_o[0:E, 0:P])
                after(dve, tag + ".bias_ps")
                dve.tensor_tensor(X[:, :], X[:, :], ps_o[:, 512:512 + D], ALU.add).then_inc(stage(tag + ".bias_used"), 1)
                after(dve, tag + ".bias_used")

                def round_of_experts(i):
                    for j in range(SLOTS):
                        e = i * SLOTS + (base + j)
                        dve.wait_ge(y_full, e + 1)
                        dve.scalar_tensor_tensor(out=X[:, :], in0=ps_o[:, (j % 2) * 512:(j % 2) * 512 + D],
                                                 scalar=comb[:, bass.ds(i * SLOTS + j, 1)], in1=X[:, :],
                                                 op0=ALU.mult, op1=ALU.add).then_inc(y_added, 1)
                        dve.wait_ge(y_added, e + 1)

                expert_rounds(dve, E, round_of_experts)

            def add_projection(tag, src, bias_row=None):
                after(dve, tag)
                if bias_row is not None:
                    link(dve.tensor_tensor(X[:, :], X[:, :], rows[:, bias_row, :], ALU.add))
                link(dve.tensor_tensor(X[:, :], X[:, :], src, ALU.add))

            arrived(dve, "x")
            layernorm("x0", X[:, :], xn[:, :])
            take("x0.xT", xT[:, :, :], ps_ring[:, 0:D].rearrange("p (c n) -> p c n", c=DC))
            arrived(dve, "x0")
            after(dve, "headmask")
            after(dve, "x0.q")
            for e in range(DC):
                link(dve.tensor_scalar(qT[:, e, :], ps_o[:, e * P:(e + 1) * P], cols[:, e:e + 1], 0.25,
                                       ALU.add, ALU.mult))
            link(head_queries(qT[:, 0, :], 0, qz[:, 0, :, :]))
            head_queries(qT[:, 1, :], 1, qz[:, 1, :, :]).then_inc(stage("x0.qz"), 1)
            link(dve.memset(O[:, :], 0.0))
            link(dve.memset(den[:, :], 0.0))
            link(dve.memset(negprev[:, :], HUGE))
            cross(L0)
            link(dve.reciprocal(den[:, :], den[:, :]))
            o0 = O[:, 0:D].rearrange("p (h d) -> p h d", h=HEADS)
            link(dve.tensor_tensor(xn[:, :].rearrange("p (h d) -> p h d", h=HEADS), o0,
                                   den[:, :].unsqueeze(2).broadcast_to([P, HEADS, 16]), ALU.mult))
            arrived(dve, "x0b")
            dve.tensor_tensor(xn[:, :], xn[:, :], rows[:, BV0, :], ALU.add).then_inc(stage("x0.attn"), 1)
            take("x0.attnT", xT[:, :, :], ps_ring[:, 0:D].rearrange("p (c n) -> p c n", c=DC))
            add_projection("x0.out", ps_o[:, 0:D], BO0)

            layernorm("la", X[:, :], xn[:, :])
            after(dve, "la.xT")
            link(dve.tensor_copy(xT[:, :, :], ps_ring[:, 0:D].rearrange("p (c n) -> p c n", c=DC)))
            pair = xT[:, :, :].rearrange("p c (n two) -> p c n two", two=2)
            link(dve.tensor_tensor(xpool, pair[:, :, :, 0], pair[:, :, :, 1], ALU.add))
            dve.tensor_scalar(xpool, xpool, 0.5, None, ALU.mult).then_inc(stage("la.xT.sb"), 1)
            after(dve, "la.proj")
            link(dve.tensor_scalar(qT[:, 0:2, :], ps_s[:, 0:D].rearrange("p (c n) -> p c n", c=2), 0.25, None, ALU.mult))
            link(dve.tensor_copy(qT[:, 2:4, :], ps_s[:, D:2 * D].rearrange("p (c n) -> p c n", c=2)))
            link(dve.tensor_copy(v_nat, ps_s[:, 512:512 + D]))
            link(dve.tensor_copy(q_nat, ps_s[:, 512 + D:1024]))
            link(dve.tensor_scalar(qT[:, 4, :], ps_s[:, 1024:1024 + P], 0.25, None, ALU.mult))
            link(dve.tensor_copy(qT[:, 5, 0:64], ps_s[:, 1024 + P:1024 + P + 64]))
            link(dve.tensor_copy(gv_nat, ps_s[0:64, 1536:1536 + P]))
            link(head_queries(qT[:, 2, :], 0, kz[:, 0, :, :]))
            link(head_queries(qT[:, 3, :], 1, kz[:, 1, :, :]))
            dve.tensor_tensor(gkz, qT[:, 5, 0:64].unsqueeze(1).broadcast_to([P, 8, 64]),
                              headmask[:, :].unsqueeze(2).broadcast_to([P, 8, 64]), ALU.mult).then_inc(stage("la.kz"), 1)
            after(dve, "consts")
            after(dve, "la.scores")
            link(dve.tensor_tensor(wide_a.rearrange("p (h k) -> p h k", h=HEADS),
                                   ps_s[:, :].rearrange("p (h k) -> p h k", h=HEADS),
                                   window[:, :].unsqueeze(1).broadcast_to([P, HEADS, P]), ALU.add))
            link(dve.tensor_tensor(lat_s.rearrange("p (h k) -> p h k", h=8),
                                   ps_ring[:, 0:512].rearrange("p (h k) -> p h k", h=8),
                                   latmask[:, :].unsqueeze(1).broadcast_to([P, 8, 64]), ALU.add))
            softmax_head("la.local", wide_a, HEADS, P, negprev[:, :], den[:, :])
            softmax_head("la.lat", lat_s, 8, 64, negcur[:, 0:8], rowsum[:, 0:8])
            arrived(dve, "la")
            for i, r in ((0, GL), (1, GR)):
                link(dve.tensor_tensor(xn[:, :], q_nat, rows[:, r, :], ALU.mult))
                link(dve.tensor_reduce(gates[:, 16 * i:16 * i + 16], xn[:, :].rearrange("p (h d) -> p h d", h=HEADS),
                                       AX.X, ALU.add))
            dve.tensor_scalar(gates[:, :], gates[:, :], 1.0, None, ALU.mult).then_inc(stage("la.gates"), 1)
            after(dve, "la.gexp")
            link(dve.tensor_scalar(gates[:, :], gates[:, :], 1.0, None, ALU.add))
            link(dve.reciprocal(gates[:, :], gates[:, :]))
            link(dve.reciprocal(den[:, :], den[:, :]))
            link(dve.reciprocal(rowsum[:, 0:8], rowsum[:, 0:8]))
            link(dve.tensor_tensor(gates[:, 0:16], gates[:, 0:16], den[:, :], ALU.mult))
            take("la.turned", wide_b, ps_s[:, :])
            after(dve, "la.pv")
            link(dve.tensor_tensor(attn.rearrange("p (h d) -> p h d", h=HEADS),
                                   ps_o[:, 0:D].rearrange("p (h d) -> p h d", h=HEADS),
                                   gates[:, 0:16].unsqueeze(2).broadcast_to([P, HEADS, 16]), ALU.mult))
            take("la.lturned", wide_a[0:64, 0:1024], ps_s[0:64, 0:1024])
            after(dve, "la.lpv")
            dve.tensor_tensor(rem.rearrange("p (h d) -> p h d", h=8),
                              ps_o[:, 512:512 + P].rearrange("p (h d) -> p h d", h=8),
                              rowsum[:, 0:8].unsqueeze(2).broadcast_to([P, 8, 16]), ALU.mult).then_inc(stage("la.rem"), 1)
            take("la.remT", qT[:, 0, :], ps_ring[:, 0:P])
            after(dve, "la.rproj")
            link(dve.tensor_tensor(xn[:, :].rearrange("p (h d) -> p h d", h=HEADS),
                                   ps_ring[:, 512:512 + D].rearrange("p (h d) -> p h d", h=HEADS),
                                   gates[:, 16:32].unsqueeze(2).broadcast_to([P, HEADS, 16]), ALU.mult))
            dve.tensor_tensor(xn[:, :], xn[:, :], attn, ALU.add).then_inc(stage("la.attn"), 1)
            take("la.attnT", xT[:, :, :], ps_ring[:, 0:D].rearrange("p (c n) -> p c n", c=DC))
            add_projection("la.out_ps", ps_o[:, 0:D])

            layernorm("f0", X[:, :], xn[:, :])
            take("f0.xT", xT[:, :, :], ps_ring[:, 0:D].rearrange("p (c n) -> p c n", c=DC))
            take("f0.bias", bin_cols[:, :], ps_ring[:, 512:512 + 8 * HT])
            after(dve, "f0.logits")
            link(dve.tensor_copy(gate[:, 4, 0:8], ps_o[:, 0:8]))
            route("f0", 8, gate[:, 4, 0:8], rev8, True)
            experts("f0", 8, 0)

            layernorm("x1", X[:, :], xn[:, :])
            after(dve, "x1.xn")
            layernorm("xm", xn[:, :], xm[:, :])
            arrived(dve, "x1")
            after(dve, "xm.xn")
            link(dve.tensor_tensor(xm[:, :], xm[:, :], rows[:, LNG, :], ALU.mult))
            dve.tensor_tensor(xm[:, :], xm[:, :], rows[:, LNB, :], ALU.add).then_inc(stage("xm.affine"), 1)
            take("xm.xT", xT[:, :, :], ps_ring[:, 0:D].rearrange("p (c n) -> p c n", c=DC))
            after(dve, "x1.proj")
            link(dve.tensor_scalar(qT[:, :, :], ps_s[:, 0:1024].rearrange("p (t n) -> p t n", t=8), 0.125, None, ALU.mult))
            link(dve.tensor_copy(k_self, ps_s[:, 1024:2048].rearrange("p (t n) -> p t n", t=8)))
            dve.tensor_copy(v_self[:, :], ps_o[:, :]).then_inc(stage("x1.qk"), 1)
            after(dve, "x1.self_scores")
            link(dve.tensor_copy(wide_a, ps_s[:, :]))
            softmax_head("x1.self", wide_a, HEADS, P, negprev[:, :], den[:, :])
            take("x1.turned", wide_b, ps_s[:, :])
            after(dve, "x1.self_pv")
            link(dve.tensor_copy(O[:, :], ps_o[:, :]))
            dve.tensor_copy(negcur[:, :], negprev[:, :]).then_inc(stage("x1.start"), 1)
            after(dve, "x1.start")
            cross(L1)
            link(dve.reciprocal(den[:, :], den[:, :]))
            dve.tensor_tensor(v_self[:, :].rearrange("p (t c d) -> p c t d", t=8, c=2),
                              O[:, :].rearrange("p (c t d) -> p c t d", t=8, c=2),
                              den[:, :].rearrange("p (c t) -> p c t", c=2).unsqueeze(3).broadcast_to([P, 2, 8, 64]),
                              ALU.mult).then_inc(stage("x1.attn"), 1)
            take("x1.attnT", attnT, ps_s[:, 0:1024].rearrange("p (t n) -> p t n", t=8))
            add_projection("x1.out", ps_o[:, 0:D], BO1)

            layernorm("l1", X[:, :], xn[:, :])
            take("l1.wT", wide_b, ps_s[:, :])
            take("l1.xT", xT[:, :, :], ps_ring[:, 0:D].rearrange("p (c n) -> p c n", c=DC))
            after(dve, "l1.proj")
            link(dve.tensor_copy(sp_z, ps_s[:, 0:512]))
            link(dve.memset(v_ext, 1.0))
            link(dve.tensor_copy(v_ext[:, :, 0:16], ps_s[:, 512:512 + D].rearrange("p (h d) -> p h d", h=HEADS)))
            link(dve.tensor_scalar(sp_w, sp_z, -1.0, None, ALU.mult))
            dve.tensor_tensor(sp_a, sp_z, sp_w, ALU.max).then_inc(stage("l1.abs"), 1)
            after(dve, "l1.u")
            dve.tensor_scalar(sp_w, sp_u, 1.0, None, ALU.add).then_inc(stage("l1.w"), 1)
            after(dve, "l1.w")
            link(dve.scalar_tensor_tensor(out=sp_u, in0=sp_w, scalar=-1.0, in1=sp_u, op0=ALU.add, op1=ALU.subtract))
            after(dve, "l1.ln")
            link(dve.reciprocal(sp_w, sp_w))
            link(dve.tensor_tensor(sp_u, sp_u, sp_w, ALU.mult))
            link(dve.tensor_tensor(sp_a, sp_a, sp_u, ALU.subtract))
            link(dve.tensor_scalar(sp_z, sp_z, 0.0, None, ALU.max))
            link(dve.tensor_tensor(sp_z, sp_z, sp_a, ALU.add))
            link(dve.tensor_scalar(sp_z, sp_z, 1e-6, None, ALU.add))
            link(head_queries(sp_z[:, 0:P], 0, kz[:, 0, :, :]))
            head_queries(sp_z[:, P:2 * P], 1, kz[:, 1, :, :]).then_inc(stage("l1.qz"), 1)
            after(dve, "l1.scores")
            dve.tensor_tensor(wide_a.rearrange("p (h k) -> p h k", h=HEADS),
                              ps_s[:, :].rearrange("p (h k) -> p h k", h=HEADS),
                              causal[:, :].unsqueeze(1).broadcast_to([P, HEADS, P]), ALU.mult).then_inc(stage("l1.causal"), 1)
            after(dve, "l1.pv")
            pv = ps_o[:, 0:HEADS * 17].rearrange("p (h d) -> p h d", h=HEADS)
            link(dve.tensor_scalar(den[:, :], pv[:, :, 16], 1e-6, None, ALU.add))
            link(dve.reciprocal(den[:, :], den[:, :]))
            dve.tensor_tensor(xn[:, :].rearrange("p (h d) -> p h d", h=HEADS), pv[:, :, 0:16],
                              den[:, :].unsqueeze(2).broadcast_to([P, HEADS, 16]), ALU.mult).then_inc(stage("l1.attn"), 1)
            take("l1.attnT", xT[:, :, :], ps_ring[:, 0:D].rearrange("p (c n) -> p c n", c=DC))
            add_projection("l1.out", ps_o[:, 512:512 + D])

            layernorm("f1", X[:, :], xn[:, :])
            take("f1.xT", xT[:, :, :], ps_ring[:, 0:D].rearrange("p (c n) -> p c n", c=DC))
            take("f1.bias", b1_cols[:, :], ps_ring[:, 512:512 + P])
            after(dve, "f1.logits")
            arrived(dve, "f1")
            link(dve.tensor_tensor(gate[:, 4, 0:16], ps_o[:, 0:16], br1[:, :], ALU.add))
            route("f1", 16, gate[:, 4, 0:16], rev16, False)
            experts("f1", 16, 8)
            dve.tensor_copy(gate[:, 0, 0:1], X[:, 0:1]).then_inc(stage("f1.done"), 1)

        @block.tensor
        def _(pe):
            def turn(src, dst, n):
                for t in range(n):
                    ins = pe.transpose(dst[:, t * P:(t + 1) * P], src[:, t * P:(t + 1) * P], ident[:, :])
                return ins

            def project(dst, lhs, rhs, chunks=DC):
                for c in range(chunks):
                    ins = pe.matmul(dst, lhs(c), rhs(c), start=c == 0, stop=c == chunks - 1)
                return ins

            def turn_norm(tag, ready, src):
                after(pe, ready)
                turn(src, ps_ring[:, 0:D], DC).then_inc(stage(tag), 1)

            def next_keys(L, b, j, first=False):
                def free(jj):
                    if not (first and jj < j + 2):
                        pe.wait_ge(L.ring_free[jj % 2], L.seq(b, jj) - 1)
                w = wk0 if L is L0 else wm1
                pe.wait_ge(L.ctx_in, 16 if first else (b + 2) * 16)
                ranges = ((0, SPLIT), (SPLIT, TILES))
                for c in range(DC):
                    for r, (t0, t1) in enumerate(ranges):
                        jj = j + 2 * c + r
                        free(jj)
                        for t in range(t0, t1):
                            col = r * 512 + (t - t0) * P
                            ins = pe.transpose(ps_ring[:, col:col + P], ctx_nat[:, t, c * P:(c + 1) * P], ident[:, :])
                        ins.then_inc(L.ring_full[r], 1)
                pe.wait_ge(L.ring_free[0], L.seq(b, j + 2 * DC - 2))
                pe.wait_ge(L.ring_free[1], L.seq(b, j + 2 * DC - 1))
                for f in range(L.k_tiles):
                    for r, (t0, t1) in enumerate(ranges):
                        jj = j + 2 * DC + 2 * f + r
                        free(jj)
                        n = (t1 - t0) * P
                        project(ps_ring[:, r * 512:r * 512 + n], lambda c: w[:, c, f * P:(f + 1) * P],
                                lambda c: ctxT[:, c, t0 * P:t1 * P]).then_inc(L.ring_full[r], 1)

            def cross_block(L, b, more):
                first = isinstance(b, int) and b == 0
                def scores(h):
                    n = h % 2
                    used = L.blkmax if L.masked else L.probs
                    if h >= 2:
                        pe.wait_ge(used, b * HEADS + h - 1)
                    elif not first:
                        pe.wait_ge(used, b * HEADS + h - 1)
                    for t0, t1 in ((0, SPLIT), (SPLIT, TILES)):
                        dst = ps_s[:, 1024 * n + t0 * P:1024 * n + t1 * P]
                        if L is L0:
                            ins = pe.matmul(dst, qz[:, h // 8, h % 8, :], kT[:, h // 8, t0 * P:t1 * P],
                                            start=True, stop=True)
                        else:
                            base = 64 * (h // 8)
                            ins = pe.matmul(dst, qT[base:base + 64, h % 8, :], kT[base:base + 64, h % 8, t0 * P:t1 * P],
                                            start=True, stop=True)
                    ins.then_inc(L.scores, 1)

                def turn_probs(h):
                    j = L.j_probs(h, more)
                    pe.wait_ge(L.probs, b * HEADS + h + 1)
                    for r, (t0, t1) in enumerate(((0, SPLIT), (SPLIT, TILES))):
                        pe.wait_ge(L.ring_free[r], L.seq(b, j + r) - 1)
                        turn(probs[:, h % 2, t0 * P:t1 * P], ps_ring[:, r * 512:(r + 1) * 512],
                             t1 - t0).then_inc(L.ring_full[r], 1)

                def weighted(h):
                    j = L.j_probs(h, more)
                    pe.wait_ge(L.ring_free[0], L.seq(b, j))
                    pe.wait_ge(L.ring_free[1], L.seq(b, j + 1))
                    if h == 0 and not first:
                        pe.wait_ge(L.acc, b)
                    head = h if L is L0 else 2 * (h % 8) + h // 8
                    for t in range(TILES):
                        v = v0[:, t * D + head * 16:t * D + head * 16 + 16] if L is L0 else \
                            vals[:, t, head * 64:(head + 1) * 64]
                        ins = pe.matmul(ps_o[:, h * L.dv:(h + 1) * L.dv], probsT[:, h % 2, t * P:(t + 1) * P], v,
                                        start=t == 0, stop=t == TILES - 1)
                    if h == HEADS - 1:
                        ins.then_inc(L.pv, 1)

                def values():
                    for j in range(L.vgroups):
                        pe.wait_ge(L.ring_free[j % 2], L.seq(b, j) - 1)
                        bank = ps_ring[:, (j % 2) * 512:(j % 2) * 512 + 512]
                        if L is L0:
                            for t in range(2 * j, min(2 * j + 2, TILES)):
                                ins = project(bank[:, (t % 2) * D:(t % 2) * D + D],
                                              lambda c: ctxT[:, c, t * P:(t + 1) * P], lambda c: wv0[:, c, :])
                        else:
                            t = j // 2
                            for f in range(4):
                                ins = pe.transpose(bank[:, f * P:(f + 1) * P],
                                                   kT[:, 4 * (j % 2) + f, t * P:(t + 1) * P], ident[:, :])
                        ins.then_inc(L.ring_full[j % 2], 1)

                if first:
                    pe.wait_ge(L.ring_free[0], L.seq(0, -2))
                    pe.wait_ge(L.ring_free[1], L.seq(0, -1))
                else:
                    pe.wait_ge(L.ring_free[0], L.seq(b, -4))
                    pe.wait_ge(L.ring_free[1], L.seq(b, -3))
                scores(0)
                scores(1)
                values()
                turn_probs(0)
                for h in range(2, HEADS):
                    scores(h)
                    turn_probs(h - 1)
                    weighted(h - 2)
                if more:
                    next_keys(L, b, L.j_keys())
                turn_probs(HEADS - 1)
                weighted(HEADS - 2)
                weighted(HEADS - 1)

            def cross(L):
                next_keys(L, 0, -L.kgroups, True)
                cross_block(L, 0, True)
                with pe.Fori(0, NBLK - 2) as i:
                    cross_block(L, i + 1, True)
                cross_block(L, NBLK - 1, False)

            def experts(tag, E, base):
                after(pe, tag + ".comb")
                pe.transpose(ps_o[0:E, 0:P], comb[:, 0:E], ident[:, :]).then_inc(stage(tag + ".combT"), 1)
                after(pe, tag + ".combT.sb")
                b_out = bout0 if base == 0 else b2_1
                pe.matmul(ps_o[:, 512:512 + D], combT[0:E, :], b_out[0:E, :], start=True,
                          stop=True).then_inc(stage(tag + ".bias_ps"), 1)
                after(pe, tag + ".bias.sb")
                after(pe, tag + ".bias_used")

                def round_of_experts(i):
                    for j in range(SLOTS):
                        e = i * SLOTS + (base + j)
                        fresh = isinstance(e, int) and e < 2
                        pe.wait_ge(expert_in[j], (i + (base // SLOTS + 1)) * 32)
                        for half in range(2):
                            if not fresh:
                                pe.wait_ge(hid_ready, e * 2 + (half - 3))
                            for t in range(4):
                                m = half * 4 + t
                                col = ((j % 2) * 2 + half) * 512 + t * P
                                ins = project(ps_s[:, col:col + P], lambda c: win[:, j, c, m * P:(m + 1) * P],
                                              lambda c: xT[:, c, :])
                            ins.then_inc(hid_full, 1)
                        if not fresh:
                            pe.wait_ge(y_added, e - 1)
                        for half in range(2):
                            pe.wait_ge(hid_ready, e * 2 + (half + 1))
                            for t in range(4):
                                m = half * 4 + t
                                ins = pe.matmul(ps_o[:, (j % 2) * 512:(j % 2) * 512 + D], hT[:, j % 2, m, :],
                                                wout[:, j, m, :], start=m == 0, stop=m == HT - 1)
                        ins.then_inc(y_full, 1)

                expert_rounds(pe, E, round_of_experts)

            after(pe, "ident")
            turn_norm("x0.xT", "x0.xn", xn)
            arrived(pe, "x0")
            after(pe, "x0.xT.sb")
            for e in range(DC):
                ins = project(ps_o[:, e * P:(e + 1) * P], lambda c: wq0[:, c, e * P:(e + 1) * P], lambda c: xT[:, c, :])
            ins.then_inc(stage("x0.q"), 1)
            after(pe, "x0.qz")
            cross(L0)
            turn_norm("x0.attnT", "x0.attn", xn)
            arrived(pe, "x0b")
            after(pe, "x0.attnT.sb")
            project(ps_o[:, 0:D], lambda c: xT[:, c, :], lambda c: wo0[:, c, :]).then_inc(stage("x0.out"), 1)

            turn_norm("la.xT", "la.xn", xn)
            arrived(pe, "la")
            after(pe, "la.xT.sb")
            for e in range(DC):
                cut = slice(e * P, (e + 1) * P)
                project(ps_s[:, e * P:(e + 1) * P], lambda c: la_wq[:, c, cut], lambda c: xT[:, c, :])
                project(ps_s[:, D + e * P:D + (e + 1) * P], lambda c: la_wk[:, c, cut], lambda c: xT[:, c, :])
            project(ps_s[:, 512:512 + D], lambda c: xT[:, c, :], lambda c: la_wv[:, c, :])
            project(ps_s[:, 512 + D:1024], lambda c: xT[:, c, :], lambda c: la_wq[:, c, :])
            project(ps_s[:, 1024:1024 + P], lambda c: la_wgq[:, c, :], lambda c: xT[:, c, :])
            project(ps_s[:, 1024 + P:1024 + P + 64], lambda c: la_wgk[:, c, :], lambda c: xpool[:, c, :])
            project(ps_s[0:64, 1536:1536 + P], lambda c: xpool[:, c, :],
                    lambda c: la_wgv[:, c, :]).then_inc(stage("la.proj"), 1)
            after(pe, "la.kz")
            for g in range(4):
                pe.matmul(ps_s[:, g * 512:(g + 1) * 512], qT[:, g // 2, :], kflat[:, g * 512:(g + 1) * 512],
                          start=True, stop=True)
            pe.matmul(ps_ring[:, 0:512], qT[:, 4, :], kflat[:, 2048:2560], start=True,
                      stop=True).then_inc(stage("la.scores"), 1)
            after(pe, "la.local.exps")
            turn(wide_a, ps_s, HEADS).then_inc(stage("la.turned"), 1)
            after(pe, "la.turned.sb")
            for h in range(HEADS):
                ins = pe.matmul(ps_o[:, h * 16:(h + 1) * 16], wide_b[:, h * P:(h + 1) * P],
                                v_nat[:, h * 16:(h + 1) * 16], start=True, stop=True)
            ins.then_inc(stage("la.pv"), 1)
            after(pe, "la.lat.exps")
            for h in range(8):
                ins = pe.transpose(ps_s[0:64, h * P:(h + 1) * P], lat_s[:, h * 64:(h + 1) * 64], ident[:, :])
            ins.then_inc(stage("la.lturned"), 1)
            after(pe, "la.lturned.sb")
            for h in range(8):
                ins = pe.matmul(ps_o[:, 512 + h * 16:512 + (h + 1) * 16], wide_a[0:64, h * P:(h + 1) * P],
                                gv_nat[:, h * 16:(h + 1) * 16], start=True, stop=True)
            ins.then_inc(stage("la.lpv"), 1)
            after(pe, "la.rem")
            turn(rem, ps_ring[:, 0:P], 1).then_inc(stage("la.remT"), 1)
            after(pe, "la.remT.sb")
            pe.matmul(ps_ring[:, 512:512 + D], qT[:, 0, :], la_rout[:, :], start=True,
                      stop=True).then_inc(stage("la.rproj"), 1)
            turn_norm("la.attnT", "la.attn", xn)
            after(pe, "la.attnT.sb")
            project(ps_o[:, 0:D], lambda c: xT[:, c, :], lambda c: la_wout[:, c, :]).then_inc(stage("la.out_ps"), 1)

            arrived(pe, "f0")
            pe.transpose(ps_ring[:, 512:512 + 8 * HT], bin_rows[0:8 * HT, :],
                         ident[0:8 * HT, 0:8 * HT]).then_inc(stage("f0.bias"), 1)
            turn_norm("f0.xT", "f0.xn", xn)
            after(pe, "f0.xT.sb")
            project(ps_o[:, 0:8], lambda c: xT[:, c, :], lambda c: wgate0[:, c, :]).then_inc(stage("f0.logits"), 1)
            experts("f0", 8, 0)

            turn_norm("xm.xT", "xm.affine", xm)
            arrived(pe, "x1big")
            arrived(pe, "x1")
            after(pe, "xm.xT.sb")
            for t in range(8):
                cut = slice(t * P, (t + 1) * P)
                project(ps_s[:, t * P:(t + 1) * P], lambda c: WQ1[:, c, cut], lambda c: xT[:, c, :])
                project(ps_s[:, 1024 + t * P:1024 + (t + 1) * P], lambda c: WKV1[:, c, cut], lambda c: xT[:, c, :])
            for g in range(2):
                ins = project(ps_o[:, g * 512:(g + 1) * 512], lambda c: xT[:, c, :],
                              lambda c: WKV1[:, c, 1024 + g * 512:1024 + (g + 1) * 512])
            ins.then_inc(stage("x1.proj"), 1)
            after(pe, "x1.qk")
            for t in range(8):
                for c in range(2):
                    n = c * 8 + t
                    ins = pe.matmul(ps_s[:, n * P:(n + 1) * P], qT[64 * c:64 * c + 64, t, :],
                                    k_self[64 * c:64 * c + 64, t, :], start=True, stop=True)
            ins.then_inc(stage("x1.self_scores"), 1)
            after(pe, "x1.self.exps")
            turn(wide_a, ps_s, HEADS).then_inc(stage("x1.turned"), 1)
            after(pe, "x1.turned.sb")
            for n in range(HEADS):
                head = 2 * (n % 8) + n // 8
                ins = pe.matmul(ps_o[:, n * 64:(n + 1) * 64], wide_b[:, n * P:(n + 1) * P],
                                v_self[:, head * 64:(head + 1) * 64], start=True, stop=True)
            ins.then_inc(stage("x1.self_pv"), 1)
            after(pe, "x1.start")
            cross(L1)
            after(pe, "x1.attn")
            turn(v_self, ps_s, 8).then_inc(stage("x1.attnT"), 1)
            after(pe, "x1.attnT.sb")
            project(ps_o[:, 0:D], lambda c: attnT[:, c, :], lambda c: wo1[:, c, :], 8).then_inc(stage("x1.out"), 1)

            arrived(pe, "la1")
            for i, w in enumerate((wq0, wk0, wv0, wo0)):
                for c in range(DC):
                    for e in range(DC):
                        col = i * 512 + c * D + e * P
                        ins = pe.transpose(ps_s[:, col:col + P], w[:, e, c * P:(c + 1) * P], ident[:, :])
            ins.then_inc(stage("l1.wT"), 1)
            turn_norm("l1.xT", "l1.xn", xn)
            after(pe, "l1.wT.sb")
            after(pe, "l1.xT.sb")
            for e in range(DC):
                for i in range(2):
                    col = i * D + e * P
                    project(ps_s[:, col:col + P], lambda c: wT[:, i, c, e * P:(e + 1) * P], lambda c: xT[:, c, :])
            project(ps_s[:, 512:512 + D], lambda c: xT[:, c, :], lambda c: wT[:, 2, c, :]).then_inc(stage("l1.proj"), 1)
            after(pe, "l1.qz")
            for g in range(4):
                e = g // 2
                ins = pe.matmul(ps_s[:, g * 512:(g + 1) * 512], sp_z[:, D + e * P:D + (e + 1) * P],
                                kflat[:, g * 512:(g + 1) * 512], start=True, stop=True)
            ins.then_inc(stage("l1.scores"), 1)
            after(pe, "l1.causal")
            for h in range(HEADS):
                ins = pe.matmul(ps_o[:, h * 17:(h + 1) * 17], wide_a[:, h * P:(h + 1) * P], v_ext[:, h, :],
                                start=True, stop=True)
            ins.then_inc(stage("l1.pv"), 1)
            turn_norm("l1.attnT", "l1.attn", xn)
            after(pe, "l1.attnT.sb")
            project(ps_o[:, 512:512 + D], lambda c: xT[:, c, :], lambda c: wT[:, 3, c, :]).then_inc(stage("l1.out"), 1)

            arrived(pe, "f1")
            pe.transpose(ps_ring[:, 512:512 + P], b1_rows[:, :], ident[:, :]).then_inc(stage("f1.bias"), 1)
            turn_norm("f1.xT", "f1.xn", xn)
            after(pe, "f1.xT.sb")
            project(ps_o[:, 0:16], lambda c: xT[:, c, :], lambda c: wr1[:, c, :]).then_inc(stage("f1.logits"), 1)
            experts("f1", 16, 8)


_OUT_SHAPE = (1, P, D)


def kernel(**inputs):
    import concourse.bacc as _bacc
    from concourse.bass_utils import run_bass_kernel_spmd as _run

    nc = _bacc.Bacc("TRN2", target_bir_lowering=False, num_devices=1)
    arrays, args = {}, {}
    for name, value in inputs.items():
        v = np.ascontiguousarray(value)
        arrays[f"in_{name}_dram"] = v
        args[name] = nc.dram_tensor(f"in_{name}_dram", v.shape, mybir.dt.from_np(v.dtype), kind="ExternalInput").ap()
    out = nc.dram_tensor("out_0_dram", _OUT_SHAPE, FP32, kind="ExternalOutput").ap()
    perceiver(nc, args, out)
    r = _run(nc, [arrays], core_ids=[0])
    return r.results[0]["out_0_dram"]
```

```python
import numpy as np
import concourse.bass as bass
from concourse import mybir
from concourse.alu_op_type import AluOpType as ALU
from contextlib import ExitStack

ACT = mybir.ActivationFunctionType
AX = mybir.AxisListType
FP32 = mybir.dt.float32
FP16 = mybir.dt.float16
INT32 = mybir.dt.int32

P = 128
D = 256
DC = D // P
KEYS = 12544
TILES = 7
BLK = TILES * P
NBLK = KEYS // BLK
HEADS = 16
SPLIT = 4
WSCALE = 16.0
MASKED = -1.0e12
HUGE = 3.0e38
HID = 1024
HT = HID // P
SLOTS = 2


class Cross:

    def __init__(self, name, head_dim, feature_cols, masked, sem):
        self.name = name
        self.dv = head_dim
        self.cols = feature_cols
        self.masked = masked
        self.together = 64 // head_dim if head_dim < 64 else 2
        self.width = P // self.together
        self.turns = HEADS * head_dim // 32 if head_dim < 64 else HEADS
        self.heads_per_turn = HEADS // self.turns
        if feature_cols == 512:
            self.natural = [(t, 0, 512) for t in range(TILES - 1)] + [(TILES - 1, 0, 256), (TILES - 1, 256, 256)]
        else:
            self.natural = [(t, f, 512) for t in range(TILES) for f in (0, 512)]
        order = [("natural", n) for n in range(len(self.natural))]
        self.first_keys = 2 if self.heads_per_turn == 1 else 1
        order += [("keys", x) for x in range(self.first_keys)]
        for h in range(HEADS):
            if self.keys_after(h) is not None:
                order.append(("keys", self.keys_after(h)))
            if h >= 2:
                order += [("probs", h - 2, 0), ("probs", h - 2, 1)]
        order += [("probs", HEADS - 2, 0), ("probs", HEADS - 2, 1)]
        self.context = [("context", c, r) for c in range(DC) for r in range(2)]
        last = [("probs", HEADS - 1, 0), ("probs", HEADS - 1, 1)]
        self.order = {True: order + self.context + last, False: order + last}
        self.groups = len(self.order[True])
        assert self.groups % 2 == 0
        self.split = [g for g in self.order[True] if g[0] != "keys"]
        self.ctx_in = sem(name + "_ctx_in")
        self.ring_full = [sem(name + "_ring_full_even"), sem(name + "_ring_full_odd")]
        self.ring_free = [sem(name + "_ring_free_even"), sem(name + "_ring_free_odd")]
        self.high = sem(name + "_high")
        self.scores = sem(name + "_scores")
        self.blkmax = sem(name + "_blkmax")
        self.negmax = sem(name + "_negmax")
        self.probs = sem(name + "_probs")
        self.shift = sem(name + "_shift")
        self.corr = sem(name + "_corr")
        self.corr_rows = sem(name + "_corr_rows")
        self.sums = sem(name + "_sums")
        self.pv = sem(name + "_pv")
        self.scaled = sem(name + "_scaled")
        self.acc = sem(name + "_acc")

    def keys_after(self, h):
        if self.heads_per_turn == 1:
            return h + 2 if h + 2 < HEADS else None
        return h // 2 + 1 if h % 2 == 0 and h // 2 + 1 < self.turns else None

    def at(self, b, group, more=True):
        j = self.order[more].index(group)
        return j % 2, b * (self.groups // 2) + (len(self.context) // 2 + j // 2 + 1)

    def at_first(self, group):
        j = self.context.index(group)
        return j % 2, j // 2 + 1

    def high_at(self, b, group, more=True):
        left_out = 0 if more or group not in self.order[False][-2:] else len(self.context)
        return b * len(self.split) + (len(self.context) + self.split.index(group) + 1 - left_out)


def perceiver(nc, a, out):
    ctx = ExitStack()
    with ctx:
        def sb(name, shape, dt=FP32):
            return ctx.enter_context(nc.sbuf_tensor(name, shape, dt))

        def sem(name):
            return ctx.enter_context(nc.semaphore(name))

        norms = ["x0", "la", "f0", "x1", "xm", "l1", "f1"]
        turned_norms = ["x0", "la", "f0", "xm", "l1", "f1"]
        attentions = ["la", "l1"]
        routed = ["f0", "f1"]
        shared = {"var": norms, "sd": norms, "xn": norms, "xT": turned_norms, "xT.sb": turned_norms,
                  "attn": attentions, "attnT": attentions, "attnT.sb": attentions,
                  "bias": routed, "bias.sb": routed, "logits": routed, "top": routed, "exp": routed, "comb": routed,
                  "combT": routed, "combT.sb": routed, "bias_ps": routed, "bias_used": routed}
        stages = {}

        def place(name):
            phase, _, step = name.partition(".")
            return (step, shared[step].index(phase) + 1) if step in shared else (name, 1)

        def stage(name):
            key = place(name)[0]
            if key not in stages:
                stages[key] = sem("step_" + key.replace(".", "_"))
            return stages[key]

        X = sb("X", [P, D])
        xn = sb("xn", [P, D])
        xm = sb("xm", [P, D])
        xT = sb("xT", [P, DC, P])
        ident = sb("ident", [P, P])
        headmask = sb("headmask", [P, 8])
        window = sb("window", [P, P])
        latmask = sb("latmask", [P, 64])
        causal = sb("causal", [P, P])
        rev8 = sb("rev8", [P, 8])
        rev16 = sb("rev16", [P, 16])
        stats = sb("stats", [P, 6])
        meanvar = sb("meanvar", [P, 2])
        sd = sb("sd", [P, 2])
        ctx_nat = sb("ctx_nat", [P, TILES, D])
        ctxT = sb("ctxT", [P, 2, DC, BLK], FP16)
        kT = sb("kT", [P, 4, BLK], FP16)
        vals = sb("vals", [P, TILES * 2048], FP16)
        probs = sb("probs", [P, 2, 1024])
        probsT = sb("probsT", [P, 8, 2, BLK], FP16)
        q16 = sb("q16", [P, HEADS, 2, P], FP16)
        w16 = sb("w16", [P, DC, 2, 1024], FP16)
        bk16 = sb("bk16", [2, D], FP16)
        bkf = sb("bkf", [2, 3 * D])
        ident16 = sb("ident16", [P, P], FP16)
        ones16 = sb("ones16", [2, P], FP16)
        masked_s = sb("masked_s", [P, 2, BLK])
        mask_raw = sb("mask_raw", [P, BLK], INT32)
        mask_add = sb("mask_add", [P, BLK])
        O = sb("O", [P, 1024])
        den = sb("den", [P, HEADS])
        negcur = sb("negcur", [P, HEADS])
        negprev = sb("negprev", [P, HEADS])
        blkmax = sb("blkmax", [P, HEADS])
        rowsum = sb("rowsum", [P, HEADS])
        shift = sb("shift", [P, HEADS])
        factors = sb("factors", [P, 1024])
        wq0 = sb("wq0", [P, DC, D])
        wk0 = sb("wk0", [P, DC, D])
        wv0 = sb("wv0", [P, DC, D])
        wox = sb("wox", [P, 4, D])
        bvcol = sb("bvcol", [P, 4])
        la_wq = sb("la_wq", [P, DC, D])
        la_wk = sb("la_wk", [P, DC, D])
        la_wv = sb("la_wv", [P, DC, D])
        la_wgq = sb("la_wgq", [P, DC, P])
        la_wgk = sb("la_wgk", [P, DC, P])
        la_wgv = sb("la_wgv", [P, DC, P])
        la_rout = sb("la_rout", [P, D])
        la_wout = sb("la_wout", [P, DC, D])
        wo1 = sb("wo1", [P, 8, D])
        rows = sb("rows", [P, 7, D])
        BQ0, BO0, GL, GR, LNG, LNB, BO1 = range(7)
        wgate0 = sb("wgate0", [P, DC, 8])
        wr1 = sb("wr1", [P, DC, 16])
        br1 = sb("br1", [P, 16])
        bout0 = sb("bout0", [8, D])
        b2_1 = sb("b2_1", [16, D])
        bin_rows = sb("bin_rows", [P, P])
        b1_rows = sb("b1_rows", [P, P])
        bin_cols = sb("bin_cols", [P, 8 * HT])
        b1_cols = sb("b1_cols", [P, 16 * HT])
        win = sb("win", [P, SLOTS, DC, HID])
        wout = sb("wout", [P, SLOTS, HT, D])
        gate = sb("gate", [P, 8, 16])
        comb = sb("comb", [P, 16])
        combT = sb("combT", [16, P])
        pad = sb("pad", [P, 2])
        gatecol = sb("gatecol", [P, 8])
        gates = sb("gates", [P, 32])
        kflat = probsT[:, :, :, :].rearrange("p a b c -> p (a b c)").bitcast(FP32)
        vflat = vals[:, :].bitcast(FP32)
        wide_a = probs[:, :, :].rearrange("p a b -> p (a b)")
        wide_b = vflat[:, 0:2048]
        v_self = vflat[:, 6144:7168]
        wm1 = wide_a.rearrange("p (c n) -> p c n", c=DC)
        qT = q16[:, :, :, :].rearrange("p h t q -> p (h t q)").bitcast(FP32)[:, 0:1024].rearrange("p (t q) -> p t q", t=8)
        hT = vflat[:, 4096:4096 + 2 * HID].rearrange("p (s t n) -> p s t n", s=2, t=HT)
        attn = kflat[:, 4224:4224 + D]
        kflat16 = probsT[:, :, :, :].rearrange("p a b c -> p (a b c)")
        qx = kflat16[:, 0:4096]
        qhi = kflat16[:, 4096:5120]
        qlo = kflat16[:, 5120:6144]
        qn = masked_s[:, :, :].rearrange("p a b -> p (a b)")[:, 0:1024]
        kz = kflat[:, 0:2048].rearrange("p (e h k) -> p e h k", e=2, h=8)
        gkz = kflat[:, 2048:2560].rearrange("p (h k) -> p h k", h=8)
        lat_s = kflat[:, 2560:3072]
        q_nat = kflat[:, 3072:3328]
        v_nat = kflat[:, 3328:3584]
        gv_nat = kflat[0:64, 3584:3712]
        rem = kflat[:, 3712:3840]
        xpool = kflat[:, 3840:3968].rearrange("p (c n) -> p c n", c=DC)
        k_self = kflat[:, 6144:7168].rearrange("p (t n) -> p t n", t=8)
        v_ext = kflat[:, 2048:2048 + HEADS * 17].rearrange("p (h d) -> p h d", h=HEADS)
        sp_z, sp_a, sp_w, sp_u = (kflat[:, 4096 + 512 * i:4096 + 512 * (i + 1)] for i in range(4))
        wT = wide_b.rearrange("p (w c n) -> p w c n", w=4, c=DC)

        ps_s = ctx.enter_context(nc.psum_tensor("ps_s", [P, 4 * 512], FP32))
        ps_ring = ctx.enter_context(nc.psum_tensor("ps_ring", [P, 2 * 512], FP32))
        ps_o = ctx.enter_context(nc.psum_tensor("ps_o", [P, 2 * 512], FP32))

        ps_s16 = ps_s[:, :].bitcast(FP16)
        L0 = Cross("x0", 16, 512, True, sem)
        L1 = Cross("x1", 64, 1024, False, sem)

        def by_row(L):
            return factors[:, 0:HEADS * L.width].rearrange("p (h w) -> p h w", h=HEADS)

        def natural(L, t, heads, part):
            per = 2 * L.cols
            v = vals[:, t * per:(t + 1) * per].rearrange("p (h part d) -> p h part d", part=2, d=L.dv)
            return v[:, heads, part, :]

        def natural_group(L, n, part):
            t, f, w = L.natural[n]
            return natural(L, t, slice(f // L.dv, (f + w) // L.dv), part)

        def stationary(L, t, head, parts):
            at = t * 2 * L.cols + (head + (HEADS if L is L0 else 0)) * 2 * L.dv
            return vals[:, at + parts.start * L.dv:at + parts.stop * L.dv]
        mask_in = sem("mask_in")
        mask_ready = sem("mask_ready")
        expert_in = [sem(f"expert_in{s}") for s in range(SLOTS)]
        hid_full = sem("hid_full")
        hid_ready = sem("hid_ready")
        y_full = sem("y_full")
        y_added = sem("y_added")
        loads = {k: sem("load_" + k) for k in ("x", "x0", "x0b", "la", "f0", "x1", "x1big", "la1", "f1")}
        stored = sem("stored")
        act_step = sem("act_step")
        dve_step = sem("dve_step")
        pool_step = sem("pool_step")

        def chunked(w):
            return w.rearrange("(c p) n -> p c n", p=P)

        def row(v, n=D):
            return v.rearrange("(a n) -> a n", a=1).broadcast_to([P, n])

        LOADS = {
            "x": [(X[:, :], a["x"].rearrange("a s d -> (a s) d"))],
            "x0": [(wq0[:, :, :], chunked(a["L0_xattn_Wq"])), (wk0[:, :, :], chunked(a["L0_xattn_Wk"])),
                   (wv0[:, :, :], chunked(a["L0_xattn_Wv"])),
                   (rows[:, BQ0, :], row(a["L0_xattn_bq"])),
                   (bkf[:, 0:D], a["L0_xattn_bk"].rearrange("(a n) -> a n", a=1).broadcast_to([2, D]))],
            "x0b": [(wox[i * 32 + part * 16:i * 32 + part * 16 + 16, :, :],
                     a["L0_xattn_Wo"].rearrange("(g i d) n -> i d g n", g=4, i=4)[i])
                    for i in range(4) for part in range(2)]
                   + [(bvcol[i * 32:i * 32 + 16, :], a["L0_xattn_bv"].rearrange("(g i d) -> i d g", g=4, i=4)[i])
                      for i in range(4)]
                   + [(rows[:, BO0, :], row(a["L0_xattn_bo"]))],
            "la": [(la_wq[:, :, :], chunked(a["L0_attn_wq"])), (la_wk[:, :, :], chunked(a["L0_attn_wk"])),
                   (la_wv[:, :, :], chunked(a["L0_attn_wv"])), (la_wgq[:, :, :], chunked(a["L0_attn_wgq"])),
                   (la_wgk[:, :, :], chunked(a["L0_attn_wgk"])), (la_wgv[:, :, :], chunked(a["L0_attn_wgv"])),
                   (la_rout[:, :], a["L0_attn_r_out_w"]), (la_wout[:, :, :], chunked(a["L0_attn_w_out"])),
                   (rows[:, GL, :], row(a["L0_attn_gate_local_w"].rearrange("h d -> (h d)"))),
                   (rows[:, GR, :], row(a["L0_attn_gate_remote_w"].rearrange("h d -> (h d)")))],
            "f0": [(wgate0[:, :, :], chunked(a["L0_ffn_W_gate"])), (bout0[:, :], a["L0_ffn_b_out"]),
                   (bin_rows[0:8 * HT, :], a["L0_ffn_b_in"].rearrange("e (t p) -> (e t) p", p=P))],
            "x1": [(wo1[:, :, :], chunked(a["L1_xattn_Wo"])),
                   (rows[:, LNG, :], row(a["L1_xattn_ln_g"])), (rows[:, LNB, :], row(a["L1_xattn_ln_b"])),
                   (rows[:, BO1, :], row(a["L1_xattn_bo"]))],
            "x1big": [(kflat[:, 4096:6144].rearrange("p (c n) -> p c n", c=DC), chunked(a["L1_xattn_Wq"])),
                      (vflat[:, 0:4096].rearrange("p (c n) -> p c n", c=DC), chunked(a["L1_xattn_Wkv"])),
                      (wm1, chunked(a["L1_xattn_Wm"]))],
            "la1": [(la_wq[:, :, :], chunked(a["L1_attn_Wq"])), (la_wk[:, :, :], chunked(a["L1_attn_Wk"])),
                    (la_wv[:, :, :], chunked(a["L1_attn_Wv"])), (la_wout[:, :, :], chunked(a["L1_attn_Wo"]))],
            "f1": [(wr1[:, :, :], chunked(a["L1_ffn_Wr"])), (br1[:, :], row(a["L1_ffn_br"], 16)),
                   (b2_1[:, :], a["L1_ffn_b2"]), (b1_rows[:, :], a["L1_ffn_b1"].rearrange("e (t p) -> (e t) p", p=P))],
        }
        WQ1 = LOADS["x1big"][0][0]
        WKV1 = LOADS["x1big"][1][0]
        ctx_blocks = a["ctx_1024"].rearrange("a (b p t) d -> (a b) p t d", p=P, t=TILES)
        mask_blocks = a["mask_Bx1xSxS2_ik1"].rearrange("a c q (b n) -> (a c b) q n", n=BLK)

        def arrived(eng, key):
            eng.wait_ge(loads[key], 16 * len(LOADS[key]))

        def after(eng, name):
            eng.wait_ge(stage(name), place(name)[1])

        def expert_rounds(eng, E, body):
            body(0)
            with eng.Fori(0, E // SLOTS - 1) as i:
                body(i + 1)

        block = ctx.enter_context(nc.Block())

        @block.sync
        def _(sp):
            def load(key):
                for dst, src in LOADS[key]:
                    with nc.allow_non_contiguous_dma(reason="a bias vector of 256 values as columns"):
                        sp.dma_start(dst, src).then_inc(loads[key], 16)

            def load_bias_rows():
                after(sp, "bvcol")
                load("x0b")

            def ctx_load(L, b):
                sp.dma_start(ctx_nat[:, :, :], ctx_blocks[b]).then_inc(L.ctx_in, 16)

            def mask_load(b):
                sp.dma_start(mask_raw[:, :], mask_blocks[b]).then_inc(mask_in, 16)

            def expert_load(w1, w2, e, slot):
                sp.dma_start(win[:, slot, :, :], w1[e].rearrange("(c p) n -> p c n", p=P)).then_inc(expert_in[slot], 16)
                sp.dma_start(wout[:, slot, :, :], w2[e].rearrange("(t p) n -> p t n", p=P)).then_inc(expert_in[slot], 16)

            def ctx_stream(L):
                for g in L.context[-2:]:
                    bank, seq = L.at_first(g)
                    sp.wait_ge(L.ring_full[bank], seq)
                ctx_load(L, 1)
                if L.masked:
                    sp.wait_ge(mask_ready, 1)
                    mask_load(1)
                with sp.Fori(0, NBLK - 2) as i:
                    for g in L.context[-2:]:
                        bank, seq = L.at(i, g)
                        sp.wait_ge(L.ring_full[bank], seq)
                    ctx_load(L, i + 2)
                    if L.masked:
                        sp.wait_ge(mask_ready, i + 2)
                        mask_load(i + 2)

            w0 = (a["L0_ffn_W_in"], a["L0_ffn_W_out"])
            w1 = (a["L1_ffn_W1"], a["L1_ffn_W2"])
            load("x")
            ctx_load(L0, 0)
            mask_load(0)
            load("x0")
            load_bias_rows()
            load("la")
            load("f0")
            load("x1")
            load("f1")
            for s in range(SLOTS):
                expert_load(*w0, s, s)
            ctx_stream(L0)
            after(sp, "la.out_ps")
            ctx_load(L1, 0)
            load("x1big")
            load("la1")
            with sp.Fori(0, 8 // SLOTS - 1) as i:
                for s in range(SLOTS):
                    sp.wait_ge(y_full, i * SLOTS + (s + 1))
                    expert_load(*w0, i * SLOTS + (SLOTS + s), s)
            for s in range(SLOTS):
                sp.wait_ge(y_full, 8 - SLOTS + s + 1)
                expert_load(*w1, s, s)
            ctx_stream(L1)
            with sp.Fori(0, 16 // SLOTS - 1) as i:
                for s in range(SLOTS):
                    sp.wait_ge(y_full, i * SLOTS + (8 + s + 1))
                    expert_load(*w1, i * SLOTS + (SLOTS + s), s)
            after(sp, "f1.done")
            sp.dma_start(out.rearrange("a s d -> (a s) d"), X[:, :]).then_inc(stored, 16)
            sp.wait_ge(stored, 16)

        @block.gpsimd
        def _(pool):
            count = [0]

            def link(ins):
                count[0] += 1
                ins.then_inc(pool_step, 1)
                pool.wait_ge(pool_step, count[0])

            link(pool.memset(ident[:, :], 0.0))
            pool.affine_select(out=ident[:, :], in_=ident[:, :], compare_op=ALU.not_equal, fill=1.0, base=0,
                               pattern=[[-1, P]], channel_multiplier=1).then_inc(stage("ident"), 1)
            pool.memset(bvcol[:, :], 0.0).then_inc(stage("bvcol"), 1)
            link(pool.memset(ident16[:, :], 0.0))
            pool.affine_select(out=ident16[:, :], in_=ident16[:, :], compare_op=ALU.not_equal, fill=1.0, base=0,
                               pattern=[[-1, P]], channel_multiplier=1).then_inc(stage("ident16"), 1)
            pool.memset(ones16[:, :], 1.0).then_inc(stage("ones16"), 1)
            link(pool.memset(headmask[:, :], 1.0))
            link(pool.affine_select(out=headmask[:, :], in_=headmask[:, :], compare_op=ALU.is_ge, fill=0.0, base=0,
                                    pattern=[[-16, 8]], channel_multiplier=1))
            pool.affine_select(out=headmask[:, :], in_=headmask[:, :], compare_op=ALU.is_ge, fill=0.0, base=15,
                               pattern=[[16, 8]], channel_multiplier=-1).then_inc(stage("headmask"), 1)

            def mask_convert(b):
                pool.wait_ge(mask_in, (b + 1) * 16)
                if not (isinstance(b, int) and b == 0):
                    pool.wait_ge(L0.blkmax, b * HEADS)
                pool.tensor_tensor(pad[:, 1:2], headmask[:, 0:1], headmask[:, 1:2], ALU.add)
                pool.tensor_scalar(mask_add[:, :].rearrange("q (t p) -> q t p", p=P),
                                   mask_raw[:, :].rearrange("q (p t) -> q t p", t=TILES),
                                   0.0, MASKED, ALU.is_equal, ALU.mult).then_inc(mask_ready, 1)

            after(pool, "headmask")
            mask_convert(0)
            link(pool.memset(window[:, :], 0.0))
            link(pool.affine_select(out=window[:, :], in_=window[:, :], compare_op=ALU.is_ge, fill=-HUGE, base=0,
                                    pattern=[[-1, P]], channel_multiplier=1))
            link(pool.affine_select(out=window[:, :], in_=window[:, :], compare_op=ALU.is_ge, fill=-HUGE, base=63,
                                    pattern=[[1, P]], channel_multiplier=-1))
            link(pool.memset(latmask[:, :], 0.0))
            link(pool.affine_select(out=latmask[:, :], in_=latmask[:, :], compare_op=ALU.is_ge, fill=-HUGE, base=0,
                                    pattern=[[-2, 64]], channel_multiplier=1))
            link(pool.memset(causal[:, :], 1.0))
            link(pool.affine_select(out=causal[:, :], in_=causal[:, :], compare_op=ALU.is_ge, fill=0.0, base=0,
                                    pattern=[[1, P]], channel_multiplier=-1))
            for e in range(16):
                if e < 8:
                    link(pool.memset(rev8[:, e:e + 1], float(8 - e)))
                link(pool.memset(rev16[:, e:e + 1], float(16 - e)))
            pool.memset(rev16[:, 0:1], 16.0).then_inc(stage("consts"), 1)
            with pool.Fori(0, NBLK - 1) as i:
                mask_convert(i + 1)

        @block.scalar
        def _(act):
            count = [0]

            def link(ins):
                count[0] += 1
                ins.then_inc(act_step, 1)
                act.wait_ge(act_step, count[0])

            def ln_root(tag):
                after(act, tag + ".var")
                act.activation(sd[:, 0:1], sd[:, 1:2], ACT.Sqrt).then_inc(stage(tag + ".sd"), 1)

            def leading(L, place, dst, n, scale=1.0):
                bank, seq = place
                act.wait_ge(L.ring_full[bank], seq)
                src = ps_ring[:, bank * 512:bank * 512 + n]
                if len(dst.shape) == 3:
                    src = src.rearrange("p (h d) -> p h d", d=L.dv)
                act.activation(dst, src, ACT.Copy, scale=scale).then_inc(L.high, 1)

            def context(L, places):
                for (_, c, r), at in places:
                    leading(L, at, ctxT[:, 0, c, r * 512:(BLK if r else 512)], 384 if r else 512)

            def cross_block(L, b, more):
                first = isinstance(b, int) and b == 0

                def keys(x):
                    if x is not None and x % 2 == 0:
                        bank, seq = L.at(b, ("keys", x))
                        act.wait_ge(L.ring_full[bank], seq)
                        act.activation(kT[:, x % 4, :], ps_ring[:, bank * 512:bank * 512 + 512].bitcast(FP16)[:, 0:BLK],
                                       ACT.Copy).then_inc(L.ring_free[bank], 1)

                def exps(h):
                    n = h % 2
                    act.wait_ge(L.negmax, b * HEADS + (h + 1))
                    if h >= 2:
                        bank, seq = L.at(b, ("probs", h - 2, 1), more)
                        act.wait_ge(L.ring_full[bank], seq)
                    elif not first:
                        bank, seq = L.at(b - 1, ("probs", HEADS - 2 + h, 1))
                        act.wait_ge(L.ring_full[bank], seq)
                    src = masked_s[:, n, :] if L.masked else ps_s[:, 1024 * n:1024 * n + BLK]
                    act.activation(probs[:, n, 0:BLK], src, ACT.Exp, bias=negcur[:, h:h + 1],
                                   accum_out=rowsum[:, h:h + 1]).then_inc(L.probs, 1)

                def turned(h):
                    for r in range(2):
                        leading(L, L.at(b, ("probs", h, r), more),
                                probsT[:, h % (2 * L.together), 0, r * 512:(BLK if r else 512)], 384 if r else 512)

                for n in range(len(L.natural)):
                    leading(L, L.at(b, ("natural", n)), natural_group(L, n, 0), L.natural[n][2], 1.0 / WSCALE)
                for x in range(L.first_keys):
                    keys(x)
                if not first:
                    act.wait_ge(L.sums, b)
                for h in range(HEADS):
                    if h >= 1:
                        exps(h - 1)
                    keys(L.keys_after(h))
                    if h >= 2:
                        turned(h - 2)
                exps(HEADS - 1)
                act.wait_ge(L.shift, b + 1)
                act.activation(by_row(L), shift[:, :].unsqueeze(2).broadcast_to([P, HEADS, L.width]),
                               ACT.Exp).then_inc(L.corr, 1)
                turned(HEADS - 2)
                if more:
                    context(L, [(g, L.at(b, g)) for g in L.context])
                turned(HEADS - 1)

            def cross(L):
                context(L, [(g, L.at_first(g)) for g in L.context])
                cross_block(L, 0, True)
                with act.Fori(0, NBLK - 2) as i:
                    cross_block(L, i + 1, True)
                cross_block(L, NBLK - 1, False)

            def softmax_exps(tag, src):
                after(act, tag + ".shifted")
                act.activation(src, src, ACT.Exp).then_inc(stage(tag + ".exps"), 1)

            def experts(E, func, bias_cols, base):
                def round_of_experts(i):
                    for j in range(SLOTS):
                        for half in range(2):
                            act.wait_ge(hid_full, i * (2 * SLOTS) + ((base + j) * 2 + half + 1))
                            bank = (j % 2) * 2 + half
                            for t in range(4):
                                m = half * 4 + t
                                ins = act.activation(
                                    hT[:, j % 2, m, :], ps_s[:, bank * 512 + t * P:bank * 512 + (t + 1) * P], func,
                                    bias=bias_cols[:, bass.ds(i * (SLOTS * HT) + (j * HT + m), 1)])
                            ins.then_inc(hid_ready, 1)

                expert_rounds(act, E, round_of_experts)

            ln_root("x0")
            cross(L0)
            ln_root("la")
            softmax_exps("la.local", wide_a)
            softmax_exps("la.lat", lat_s)
            after(act, "la.gates")
            act.activation(gates[:, :], gates[:, :], ACT.Exp, scale=-1.0).then_inc(stage("la.gexp"), 1)
            ln_root("f0")
            after(act, "f0.top")
            act.activation(gate[:, 6, 0:8], gate[:, 5, 0:8], ACT.Exp).then_inc(stage("f0.exp"), 1)
            experts(8, ACT.Gelu, bin_cols, 0)
            ln_root("x1")
            ln_root("xm")
            softmax_exps("x1.self", wide_a)
            cross(L1)
            ln_root("l1")
            after(act, "l1.abs")
            act.activation(sp_u, sp_a, ACT.Exp, scale=-1.0).then_inc(stage("l1.u"), 1)
            after(act, "l1.w")
            act.activation(sp_a, sp_w, ACT.Ln).then_inc(stage("l1.ln"), 1)
            ln_root("f1")
            after(act, "f1.top")
            act.activation(gate[:, 6, 0:16], gate[:, 5, 0:16], ACT.Exp).then_inc(stage("f1.exp"), 1)
            experts(16, ACT.Relu, b1_cols, 8)

        @block.vector
        def _(dve):
            count = [0]

            def link(ins):
                count[0] += 1
                ins.then_inc(dve_step, 1)
                dve.wait_ge(dve_step, count[0])

            def layernorm(tag, src, dst, eps=1e-5):
                link(dve.bn_stats(stats[:, :], src))
                link(dve.bn_aggr(meanvar[:, :], stats[:, :]))
                dve.tensor_scalar(sd[:, 1:2], meanvar[:, 1:2], eps, None, ALU.add).then_inc(stage(tag + ".var"), 1)
                after(dve, tag + ".sd")
                link(dve.reciprocal(sd[:, 1:2], sd[:, 0:1]))
                dve.tensor_scalar(dst, src, meanvar[:, 0:1], sd[:, 1:2], ALU.subtract,
                                  ALU.mult).then_inc(stage(tag + ".xn"), 1)

            def take(tag, dst, src):
                after(dve, tag)
                dve.tensor_copy(dst, src).then_inc(stage(tag + ".sb"), 1)

            def trailing(L, place, high, dst, lead, n, scale=1.0):
                bank, _ = place
                dve.wait_ge(L.high, high)
                src = ps_ring[:, bank * 512:bank * 512 + n]
                if len(dst.shape) == 3:
                    src = src.rearrange("p (h d) -> p h d", d=L.dv)
                dve.scalar_tensor_tensor(out=dst, in0=src, scalar=scale, in1=lead, op0=ALU.mult,
                                         op1=ALU.subtract).then_inc(L.ring_free[bank], 1)

            def context(L, places):
                for (_, c, r), at, high in places:
                    cut = slice(r * 512, BLK if r else 512)
                    trailing(L, at, high, ctxT[:, 1, c, cut], ctxT[:, 0, c, cut], 384 if r else 512)

            def cross_block(L, b, more):
                first = isinstance(b, int) and b == 0
                used = HEADS // L.together * P

                def keys(x):
                    if x is not None and x % 2 == 1:
                        bank, seq = L.at(b, ("keys", x))
                        dve.wait_ge(L.ring_full[bank], seq)
                        dve.tensor_copy(kT[:, x % 4, :], ps_ring[:, bank * 512:bank * 512 + 512].bitcast(FP16)[:, 0:BLK])\
                           .then_inc(L.ring_free[bank], 1)

                def maximum(h):
                    n = h % 2
                    dve.wait_ge(L.scores, b * HEADS + (h + 1))
                    s = ps_s[:, 1024 * n:1024 * n + BLK]
                    if L.masked:
                        if h >= 2 or not first:
                            dve.wait_ge(L.probs, b * HEADS + (h - 1))
                        if h == 0:
                            dve.wait_ge(mask_ready, b + 1)
                        dve.memset(pad[:, 0:1], 0.0)
                        dve.tensor_tensor_reduce(masked_s[:, n, :], s, mask_add[:, :], 1.0, -HUGE, ALU.add, ALU.max,
                                                 blkmax[:, h:h + 1]).then_inc(L.blkmax, 1)
                    else:
                        dve.tensor_reduce(blkmax[:, h:h + 1], s, AX.X, ALU.max).then_inc(L.blkmax, 1)
                    dve.wait_ge(L.blkmax, b * HEADS + (h + 1))
                    dve.scalar_tensor_tensor(out=negcur[:, h:h + 1], in0=blkmax[:, h:h + 1], scalar=-1.0,
                                             in1=negprev[:, h:h + 1], op0=ALU.mult,
                                             op1=ALU.min).then_inc(L.negmax, 1)

                def turned(h):
                    slot = h % (2 * L.together)
                    for r in range(2):
                        cut = slice(r * 512, BLK if r else 512)
                        g = ("probs", h, r)
                        trailing(L, L.at(b, g, more), L.high_at(b, g, more), probsT[:, slot, 1, cut],
                                 probsT[:, slot, 0, cut], 384 if r else 512)

                for n in range(len(L.natural)):
                    g = ("natural", n)
                    trailing(L, L.at(b, g), L.high_at(b, g), natural_group(L, n, 1), natural_group(L, n, 0),
                             L.natural[n][2], 1.0 / WSCALE)
                for x in range(L.first_keys):
                    keys(x)
                for h in range(HEADS):
                    maximum(h)
                    keys(L.keys_after(h))
                    if h >= 2:
                        turned(h - 2)
                dve.wait_ge(L.negmax, b * HEADS + HEADS)
                dve.tensor_tensor(shift[:, :], negcur[:, :], negprev[:, :], ALU.subtract).then_inc(L.shift, 1)
                turned(HEADS - 2)
                if more:
                    context(L, [(g, L.at(b, g), L.high_at(b, g)) for g in L.context])
                dve.wait_ge(L.corr, b + 1)
                dve.wait_ge(L.probs, b * HEADS + HEADS)
                dve.tensor_copy(negprev[:, :], negcur[:, :])
                dve.tensor_tensor(den[:, :], den[:, :], by_row(L)[:, :, 0], ALU.mult).then_inc(L.scaled, 1)
                turned(HEADS - 1)
                dve.wait_ge(L.scaled, b * 2 + 1)
                dve.tensor_tensor(den[:, :], den[:, :], rowsum[:, :], ALU.add).then_inc(L.sums, 1)
                dve.wait_ge(L.corr_rows, b + 1)
                dve.tensor_tensor(O[:, 0:used], O[:, 0:used], ps_s[:, 0:used], ALU.mult).then_inc(L.scaled, 1)
                dve.wait_ge(L.scaled, b * 2 + 2)
                dve.wait_ge(L.sums, b + 1)
                dve.wait_ge(L.pv, b + 1)
                dve.tensor_tensor(O[:, 0:used], O[:, 0:used], ps_o[:, 0:used], ALU.add).then_inc(L.acc, 1)
                dve.wait_ge(L.acc, b + 1)

            def cross(L):
                context(L, [(g, L.at_first(g), i + 1) for i, g in enumerate(L.context)])
                cross_block(L, 0, True)
                with dve.Fori(0, NBLK - 2) as i:
                    cross_block(L, i + 1, True)
                cross_block(L, NBLK - 1, False)

            def split_weights(parts):
                for src, lo, n in parts:
                    link(dve.tensor_scalar(w16[:, :, 0, lo:lo + n], src, WSCALE, None, ALU.mult))
                    ins = dve.scalar_tensor_tensor(out=w16[:, :, 1, lo:lo + n], in0=src, scalar=WSCALE,
                                                   in1=w16[:, :, 0, lo:lo + n], op0=ALU.mult, op1=ALU.subtract)
                return ins

            def divide(L, tag):
                used = HEADS // L.together * P
                link(dve.reciprocal(den[:, :], den[:, :]))
                dve.tensor_copy(by_row(L), den[:, :].unsqueeze(2).broadcast_to([P, HEADS, L.width]))\
                   .then_inc(stage(tag + ".rden"), 1)
                after(dve, tag + ".rden_rows")
                return dve.tensor_tensor(O[:, 0:used], O[:, 0:used], ps_s[:, 0:used], ALU.mult)

            def head_queries(src, e, dst):
                return dve.tensor_tensor(dst, src.unsqueeze(1).broadcast_to([P, 8, P]),
                                         headmask[:, :].unsqueeze(2).broadcast_to([P, 8, P]), ALU.mult)

            def softmax_head(tag, s, heads, keys, negmax, sums):
                s3 = s.rearrange("p (h k) -> p h k", h=heads)
                link(dve.tensor_reduce(negmax, s3, AX.X, ALU.max, negate=True))
                dve.tensor_tensor(s3, s3, negmax.unsqueeze(2).broadcast_to([P, heads, keys]),
                                  ALU.add).then_inc(stage(tag + ".shifted"), 1)
                after(dve, tag + ".exps")
                link(dve.tensor_reduce(sums, s3, AX.X, ALU.add))

            def route(tag, E, logits, rev, renormalise):
                g = [gate[:, i, 0:E] for i in range(8)]
                m = gatecol
                link(dve.tensor_reduce(m[:, 0:1], logits, AX.X, ALU.max))
                dve.tensor_scalar(g[5], logits, m[:, 0:1], None, ALU.subtract).then_inc(stage(tag + ".top"), 1)
                after(dve, tag + ".exp")
                if renormalise:
                    score = logits
                else:
                    link(dve.tensor_reduce(m[:, 1:2], g[6], AX.X, ALU.add))
                    link(dve.reciprocal(m[:, 2:3], m[:, 1:2]))
                    link(dve.tensor_scalar(g[6], g[6], m[:, 2:3], None, ALU.mult))
                    score = g[6]
                    link(dve.tensor_reduce(m[:, 0:1], score, AX.X, ALU.max))
                link(dve.scalar_tensor_tensor(out=g[0], in0=score, scalar=m[:, 0:1], in1=rev[:, :],
                                              op0=ALU.is_equal, op1=ALU.mult))
                link(dve.tensor_reduce(m[:, 3:4], g[0], AX.X, ALU.max))
                link(dve.tensor_scalar(g[1], g[0], m[:, 3:4], None, ALU.is_equal))
                link(dve.scalar_tensor_tensor(out=g[2], in0=g[1], scalar=-HUGE, in1=score,
                                              op0=ALU.mult, op1=ALU.add))
                link(dve.tensor_reduce(m[:, 4:5], g[2], AX.X, ALU.max))
                link(dve.scalar_tensor_tensor(out=g[0], in0=g[2], scalar=m[:, 4:5], in1=rev[:, :],
                                              op0=ALU.is_equal, op1=ALU.mult))
                link(dve.tensor_reduce(m[:, 5:6], g[0], AX.X, ALU.max))
                link(dve.tensor_scalar(g[3], g[0], m[:, 5:6], None, ALU.is_equal))
                link(dve.tensor_tensor(g[1], g[1], g[3], ALU.add))
                if renormalise:
                    link(dve.tensor_tensor(g[2], g[1], g[6], ALU.mult))
                    link(dve.tensor_reduce(m[:, 1:2], g[2], AX.X, ALU.add))
                    link(dve.reciprocal(m[:, 2:3], m[:, 1:2]))
                    dve.tensor_scalar(comb[:, 0:E], g[2], m[:, 2:3], None, ALU.mult).then_inc(stage(tag + ".comb"), 1)
                else:
                    dve.tensor_tensor(comb[:, 0:E], g[1], g[6], ALU.mult).then_inc(stage(tag + ".comb"), 1)

            def experts(tag, E, base):
                take(tag + ".combT", combT[0:E, :], ps_o[0:E, 0:P])
                after(dve, tag + ".bias_ps")
                dve.tensor_tensor(X[:, :], X[:, :], ps_o[:, 512:512 + D], ALU.add).then_inc(stage(tag + ".bias_used"), 1)
                after(dve, tag + ".bias_used")

                def round_of_experts(i):
                    for j in range(SLOTS):
                        e = i * SLOTS + (base + j)
                        dve.wait_ge(y_full, e + 1)
                        dve.scalar_tensor_tensor(out=X[:, :], in0=ps_o[:, (j % 2) * 512:(j % 2) * 512 + D],
                                                 scalar=comb[:, bass.ds(i * SLOTS + j, 1)], in1=X[:, :],
                                                 op0=ALU.mult, op1=ALU.add).then_inc(y_added, 1)
                        dve.wait_ge(y_added, e + 1)

                expert_rounds(dve, E, round_of_experts)

            def add_projection(tag, src, bias_row=None):
                after(dve, tag)
                if bias_row is not None:
                    link(dve.tensor_tensor(X[:, :], X[:, :], rows[:, bias_row, :], ALU.add))
                link(dve.tensor_tensor(X[:, :], X[:, :], src, ALU.add))

            arrived(dve, "x")
            layernorm("x0", X[:, :], xn[:, :])
            take("x0.xT", xT[:, :, :], ps_ring[:, 0:D].rearrange("p (c n) -> p c n", c=DC))
            arrived(dve, "x0")
            after(dve, "x0.q")
            split_weights([(wk0[:, :, :], 0, D), (wv0[:, :, :], D, D)]).then_inc(stage("x0.w16"), 1)
            after(dve, "ident")
            link(dve.tensor_scalar(bk16[:, :], bkf[:, 0:D], WSCALE, None, ALU.mult))
            link(dve.scalar_tensor_tensor(out=bkf[:, D:2 * D], in0=bkf[:, 0:D], scalar=WSCALE, in1=bk16[:, :],
                                          op0=ALU.mult, op1=ALU.subtract))
            link(dve.tensor_scalar(bkf[:, 2 * D:3 * D], bk16[:, :], ident[0:2, 0:1], None, ALU.mult))
            dve.scalar_tensor_tensor(out=bk16[:, :], in0=bkf[:, D:2 * D], scalar=ident[0:2, 1:2],
                                     in1=bkf[:, 2 * D:3 * D], op0=ALU.mult, op1=ALU.add).then_inc(stage("x0.bk"), 1)
            link(dve.tensor_tensor(qn[:, 0:D], ps_o[:, 0:D], rows[:, BQ0, :], ALU.add))
            link(dve.tensor_scalar(qn[:, 0:D], qn[:, 0:D], 0.25, None, ALU.mult))
            link(dve.tensor_copy(qhi[:, 0:D], qn[:, 0:D]))
            link(dve.tensor_tensor(qlo[:, 0:D], qn[:, 0:D], qhi[:, 0:D], ALU.subtract))
            link(dve.memset(qx[:, 0:2048], 0.0))
            view = qx[:, 0:2048].rearrange("p (pair s copy s2 part d) -> p pair s copy s2 part d",
                                           pair=8, s=2, copy=2, s2=2, part=2)
            for i, part_of_q in enumerate((qhi, qlo)):
                q4 = part_of_q[:, 0:D].rearrange("p (pair s d) -> p pair s d", pair=8, s=2)
                for s_ in range(2):
                    for part in range(2):
                        ins = dve.tensor_copy(view[:, :, s_, i, s_, part, :], q4[:, :, s_, :])
            link(ins)
            dve.memset(O[:, :], 0.0).then_inc(stage("x0.qx"), 1)
            after(dve, "x0.qxT")
            dve.tensor_copy(q16[:, :, 0, :], ps_s16[:, 0:2048].rearrange("p (h q) -> p h q", h=HEADS))\
               .then_inc(stage("x0.q16"), 1)
            link(dve.memset(den[:, :], 0.0))
            link(dve.memset(negprev[:, :], HUGE))
            cross(L0)
            link(divide(L0, "x0"))
            arrived(dve, "x0b")
            after(dve, "bvcol")
            dve.tensor_tensor(O[:, 0:512].rearrange("p (g q) -> p g q", g=4), O[:, 0:512].rearrange("p (g q) -> p g q", g=4),
                              bvcol[:, :].unsqueeze(2).broadcast_to([P, 4, P]), ALU.add).then_inc(stage("x0.done"), 1)
            add_projection("x0.out", ps_o[:, 0:D], BO0)

            layernorm("la", X[:, :], xn[:, :])
            after(dve, "la.xT")
            link(dve.tensor_copy(xT[:, :, :], ps_ring[:, 0:D].rearrange("p (c n) -> p c n", c=DC)))
            pair = xT[:, :, :].rearrange("p c (n two) -> p c n two", two=2)
            link(dve.tensor_tensor(xpool, pair[:, :, :, 0], pair[:, :, :, 1], ALU.add))
            dve.tensor_scalar(xpool, xpool, 0.5, None, ALU.mult).then_inc(stage("la.xT.sb"), 1)
            after(dve, "la.proj")
            link(dve.tensor_scalar(qT[:, 0:2, :], ps_s[:, 0:D].rearrange("p (c n) -> p c n", c=2), 0.25, None, ALU.mult))
            link(dve.tensor_copy(qT[:, 2:4, :], ps_s[:, D:2 * D].rearrange("p (c n) -> p c n", c=2)))
            link(dve.tensor_copy(v_nat, ps_s[:, 512:512 + D]))
            link(dve.tensor_copy(q_nat, ps_s[:, 512 + D:1024]))
            link(dve.tensor_scalar(qT[:, 4, :], ps_s[:, 1024:1024 + P], 0.25, None, ALU.mult))
            link(dve.tensor_copy(qT[:, 5, 0:64], ps_s[:, 1024 + P:1024 + P + 64]))
            link(dve.tensor_copy(gv_nat, ps_s[0:64, 1536:1536 + P]))
            after(dve, "headmask")
            link(head_queries(qT[:, 2, :], 0, kz[:, 0, :, :]))
            link(head_queries(qT[:, 3, :], 1, kz[:, 1, :, :]))
            dve.tensor_tensor(gkz, qT[:, 5, 0:64].unsqueeze(1).broadcast_to([P, 8, 64]),
                              headmask[:, :].unsqueeze(2).broadcast_to([P, 8, 64]), ALU.mult).then_inc(stage("la.kz"), 1)
            after(dve, "consts")
            after(dve, "la.scores")
            link(dve.tensor_tensor(wide_a.rearrange("p (h k) -> p h k", h=HEADS),
                                   ps_s[:, :].rearrange("p (h k) -> p h k", h=HEADS),
                                   window[:, :].unsqueeze(1).broadcast_to([P, HEADS, P]), ALU.add))
            link(dve.tensor_tensor(lat_s.rearrange("p (h k) -> p h k", h=8),
                                   ps_ring[:, 0:512].rearrange("p (h k) -> p h k", h=8),
                                   latmask[:, :].unsqueeze(1).broadcast_to([P, 8, 64]), ALU.add))
            softmax_head("la.local", wide_a, HEADS, P, negprev[:, :], den[:, :])
            softmax_head("la.lat", lat_s, 8, 64, negcur[:, 0:8], rowsum[:, 0:8])
            arrived(dve, "la")
            for i, r in ((0, GL), (1, GR)):
                link(dve.tensor_tensor(xn[:, :], q_nat, rows[:, r, :], ALU.mult))
                link(dve.tensor_reduce(gates[:, 16 * i:16 * i + 16], xn[:, :].rearrange("p (h d) -> p h d", h=HEADS),
                                       AX.X, ALU.add))
            dve.tensor_scalar(gates[:, :], gates[:, :], 1.0, None, ALU.mult).then_inc(stage("la.gates"), 1)
            after(dve, "la.gexp")
            link(dve.tensor_scalar(gates[:, :], gates[:, :], 1.0, None, ALU.add))
            link(dve.reciprocal(gates[:, :], gates[:, :]))
            link(dve.reciprocal(den[:, :], den[:, :]))
            link(dve.reciprocal(rowsum[:, 0:8], rowsum[:, 0:8]))
            link(dve.tensor_tensor(gates[:, 0:16], gates[:, 0:16], den[:, :], ALU.mult))
            take("la.turned", wide_b, ps_s[:, :])
            after(dve, "la.pv")
            link(dve.tensor_tensor(attn.rearrange("p (h d) -> p h d", h=HEADS),
                                   ps_o[:, 0:D].rearrange("p (h d) -> p h d", h=HEADS),
                                   gates[:, 0:16].unsqueeze(2).broadcast_to([P, HEADS, 16]), ALU.mult))
            take("la.lturned", wide_a[0:64, 0:1024], ps_s[0:64, 0:1024])
            after(dve, "la.lpv")
            dve.tensor_tensor(rem.rearrange("p (h d) -> p h d", h=8),
                              ps_o[:, 512:512 + P].rearrange("p (h d) -> p h d", h=8),
                              rowsum[:, 0:8].unsqueeze(2).broadcast_to([P, 8, 16]), ALU.mult).then_inc(stage("la.rem"), 1)
            take("la.remT", qT[:, 0, :], ps_ring[:, 0:P])
            after(dve, "la.rproj")
            link(dve.tensor_tensor(xn[:, :].rearrange("p (h d) -> p h d", h=HEADS),
                                   ps_ring[:, 512:512 + D].rearrange("p (h d) -> p h d", h=HEADS),
                                   gates[:, 16:32].unsqueeze(2).broadcast_to([P, HEADS, 16]), ALU.mult))
            dve.tensor_tensor(xn[:, :], xn[:, :], attn, ALU.add).then_inc(stage("la.attn"), 1)
            take("la.attnT", xT[:, :, :], ps_ring[:, 0:D].rearrange("p (c n) -> p c n", c=DC))
            add_projection("la.out_ps", ps_o[:, 0:D])

            layernorm("f0", X[:, :], xn[:, :])
            take("f0.xT", xT[:, :, :], ps_ring[:, 0:D].rearrange("p (c n) -> p c n", c=DC))
            take("f0.bias", bin_cols[:, :], ps_ring[:, 512:512 + 8 * HT])
            after(dve, "f0.logits")
            link(dve.tensor_copy(gate[:, 4, 0:8], ps_o[:, 0:8]))
            route("f0", 8, gate[:, 4, 0:8], rev8, True)
            experts("f0", 8, 0)

            layernorm("x1", X[:, :], xn[:, :])
            after(dve, "x1.xn")
            layernorm("xm", xn[:, :], xm[:, :])
            arrived(dve, "x1")
            after(dve, "xm.xn")
            link(dve.tensor_tensor(xm[:, :], xm[:, :], rows[:, LNG, :], ALU.mult))
            dve.tensor_tensor(xm[:, :], xm[:, :], rows[:, LNB, :], ALU.add).then_inc(stage("xm.affine"), 1)
            take("xm.xT", xT[:, :, :], ps_ring[:, 0:D].rearrange("p (c n) -> p c n", c=DC))
            arrived(dve, "x1big")
            split_weights([(wm1, 0, 1024)]).then_inc(stage("x1.w16"), 1)
            after(dve, "x1.proj")
            link(dve.tensor_scalar(qT[:, :, :], ps_s[:, 0:1024].rearrange("p (t n) -> p t n", t=8), 0.125, None, ALU.mult))
            link(dve.tensor_copy(k_self, ps_s[:, 1024:2048].rearrange("p (t n) -> p t n", t=8)))
            link(dve.tensor_copy(v_self[:, :], ps_o[:, :]))
            dve.tensor_scalar(qn, ps_ring[:, :], 0.125, None, ALU.mult).then_inc(stage("x1.qk"), 1)
            after(dve, "x1.qk")
            link(dve.tensor_copy(qhi, qn))
            link(dve.tensor_tensor(qlo, qn, qhi, ALU.subtract))
            view = qx.rearrange("p (h turn half d) -> p h turn half d", h=HEADS, turn=2, half=2)
            for i, part_of_q in enumerate((qhi, qlo)):
                for half in range(2):
                    ins = dve.tensor_copy(view[:, :, i, half, :], part_of_q.rearrange("p (h d) -> p h d", h=HEADS))
            ins.then_inc(stage("x1.qx"), 1)
            after(dve, "x1.self_scores")
            link(dve.tensor_copy(wide_a.rearrange("p (t c k) -> p c t k", t=8, c=2),
                                 ps_s[:, :].rearrange("p (c t k) -> p c t k", t=8, c=2)))
            softmax_head("x1.self", wide_a, HEADS, P, negprev[:, :], den[:, :])
            take("x1.turned", wide_b, ps_s[:, :])
            after(dve, "x1.self_pv")
            dve.tensor_copy(O[:, :], ps_o[:, :]).then_inc(stage("x1.start"), 1)
            after(dve, "x1.qxT")
            dve.tensor_copy(q16[:, :, :, :].rearrange("p h t q -> p (h t q)"), ps_s16[:, :]).then_inc(stage("x1.q16"), 1)
            after(dve, "x1.start")
            cross(L1)
            divide(L1, "x1").then_inc(stage("x1.done"), 1)
            add_projection("x1.out", ps_o[:, 0:D], BO1)

            layernorm("l1", X[:, :], xn[:, :])
            take("l1.wT", wide_b, ps_s[:, :])
            take("l1.xT", xT[:, :, :], ps_ring[:, 0:D].rearrange("p (c n) -> p c n", c=DC))
            after(dve, "l1.proj")
            link(dve.tensor_copy(sp_z, ps_s[:, 0:512]))
            link(dve.memset(v_ext, 1.0))
            link(dve.tensor_copy(v_ext[:, :, 0:16], ps_s[:, 512:512 + D].rearrange("p (h d) -> p h d", h=HEADS)))
            link(dve.tensor_scalar(sp_w, sp_z, -1.0, None, ALU.mult))
            dve.tensor_tensor(sp_a, sp_z, sp_w, ALU.max).then_inc(stage("l1.abs"), 1)
            after(dve, "l1.u")
            dve.tensor_scalar(sp_w, sp_u, 1.0, None, ALU.add).then_inc(stage("l1.w"), 1)
            after(dve, "l1.w")
            link(dve.scalar_tensor_tensor(out=sp_u, in0=sp_w, scalar=-1.0, in1=sp_u, op0=ALU.add, op1=ALU.subtract))
            after(dve, "l1.ln")
            link(dve.reciprocal(sp_w, sp_w))
            link(dve.tensor_tensor(sp_u, sp_u, sp_w, ALU.mult))
            link(dve.tensor_tensor(sp_a, sp_a, sp_u, ALU.subtract))
            link(dve.tensor_scalar(sp_z, sp_z, 0.0, None, ALU.max))
            link(dve.tensor_tensor(sp_z, sp_z, sp_a, ALU.add))
            link(dve.tensor_scalar(sp_z, sp_z, 1e-6, None, ALU.add))
            link(head_queries(sp_z[:, 0:P], 0, kz[:, 0, :, :]))
            head_queries(sp_z[:, P:2 * P], 1, kz[:, 1, :, :]).then_inc(stage("l1.qz"), 1)
            after(dve, "l1.scores")
            dve.tensor_tensor(wide_a.rearrange("p (h k) -> p h k", h=HEADS),
                              ps_s[:, :].rearrange("p (h k) -> p h k", h=HEADS),
                              causal[:, :].unsqueeze(1).broadcast_to([P, HEADS, P]), ALU.mult).then_inc(stage("l1.causal"), 1)
            after(dve, "l1.pv")
            pv = ps_o[:, 0:HEADS * 17].rearrange("p (h d) -> p h d", h=HEADS)
            link(dve.tensor_scalar(den[:, :], pv[:, :, 16], 1e-6, None, ALU.add))
            link(dve.reciprocal(den[:, :], den[:, :]))
            dve.tensor_tensor(xn[:, :].rearrange("p (h d) -> p h d", h=HEADS), pv[:, :, 0:16],
                              den[:, :].unsqueeze(2).broadcast_to([P, HEADS, 16]), ALU.mult).then_inc(stage("l1.attn"), 1)
            take("l1.attnT", xT[:, :, :], ps_ring[:, 0:D].rearrange("p (c n) -> p c n", c=DC))
            add_projection("l1.out", ps_o[:, 512:512 + D])

            layernorm("f1", X[:, :], xn[:, :])
            take("f1.xT", xT[:, :, :], ps_ring[:, 0:D].rearrange("p (c n) -> p c n", c=DC))
            take("f1.bias", b1_cols[:, :], ps_ring[:, 512:512 + P])
            after(dve, "f1.logits")
            arrived(dve, "f1")
            link(dve.tensor_tensor(gate[:, 4, 0:16], ps_o[:, 0:16], br1[:, :], ALU.add))
            route("f1", 16, gate[:, 4, 0:16], rev16, False)
            experts("f1", 16, 8)
            dve.tensor_copy(gate[:, 0, 0:1], X[:, 0:1]).then_inc(stage("f1.done"), 1)

        @block.tensor
        def _(pe):
            def turn(src, dst, n):
                for t in range(n):
                    ins = pe.transpose(dst[:, t * P:(t + 1) * P], src[:, t * P:(t + 1) * P], ident[:, :])
                return ins

            def project(dst, lhs, rhs, chunks=DC):
                for c in range(chunks):
                    ins = pe.matmul(dst, lhs(c), rhs(c), start=c == 0, stop=c == chunks - 1)
                return ins

            def turn_norm(tag, ready, src):
                after(pe, ready)
                turn(src, ps_ring[:, 0:D], DC).then_inc(stage(tag), 1)

            RANGES = ((0, SPLIT), (SPLIT, TILES))

            def claim(L, place, fresh=False):
                bank, seq = place
                if not fresh:
                    pe.wait_ge(L.ring_free[bank], seq - 1)
                return bank * 512

            def filled(L, place, ins):
                ins.then_inc(L.ring_full[place[0]], 1)

            def out_of_ring(L, place):
                pe.wait_ge(L.ring_free[place[0]], place[1])

            def context(L, places, arrivals, first=False):
                pe.wait_ge(L.ctx_in, arrivals * 16)
                for i, ((_, c, r), at) in enumerate(places):
                    base = claim(L, at, first and i < 2)
                    t0, t1 = RANGES[r]
                    for t in range(t0, t1):
                        col = base + (t - t0) * P
                        ins = pe.transpose(ps_ring[:, col:col + P], ctx_nat[:, t, c * P:(c + 1) * P], ident[:, :])
                    filled(L, at, ins)

            def cross_block(L, b, more):
                first = isinstance(b, int) and b == 0

                def project_keys(n):
                    at = L.at(b, ("natural", n))
                    base = claim(L, at)
                    t, f, w = L.natural[n]
                    dst = ps_ring[:, base:base + w]
                    passes = [(c, x, y) for c in range(DC) for x, y in ((0, 0), (0, 1), (1, 0))]
                    for i, (c, x, y) in enumerate(passes):
                        bias = L is L0 and f == 0
                        ins = pe.matmul(dst, ctxT[:, x, c, t * P:(t + 1) * P], w16[:, c, y, f:f + w], start=i == 0,
                                        stop=i == len(passes) - 1 and not bias)
                    if bias:
                        ins = pe.matmul(dst[:, 0:D], ones16[:, :], bk16[:, :], start=False, stop=True)
                    filled(L, at, ins)

                def turn_keys(x):
                    if x is None:
                        return
                    at = L.at(b, ("keys", x))
                    base = claim(L, at)
                    if x == 0:
                        for n in (-2, -1):
                            out_of_ring(L, L.at(b, ("natural", len(L.natural) + n)))
                    dst = ps_ring[:, base:base + 512].bitcast(FP16)
                    if L is L0:
                        pe.transpose(dst[:, 0:P], vals[:, x * 64:x * 64 + P], ident16[:, :])
                    for t in range(TILES):
                        o = t * 2 * L.cols + x * (64 if L is L0 else P)
                        if L is L0:
                            for copy in range(2):
                                ins = pe.transpose(dst[64 * copy:64 * copy + 64, t * P:(t + 1) * P], vals[:, o:o + 64],
                                                   ident16[:, :])
                        else:
                            ins = pe.transpose(dst[:, t * P:(t + 1) * P], vals[:, o:o + P], ident16[:, :])
                    filled(L, at, ins)

                def scores(h):
                    n = h % 2
                    x = h // L.heads_per_turn
                    out_of_ring(L, L.at(b, ("keys", x)))
                    if h >= 2 or not first:
                        pe.wait_ge(L.blkmax if L.masked else L.probs, b * HEADS + (h - 1))
                    if h == 0 and not first:
                        pe.wait_ge(L.acc, b)
                    passes = 1 if L is L0 else 2
                    for t0, t1 in RANGES:
                        for i in range(passes):
                            ins = pe.matmul(ps_s[:, 1024 * n + t0 * P:1024 * n + t1 * P], q16[:, h, i, :],
                                            kT[:, x % 4, t0 * P:t1 * P], start=i == 0, stop=i == passes - 1)
                    ins.then_inc(L.scores, 1)

                def turn_probs(h):
                    pe.wait_ge(L.probs, b * HEADS + (h + 1))
                    for r, (t0, t1) in enumerate(RANGES):
                        at = L.at(b, ("probs", h, r), more)
                        base = claim(L, at)
                        filled(L, at, turn(probs[:, h % 2, t0 * P:t1 * P], ps_ring[:, base:base + 512], t1 - t0))

                def weighted(g):
                    heads = range(g * L.together, (g + 1) * L.together)
                    for r in range(2):
                        out_of_ring(L, L.at(b, ("probs", heads[-1], r), more))
                    if g == 0 and not first:
                        pe.wait_ge(L.acc, b)
                    both = slice(0, 2)
                    passes = ((both, 0), (both, 1)) if L is L0 else ((slice(0, 1), 0), (slice(0, 1), 1), (slice(1, 2), 0))
                    for t in range(TILES):
                        for i, (v, p) in enumerate(passes):
                            for k, h in enumerate(heads):
                                ins = pe.matmul(ps_o[k * L.width:(k + 1) * L.width, g * P:(g + 1) * P],
                                                stationary(L, t, h, v),
                                                probsT[:, h % (2 * L.together), p, t * P:(t + 1) * P],
                                                start=t == 0 and i == 0,
                                                stop=t == TILES - 1 and i == len(passes) - 1)
                    if g == HEADS // L.together - 1:
                        ins.then_inc(L.pv, 1)

                for g in L.context[-2:]:
                    out_of_ring(L, L.at_first(g) if first else L.at(b - 1, g))
                for n in range(len(L.natural)):
                    project_keys(n)
                for x in range(L.first_keys):
                    turn_keys(x)
                for h in range(HEADS):
                    scores(h)
                    turn_keys(L.keys_after(h))
                    if h >= 2:
                        turn_probs(h - 2)
                    if h >= 3 and (h - 2) % L.together == 0:
                        weighted((h - 2) // L.together - 1)
                        done = (h - 2) // L.together
                turn_probs(HEADS - 2)
                if more:
                    context(L, [(g, L.at(b, g)) for g in L.context], b + 2)
                turn_probs(HEADS - 1)
                pe.wait_ge(L.corr, b + 1)
                per_row(L).then_inc(L.corr_rows, 1)
                for g in range(done, HEADS // L.together):
                    weighted(g)

            def per_row(L):
                for g in range(HEADS // L.together):
                    ins = pe.matmul(ps_s[:, g * P:(g + 1) * P], factors[:, g * P:(g + 1) * P], ident[:, :],
                                    start=True, stop=True)
                return ins

            def cross(L):
                context(L, [(g, L.at_first(g)) for g in L.context], 1, True)
                cross_block(L, 0, True)
                with pe.Fori(0, NBLK - 2) as i:
                    cross_block(L, i + 1, True)
                cross_block(L, NBLK - 1, False)

            def experts(tag, E, base):
                after(pe, tag + ".comb")
                pe.transpose(ps_o[0:E, 0:P], comb[:, 0:E], ident[:, :]).then_inc(stage(tag + ".combT"), 1)
                after(pe, tag + ".combT.sb")
                b_out = bout0 if base == 0 else b2_1
                pe.matmul(ps_o[:, 512:512 + D], combT[0:E, :], b_out[0:E, :], start=True,
                          stop=True).then_inc(stage(tag + ".bias_ps"), 1)
                after(pe, tag + ".bias.sb")
                after(pe, tag + ".bias_used")

                def round_of_experts(i):
                    for j in range(SLOTS):
                        e = i * SLOTS + (base + j)
                        fresh = isinstance(e, int) and e < 2
                        pe.wait_ge(expert_in[j], (i + (base // SLOTS + 1)) * 32)
                        for half in range(2):
                            if not fresh:
                                pe.wait_ge(hid_ready, e * 2 + (half - 3))
                            for t in range(4):
                                m = half * 4 + t
                                col = ((j % 2) * 2 + half) * 512 + t * P
                                ins = project(ps_s[:, col:col + P], lambda c: win[:, j, c, m * P:(m + 1) * P],
                                              lambda c: xT[:, c, :])
                            ins.then_inc(hid_full, 1)
                        if not fresh:
                            pe.wait_ge(y_added, e - 1)
                        for half in range(2):
                            pe.wait_ge(hid_ready, e * 2 + (half + 1))
                            for t in range(4):
                                m = half * 4 + t
                                ins = pe.matmul(ps_o[:, (j % 2) * 512:(j % 2) * 512 + D], hT[:, j % 2, m, :],
                                                wout[:, j, m, :], start=m == 0, stop=m == HT - 1)
                        ins.then_inc(y_full, 1)

                expert_rounds(pe, E, round_of_experts)

            after(pe, "ident")
            turn_norm("x0.xT", "x0.xn", xn)
            arrived(pe, "x0")
            after(pe, "x0.xT.sb")
            project(ps_o[:, 0:D], lambda c: xT[:, c, :], lambda c: wq0[:, c, :]).then_inc(stage("x0.q"), 1)
            after(pe, "x0.qx")
            after(pe, "ident16")
            for h in range(HEADS):
                ins = pe.transpose(ps_s16[:, h * P:(h + 1) * P], qx[:, h * P:(h + 1) * P], ident16[:, :])
            ins.then_inc(stage("x0.qxT"), 1)
            after(pe, "x0.q16")
            after(pe, "x0.w16")
            after(pe, "x0.bk")
            after(pe, "ones16")
            cross(L0)
            after(pe, "x0.rden")
            per_row(L0).then_inc(stage("x0.rden_rows"), 1)
            arrived(pe, "x0b")
            after(pe, "x0.done")
            project(ps_o[:, 0:D], lambda g: O[:, g * P:(g + 1) * P], lambda g: wox[:, g, :],
                    4).then_inc(stage("x0.out"), 1)

            turn_norm("la.xT", "la.xn", xn)
            arrived(pe, "la")
            after(pe, "la.xT.sb")
            for e in range(DC):
                cut = slice(e * P, (e + 1) * P)
                project(ps_s[:, e * P:(e + 1) * P], lambda c: la_wq[:, c, cut], lambda c: xT[:, c, :])
                project(ps_s[:, D + e * P:D + (e + 1) * P], lambda c: la_wk[:, c, cut], lambda c: xT[:, c, :])
            project(ps_s[:, 512:512 + D], lambda c: xT[:, c, :], lambda c: la_wv[:, c, :])
            project(ps_s[:, 512 + D:1024], lambda c: xT[:, c, :], lambda c: la_wq[:, c, :])
            project(ps_s[:, 1024:1024 + P], lambda c: la_wgq[:, c, :], lambda c: xT[:, c, :])
            project(ps_s[:, 1024 + P:1024 + P + 64], lambda c: la_wgk[:, c, :], lambda c: xpool[:, c, :])
            project(ps_s[0:64, 1536:1536 + P], lambda c: xpool[:, c, :],
                    lambda c: la_wgv[:, c, :]).then_inc(stage("la.proj"), 1)
            after(pe, "la.kz")
            for g in range(4):
                pe.matmul(ps_s[:, g * 512:(g + 1) * 512], qT[:, g // 2, :], kflat[:, g * 512:(g + 1) * 512],
                          start=True, stop=True)
            pe.matmul(ps_ring[:, 0:512], qT[:, 4, :], kflat[:, 2048:2560], start=True,
                      stop=True).then_inc(stage("la.scores"), 1)
            after(pe, "la.local.exps")
            turn(wide_a, ps_s, HEADS).then_inc(stage("la.turned"), 1)
            after(pe, "la.turned.sb")
            for h in range(HEADS):
                ins = pe.matmul(ps_o[:, h * 16:(h + 1) * 16], wide_b[:, h * P:(h + 1) * P],
                                v_nat[:, h * 16:(h + 1) * 16], start=True, stop=True)
            ins.then_inc(stage("la.pv"), 1)
            after(pe, "la.lat.exps")
            for h in range(8):
                ins = pe.transpose(ps_s[0:64, h * P:(h + 1) * P], lat_s[:, h * 64:(h + 1) * 64], ident[:, :])
            ins.then_inc(stage("la.lturned"), 1)
            after(pe, "la.lturned.sb")
            for h in range(8):
                ins = pe.matmul(ps_o[:, 512 + h * 16:512 + (h + 1) * 16], wide_a[0:64, h * P:(h + 1) * P],
                                gv_nat[:, h * 16:(h + 1) * 16], start=True, stop=True)
            ins.then_inc(stage("la.lpv"), 1)
            after(pe, "la.rem")
            turn(rem, ps_ring[:, 0:P], 1).then_inc(stage("la.remT"), 1)
            after(pe, "la.remT.sb")
            pe.matmul(ps_ring[:, 512:512 + D], qT[:, 0, :], la_rout[:, :], start=True,
                      stop=True).then_inc(stage("la.rproj"), 1)
            turn_norm("la.attnT", "la.attn", xn)
            after(pe, "la.attnT.sb")
            project(ps_o[:, 0:D], lambda c: xT[:, c, :], lambda c: la_wout[:, c, :]).then_inc(stage("la.out_ps"), 1)

            arrived(pe, "f0")
            pe.transpose(ps_ring[:, 512:512 + 8 * HT], bin_rows[0:8 * HT, :],
                         ident[0:8 * HT, 0:8 * HT]).then_inc(stage("f0.bias"), 1)
            turn_norm("f0.xT", "f0.xn", xn)
            after(pe, "f0.xT.sb")
            project(ps_o[:, 0:8], lambda c: xT[:, c, :], lambda c: wgate0[:, c, :]).then_inc(stage("f0.logits"), 1)
            experts("f0", 8, 0)

            turn_norm("xm.xT", "xm.affine", xm)
            arrived(pe, "x1big")
            arrived(pe, "x1")
            after(pe, "xm.xT.sb")
            for t in range(8):
                cut = slice(t * P, (t + 1) * P)
                project(ps_s[:, t * P:(t + 1) * P], lambda c: WQ1[:, c, cut], lambda c: xT[:, c, :])
                project(ps_s[:, 1024 + t * P:1024 + (t + 1) * P], lambda c: WKV1[:, c, cut], lambda c: xT[:, c, :])
            for g in range(2):
                ins = project(ps_o[:, g * 512:(g + 1) * 512], lambda c: xT[:, c, :],
                              lambda c: WKV1[:, c, 1024 + g * 512:1024 + (g + 1) * 512])
            for g in range(2):
                ins = project(ps_ring[:, g * 512:(g + 1) * 512], lambda c: xT[:, c, :],
                              lambda c: WQ1[:, c, g * 512:(g + 1) * 512])
            ins.then_inc(stage("x1.proj"), 1)
            after(pe, "x1.qk")
            for t in range(8):
                for c in range(2):
                    n = c * 8 + t
                    ins = pe.matmul(ps_s[:, n * P:(n + 1) * P], qT[64 * c:64 * c + 64, t, :],
                                    k_self[64 * c:64 * c + 64, t, :], start=True, stop=True)
            ins.then_inc(stage("x1.self_scores"), 1)
            after(pe, "x1.self.exps")
            turn(wide_a, ps_s, HEADS).then_inc(stage("x1.turned"), 1)
            after(pe, "x1.turned.sb")
            for h in range(HEADS):
                row0 = 64 * (h % 2)
                ins = pe.matmul(ps_o[row0:row0 + 64, (h // 2) * P:(h // 2 + 1) * P], v_self[:, h * 64:(h + 1) * 64],
                                wide_b[:, h * P:(h + 1) * P], start=True, stop=True)
            ins.then_inc(stage("x1.self_pv"), 1)
            after(pe, "x1.qx")
            for i in range(2 * HEADS):
                ins = pe.transpose(ps_s16[:, i * P:(i + 1) * P], qx[:, i * P:(i + 1) * P], ident16[:, :])
            ins.then_inc(stage("x1.qxT"), 1)
            after(pe, "x1.start")
            after(pe, "x1.q16")
            after(pe, "x1.w16")
            cross(L1)
            after(pe, "x1.rden")
            per_row(L1).then_inc(stage("x1.rden_rows"), 1)
            after(pe, "x1.done")
            project(ps_o[:, 0:D], lambda t: O[:, t * P:(t + 1) * P], lambda t: wo1[:, t, :],
                    8).then_inc(stage("x1.out"), 1)

            arrived(pe, "la1")
            for i, w in enumerate((la_wq, la_wk, la_wv, la_wout)):
                for c in range(DC):
                    for e in range(DC):
                        col = i * 512 + c * D + e * P
                        ins = pe.transpose(ps_s[:, col:col + P], w[:, e, c * P:(c + 1) * P], ident[:, :])
            ins.then_inc(stage("l1.wT"), 1)
            turn_norm("l1.xT", "l1.xn", xn)
            after(pe, "l1.wT.sb")
            after(pe, "l1.xT.sb")
            for e in range(DC):
                for i in range(2):
                    col = i * D + e * P
                    project(ps_s[:, col:col + P], lambda c: wT[:, i, c, e * P:(e + 1) * P], lambda c: xT[:, c, :])
            project(ps_s[:, 512:512 + D], lambda c: xT[:, c, :], lambda c: wT[:, 2, c, :]).then_inc(stage("l1.proj"), 1)
            after(pe, "l1.qz")
            for g in range(4):
                e = g // 2
                ins = pe.matmul(ps_s[:, g * 512:(g + 1) * 512], sp_z[:, D + e * P:D + (e + 1) * P],
                                kflat[:, g * 512:(g + 1) * 512], start=True, stop=True)
            ins.then_inc(stage("l1.scores"), 1)
            after(pe, "l1.causal")
            for h in range(HEADS):
                ins = pe.matmul(ps_o[:, h * 17:(h + 1) * 17], wide_a[:, h * P:(h + 1) * P], v_ext[:, h, :],
                                start=True, stop=True)
            ins.then_inc(stage("l1.pv"), 1)
            turn_norm("l1.attnT", "l1.attn", xn)
            after(pe, "l1.attnT.sb")
            project(ps_o[:, 512:512 + D], lambda c: xT[:, c, :], lambda c: wT[:, 3, c, :]).then_inc(stage("l1.out"), 1)

            arrived(pe, "f1")
            pe.transpose(ps_ring[:, 512:512 + P], b1_rows[:, :], ident[:, :]).then_inc(stage("f1.bias"), 1)
            turn_norm("f1.xT", "f1.xn", xn)
            after(pe, "f1.xT.sb")
            project(ps_o[:, 0:16], lambda c: xT[:, c, :], lambda c: wr1[:, c, :]).then_inc(stage("f1.logits"), 1)
            experts("f1", 16, 8)


_OUT_SHAPE = (1, P, D)


def kernel(**inputs):
    import concourse.bacc as _bacc
    from concourse.bass_utils import run_bass_kernel_spmd as _run

    nc = _bacc.Bacc("TRN2", target_bir_lowering=False, num_devices=1)
    arrays, args = {}, {}
    for name, value in inputs.items():
        v = np.ascontiguousarray(value)
        arrays[f"in_{name}_dram"] = v
        args[name] = nc.dram_tensor(f"in_{name}_dram", v.shape, mybir.dt.from_np(v.dtype), kind="ExternalInput").ap()
    out = nc.dram_tensor("out_0_dram", _OUT_SHAPE, FP32, kind="ExternalOutput").ap()
    perceiver(nc, args, out)
    r = _run(nc, [arrays], core_ids=[0])
    return r.results[0]["out_0_dram"]
```

```python
import numpy as np
import concourse.bass as bass
from concourse import mybir
from concourse.alu_op_type import AluOpType as ALU
from contextlib import ExitStack

ACT = mybir.ActivationFunctionType
AX = mybir.AxisListType
FP32 = mybir.dt.float32
FP16 = mybir.dt.float16
INT32 = mybir.dt.int32

P = 128
D = 256
DC = D // P
KEYS = 12544
TILES = 7
BLK = TILES * P
NBLK = KEYS // BLK
HEADS = 16
SPLIT = 4
WSCALE = 16.0
MASKED = -1.0e12
HUGE = 3.0e38
HID = 1024
HT = HID // P
SLOTS = 2


class Cross:

    def __init__(self, name, head_dim, feature_cols, masked, sem):
        self.name = name
        self.dv = head_dim
        self.cols = feature_cols
        self.masked = masked
        self.together = 64 // head_dim if head_dim < 64 else 2
        self.width = P // self.together
        self.used = HEADS // self.together * P
        self.heads_per_turn = max(32 // head_dim, 1)
        self.slots = 2 * self.together

        self.before = self.context_groups() + [("natural", 0, t) for t in range(TILES)] \
            + [("keys", x) for x in self.keys_at(-1)]
        self.first, self.body, self.final = ([g for h in range(HEADS) for g in self.period(h, kind)]
                                             for kind in ("first", "body", "final"))
        self.epilogue = [g for h in range(HEADS, HEADS + 4) for g in self.period(h, "final")]
        self.banks = {g: j % 3 for j, g in enumerate(self.body)}
        for k in (0, 1):
            for r in range(2):
                self.banks["probs", HEADS - 2 + k, r] = self.banks["probs", k - 2, r]
        self.banks["factors", 1] = self.banks["factors", -1]
        self.ctx_in = sem(name + "_ctx_in")
        self.ring_full = [sem(f"{name}_ring_full{i}") for i in range(3)]
        self.ring_free = [sem(f"{name}_ring_free{i}") for i in range(3)]
        self.high = sem(name + "_high")
        self.scores = sem(name + "_scores")
        self.blkmax = sem(name + "_blkmax")
        self.negmax = sem(name + "_negmax")
        self.probs = sem(name + "_probs")
        self.shift = sem(name + "_shift")
        self.corr = sem(name + "_corr")
        self.sums = sem(name + "_sums")
        self.pv = sem(name + "_pv")
        self.scaled = sem(name + "_scaled")
        self.acc = sem(name + "_acc")

    def context_groups(self):
        return [("context", c, r) for c in range(DC) for r in range(2)]

    def keys_at(self, h):
        ahead = {7: (h + 1, h + 2), 6: ()}.get(h % 8, (h + 2,))
        return [k % HEADS // self.heads_per_turn for k in ahead if k % self.heads_per_turn == 0]

    def natural_at(self, h):
        tiles = {2: (0,), 3: (1, 2), 4: (3,), 5: (4, 5), 6: (6,)}
        return (1 if h < HEADS // 2 else 0), tiles.get(h % (HEADS // 2), ())

    def context_at(self, h):
        return {7: self.context_groups()[0:2], 8: self.context_groups()[2:3], 9: self.context_groups()[3:4]}.get(h, [])

    def period(self, h, kind):
        last = kind == "final"
        keys = [("keys", x) for x in self.keys_at(h)] if h < HEADS - last else []
        turned = [("probs", h - 2, r) for r in range(2)] if h - 2 < HEADS and not (kind == "first" and h < 2) else []
        half, tiles = self.natural_at(h)
        nat = [("natural", half, t) for t in tiles] if h < (HEADS // 2 if last else HEADS) else []
        if h % 8 != 2:
            return keys + nat[0:1] + turned[0:1] + nat[1:2] + turned[1:2] + ([] if last else self.context_at(h))
        factors = [("factors", h // 8 - 1)] if not (kind == "first" and h == 2) else []
        return keys + turned + factors + nat

    def count(self, b, group, what):
        done = lambda groups: sum(1 for g in groups if what(g))
        upto = lambda groups: done(groups[:groups.index(group) + 1])
        if isinstance(b, int) and b == 0:
            return done(self.before) + upto(self.first)
        if isinstance(b, int) and b == NBLK - 1:
            start = done(self.before + self.first) + (NBLK - 2) * done(self.body)
            if group in self.final:
                return start + upto(self.final)
            return start + done(self.final) + upto(self.epilogue)
        return b * done(self.body) + (done(self.before + self.first) - done(self.body) + upto(self.body))

    def at(self, b, group):
        bank = self.banks[group]
        return bank, self.count(b, group, lambda g: self.banks[g] == bank)

    def at_first(self, group):
        bank = self.banks[group]
        return bank, sum(1 for g in self.before[:self.before.index(group) + 1] if self.banks[g] == bank)

    def high_at(self, b, group):
        return self.count(b, group, lambda g: g[0] in ("natural", "probs", "context"))

    def last_in_banks(self, groups):
        return list({self.banks[g]: g for g in groups}.values())

    def weighted_at(self, h):
        late = self.together + 2
        return (h - late) // self.together if (h - late) % self.together == 0 else None


def perceiver(nc, a, out):
    ctx = ExitStack()
    with ctx:
        def sb(name, shape, dt=FP32):
            return ctx.enter_context(nc.sbuf_tensor(name, shape, dt))

        def sem(name):
            return ctx.enter_context(nc.semaphore(name))

        norms = ["x0", "la", "f0", "x1", "xm", "l1", "f1"]
        turned_norms = ["x0", "la", "f0", "xm", "l1", "f1"]
        attentions = ["la", "l1"]
        routed = ["f0", "f1"]
        shared = {"var": norms, "sd": norms, "xn": norms, "xT": turned_norms, "xT.sb": turned_norms,
                  "attn": attentions, "attnT": attentions, "attnT.sb": attentions,
                  "bias": routed, "bias.sb": routed, "logits": routed, "top": routed, "exp": routed, "comb": routed,
                  "combT": routed, "combT.sb": routed, "bias_ps": routed, "bias_used": routed}
        stages = {}

        def place(name):
            phase, _, step = name.partition(".")
            return (step, shared[step].index(phase) + 1) if step in shared else (name, 1)

        def stage(name):
            key = place(name)[0]
            if key not in stages:
                stages[key] = sem("step_" + key.replace(".", "_"))
            return stages[key]

        X = sb("X", [P, D])
        xn = sb("xn", [P, D])
        xm = sb("xm", [P, D])
        xT = sb("xT", [P, DC, P])
        ident = sb("ident", [P, P])
        headmask = sb("headmask", [P, 8])
        window = sb("window", [P, P])
        latmask = sb("latmask", [P, 64])
        causal = sb("causal", [P, P])
        rev8 = sb("rev8", [P, 8])
        rev16 = sb("rev16", [P, 16])
        stats = sb("stats", [P, 6])
        meanvar = sb("meanvar", [P, 2])
        sd = sb("sd", [P, 2])
        ctx_nat = sb("ctx_nat", [P, TILES, D])
        ctxT = sb("ctxT", [P, 2, DC, BLK], FP16)
        kT = sb("kT", [P, 4, BLK], FP16)
        vals = sb("vals", [P, TILES * 2048], FP16)
        probs = sb("probs", [P, 2, 1024])
        probsT = sb("probsT", [P, 8, 2, BLK], FP16)
        q16 = sb("q16", [P, HEADS, 2, P], FP16)
        w16 = sb("w16", [P, DC, 2, 1024], FP16)
        bk16 = sb("bk16", [2, D], FP16)
        bkf = sb("bkf", [2, 3 * D])
        ident16 = sb("ident16", [P, P], FP16)
        ones16 = sb("ones16", [2, P], FP16)
        masked_s = sb("masked_s", [P, 2, BLK])
        mask_raw = sb("mask_raw", [P, BLK], INT32)
        mask_add = sb("mask_add", [P, BLK])
        O = sb("O", [P, 1024])
        den = sb("den", [P, HEADS])
        negcur = sb("negcur", [P, HEADS])
        negprev = sb("negprev", [P, HEADS])
        blkmax = sb("blkmax", [P, HEADS])
        rowsum = sb("rowsum", [P, HEADS])
        shift = sb("shift", [P, HEADS])
        factors = sb("factors", [P, 1024])
        wq0 = sb("wq0", [P, DC, D])
        wk0 = sb("wk0", [P, DC, D])
        wv0 = sb("wv0", [P, DC, D])
        wox = sb("wox", [P, 4, D])
        bvcol = sb("bvcol", [P, 4])
        la_wq = sb("la_wq", [P, DC, D])
        la_wk = sb("la_wk", [P, DC, D])
        la_wv = sb("la_wv", [P, DC, D])
        la_wgq = sb("la_wgq", [P, DC, P])
        la_wgk = sb("la_wgk", [P, DC, P])
        la_wgv = sb("la_wgv", [P, DC, P])
        la_rout = sb("la_rout", [P, D])
        la_wout = sb("la_wout", [P, DC, D])
        wo1 = sb("wo1", [P, 8, D])
        rows = sb("rows", [P, 7, D])
        BQ0, BO0, GL, GR, LNG, LNB, BO1 = range(7)
        wgate0 = sb("wgate0", [P, DC, 8])
        wr1 = sb("wr1", [P, DC, 16])
        br1 = sb("br1", [P, 16])
        bout0 = sb("bout0", [8, D])
        b2_1 = sb("b2_1", [16, D])
        bin_rows = sb("bin_rows", [P, P])
        b1_rows = sb("b1_rows", [P, P])
        bin_cols = sb("bin_cols", [P, 8 * HT])
        b1_cols = sb("b1_cols", [P, 16 * HT])
        win = sb("win", [P, SLOTS, DC, HID])
        wout = sb("wout", [P, SLOTS, HT, D])
        gate = sb("gate", [P, 8, 16])
        comb = sb("comb", [P, 16])
        combT = sb("combT", [16, P])
        pad = sb("pad", [P, 2])
        carrier = sb("carrier", [P, HEADS])
        gatecol = sb("gatecol", [P, 8])
        gates = sb("gates", [P, 32])
        kflat = probsT[:, :, :, :].rearrange("p a b c -> p (a b c)").bitcast(FP32)
        vflat = vals[:, :].bitcast(FP32)
        wide_a = probs[:, :, :].rearrange("p a b -> p (a b)")
        wide_b = vflat[:, 0:2048]
        v_self = vflat[:, 6144:7168]
        wm1 = wide_a.rearrange("p (c n) -> p c n", c=DC)
        qT = q16[:, :, :, :].rearrange("p h t q -> p (h t q)").bitcast(FP32)[:, 0:1024].rearrange("p (t q) -> p t q", t=8)
        hT = vflat[:, 4096:4096 + 2 * HID].rearrange("p (s t n) -> p s t n", s=2, t=HT)
        attn = kflat[:, 4224:4224 + D]
        kflat16 = probsT[:, :, :, :].rearrange("p a b c -> p (a b c)")
        qx = kflat16[:, 0:4096]
        qhi = kflat16[:, 4096:5120]
        qlo = kflat16[:, 5120:6144]
        qn = masked_s[:, :, :].rearrange("p a b -> p (a b)")[:, 0:1024]
        kz = kflat[:, 0:2048].rearrange("p (e h k) -> p e h k", e=2, h=8)
        gkz = kflat[:, 2048:2560].rearrange("p (h k) -> p h k", h=8)
        lat_s = kflat[:, 2560:3072]
        q_nat = kflat[:, 3072:3328]
        v_nat = kflat[:, 3328:3584]
        gv_nat = kflat[0:64, 3584:3712]
        rem = kflat[:, 3712:3840]
        xpool = kflat[:, 3840:3968].rearrange("p (c n) -> p c n", c=DC)
        k_self = kflat[:, 6144:7168].rearrange("p (t n) -> p t n", t=8)
        v_ext = kflat[:, 2048:2048 + HEADS * 17].rearrange("p (h d) -> p h d", h=HEADS)
        sp_z, sp_a, sp_w, sp_u = (kflat[:, 4096 + 512 * i:4096 + 512 * (i + 1)] for i in range(4))
        wT = wide_b.rearrange("p (w c n) -> p w c n", w=4, c=DC)

        ps_s = ctx.enter_context(nc.psum_tensor("ps_s", [P, 4 * 512], FP32))
        ps_ring = ctx.enter_context(nc.psum_tensor("ps_ring", [P, 2 * 512], FP32))
        ps_o = ctx.enter_context(nc.psum_tensor("ps_o", [P, 2 * 512], FP32))

        ps_s16 = ps_s[:, :].bitcast(FP16)
        RING = (ps_ring[:, 0:512], ps_ring[:, 512:1024], ps_o[:, 512:1024])
        L0 = Cross("x0", 16, 512, True, sem)
        L1 = Cross("x1", 64, 1024, False, sem)

        def by_row(L):
            return factors[:, 0:HEADS * L.width].rearrange("p (h w) -> p h w", h=HEADS)

        def natural(L, t, heads, part):
            per = 2 * L.cols
            v = vals[:, t * per:(t + 1) * per].rearrange("p (h part d) -> p h part d", part=2, d=L.dv)
            return v[:, heads, part, :]

        def natural_group(L, half, t, part):
            units = L.cols // L.dv // 2
            return natural(L, t, slice(half * units, (half + 1) * units), part)

        def stationary(L, t, head, parts):
            unit = head // 8 * 16 + 8 + head % 8 if L is L0 else head
            at = t * 2 * L.cols + unit * 2 * L.dv
            return vals[:, at + parts.start * L.dv:at + parts.stop * L.dv]
        mask_in = sem("mask_in")
        mask_converted = sem("mask_converted")
        mask_ready = sem("mask_ready")
        expert_in = [sem(f"expert_in{s}") for s in range(SLOTS)]
        hid_full = sem("hid_full")
        hid_ready = sem("hid_ready")
        y_full = sem("y_full")
        y_added = sem("y_added")
        loads = {k: sem("load_" + k) for k in ("x", "x0", "x0b", "la", "f0", "x1", "x1big", "la1", "f1")}
        stored = sem("stored")
        act_step = sem("act_step")
        dve_step = sem("dve_step")
        pool_step = sem("pool_step")

        def chunked(w):
            return w.rearrange("(c p) n -> p c n", p=P)

        def row(v, n=D):
            return v.rearrange("(a n) -> a n", a=1).broadcast_to([P, n])

        LOADS = {
            "x": [(X[:, :], a["x"].rearrange("a s d -> (a s) d"))],
            "x0": [(wq0[:, :, :], chunked(a["L0_xattn_Wq"])), (wk0[:, :, :], chunked(a["L0_xattn_Wk"])),
                   (wv0[:, :, :], chunked(a["L0_xattn_Wv"])),
                   (rows[:, BQ0, :], row(a["L0_xattn_bq"])),
                   (bkf[:, 0:D], a["L0_xattn_bk"].rearrange("(a n) -> a n", a=1).broadcast_to([2, D]))],
            "x0b": [(wox[i * 32 + part * 16:i * 32 + part * 16 + 16, :, :],
                     a["L0_xattn_Wo"].rearrange("(g i d) n -> i d g n", g=4, i=4)[i])
                    for i in range(4) for part in range(2)]
                   + [(bvcol[i * 32:i * 32 + 16, :], a["L0_xattn_bv"].rearrange("(g i d) -> i d g", g=4, i=4)[i])
                      for i in range(4)]
                   + [(rows[:, BO0, :], row(a["L0_xattn_bo"]))],
            "la": [(la_wq[:, :, :], chunked(a["L0_attn_wq"])), (la_wk[:, :, :], chunked(a["L0_attn_wk"])),
                   (la_wv[:, :, :], chunked(a["L0_attn_wv"])), (la_wgq[:, :, :], chunked(a["L0_attn_wgq"])),
                   (la_wgk[:, :, :], chunked(a["L0_attn_wgk"])), (la_wgv[:, :, :], chunked(a["L0_attn_wgv"])),
                   (la_rout[:, :], a["L0_attn_r_out_w"]), (la_wout[:, :, :], chunked(a["L0_attn_w_out"])),
                   (rows[:, GL, :], row(a["L0_attn_gate_local_w"].rearrange("h d -> (h d)"))),
                   (rows[:, GR, :], row(a["L0_attn_gate_remote_w"].rearrange("h d -> (h d)")))],
            "f0": [(wgate0[:, :, :], chunked(a["L0_ffn_W_gate"])), (bout0[:, :], a["L0_ffn_b_out"]),
                   (bin_rows[0:8 * HT, :], a["L0_ffn_b_in"].rearrange("e (t p) -> (e t) p", p=P))],
            "x1": [(wo1[:, :, :], chunked(a["L1_xattn_Wo"])),
                   (rows[:, LNG, :], row(a["L1_xattn_ln_g"])), (rows[:, LNB, :], row(a["L1_xattn_ln_b"])),
                   (rows[:, BO1, :], row(a["L1_xattn_bo"]))],
            "x1big": [(kflat[:, 4096:6144].rearrange("p (c n) -> p c n", c=DC), chunked(a["L1_xattn_Wq"])),
                      (vflat[:, 0:4096].rearrange("p (c n) -> p c n", c=DC), chunked(a["L1_xattn_Wkv"])),
                      (wm1, chunked(a["L1_xattn_Wm"]))],
            "la1": [(la_wq[:, :, :], chunked(a["L1_attn_Wq"])), (la_wk[:, :, :], chunked(a["L1_attn_Wk"])),
                    (la_wv[:, :, :], chunked(a["L1_attn_Wv"])), (la_wout[:, :, :], chunked(a["L1_attn_Wo"]))],
            "f1": [(wr1[:, :, :], chunked(a["L1_ffn_Wr"])), (br1[:, :], row(a["L1_ffn_br"], 16)),
                   (b2_1[:, :], a["L1_ffn_b2"]), (b1_rows[:, :], a["L1_ffn_b1"].rearrange("e (t p) -> (e t) p", p=P))],
        }
        WQ1 = LOADS["x1big"][0][0]
        WKV1 = LOADS["x1big"][1][0]
        ctx_blocks = a["ctx_1024"].rearrange("a (b p t) d -> (a b) p t d", p=P, t=TILES)
        mask_blocks = a["mask_Bx1xSxS2_ik1"].rearrange("a c q (b n) -> (a c b) q n", n=BLK)

        def arrived(eng, key):
            eng.wait_ge(loads[key], 16 * len(LOADS[key]))

        def after(eng, name):
            eng.wait_ge(stage(name), place(name)[1])

        def expert_rounds(eng, E, body):
            body(0)
            with eng.Fori(0, E // SLOTS - 1) as i:
                body(i + 1)

        block = ctx.enter_context(nc.Block())

        @block.sync
        def _(sp):
            def load(key):
                for dst, src in LOADS[key]:
                    with nc.allow_non_contiguous_dma(reason="a bias vector of 256 values as columns"):
                        sp.dma_start(dst, src).then_inc(loads[key], 16)

            def load_bias_rows():
                after(sp, "bvcol")
                load("x0b")

            def ctx_load(L, b):
                sp.dma_start(ctx_nat[:, :, :], ctx_blocks[b]).then_inc(L.ctx_in, 16)

            def mask_load(b):
                sp.dma_start(mask_raw[:, :], mask_blocks[b]).then_inc(mask_in, 16)

            def expert_load(w1, w2, e, slot):
                sp.dma_start(win[:, slot, :, :], w1[e].rearrange("(c p) n -> p c n", p=P)).then_inc(expert_in[slot], 16)
                sp.dma_start(wout[:, slot, :, :], w2[e].rearrange("(t p) n -> p t n", p=P)).then_inc(expert_in[slot], 16)

            def ctx_stream(L):
                bank, seq = L.at_first(L.context_groups()[-1])
                sp.wait_ge(L.ring_full[bank], seq)
                ctx_load(L, 1)
                if L.masked:
                    sp.wait_ge(mask_ready, 1)
                    mask_load(1)
                with sp.Fori(0, NBLK - 2) as i:
                    bank, seq = L.at(i, L.context_groups()[-1])
                    sp.wait_ge(L.ring_full[bank], seq)
                    ctx_load(L, i + 2)
                    if L.masked:
                        sp.wait_ge(mask_ready, i + 2)
                        mask_load(i + 2)

            w0 = (a["L0_ffn_W_in"], a["L0_ffn_W_out"])
            w1 = (a["L1_ffn_W1"], a["L1_ffn_W2"])
            load("x")
            ctx_load(L0, 0)
            mask_load(0)
            load("x0")
            load_bias_rows()
            load("la")
            load("f0")
            load("x1")
            load("f1")
            for s in range(SLOTS):
                expert_load(*w0, s, s)
            ctx_stream(L0)
            after(sp, "la.out_ps")
            ctx_load(L1, 0)
            load("x1big")
            load("la1")
            with sp.Fori(0, 8 // SLOTS - 1) as i:
                for s in range(SLOTS):
                    sp.wait_ge(y_full, i * SLOTS + (s + 1))
                    expert_load(*w0, i * SLOTS + (SLOTS + s), s)
            for s in range(SLOTS):
                sp.wait_ge(y_full, 8 - SLOTS + s + 1)
                expert_load(*w1, s, s)
            ctx_stream(L1)
            with sp.Fori(0, 16 // SLOTS - 1) as i:
                for s in range(SLOTS):
                    sp.wait_ge(y_full, i * SLOTS + (8 + s + 1))
                    expert_load(*w1, i * SLOTS + (SLOTS + s), s)
            after(sp, "f1.done")
            sp.dma_start(out.rearrange("a s d -> (a s) d"), X[:, :]).then_inc(stored, 16)
            sp.wait_ge(stored, 16)

        @block.gpsimd
        def _(pool):
            count = [0]

            def link(ins):
                count[0] += 1
                ins.then_inc(pool_step, 1)
                pool.wait_ge(pool_step, count[0])

            link(pool.memset(ident[:, :], 0.0))
            pool.affine_select(out=ident[:, :], in_=ident[:, :], compare_op=ALU.not_equal, fill=1.0, base=0,
                               pattern=[[-1, P]], channel_multiplier=1).then_inc(stage("ident"), 1)
            pool.memset(bvcol[:, :], 0.0).then_inc(stage("bvcol"), 1)
            link(pool.memset(ident16[:, :], 0.0))
            pool.affine_select(out=ident16[:, :], in_=ident16[:, :], compare_op=ALU.not_equal, fill=1.0, base=0,
                               pattern=[[-1, P]], channel_multiplier=1).then_inc(stage("ident16"), 1)
            pool.memset(ones16[:, :], 1.0).then_inc(stage("ones16"), 1)
            link(pool.memset(headmask[:, :], 1.0))
            link(pool.affine_select(out=headmask[:, :], in_=headmask[:, :], compare_op=ALU.is_ge, fill=0.0, base=0,
                                    pattern=[[-16, 8]], channel_multiplier=1))
            pool.affine_select(out=headmask[:, :], in_=headmask[:, :], compare_op=ALU.is_ge, fill=0.0, base=15,
                               pattern=[[16, 8]], channel_multiplier=-1).then_inc(stage("headmask"), 1)

            def mask_convert(b):
                pool.wait_ge(mask_in, (b + 1) * 16)
                pool.tensor_tensor(pad[:, 1:2], headmask[:, 0:1], headmask[:, 1:2], ALU.add)
                pool.tensor_scalar(mask_raw[:, :].bitcast(FP32), mask_raw[:, :], 0.0, -MASKED, ALU.is_equal,
                                   ALU.mult).then_inc(mask_converted, 1)

            after(pool, "headmask")
            mask_convert(0)
            link(pool.memset(window[:, :], 0.0))
            link(pool.affine_select(out=window[:, :], in_=window[:, :], compare_op=ALU.is_ge, fill=-HUGE, base=0,
                                    pattern=[[-1, P]], channel_multiplier=1))
            link(pool.affine_select(out=window[:, :], in_=window[:, :], compare_op=ALU.is_ge, fill=-HUGE, base=63,
                                    pattern=[[1, P]], channel_multiplier=-1))
            link(pool.memset(latmask[:, :], 0.0))
            link(pool.affine_select(out=latmask[:, :], in_=latmask[:, :], compare_op=ALU.is_ge, fill=-HUGE, base=0,
                                    pattern=[[-2, 64]], channel_multiplier=1))
            link(pool.memset(causal[:, :], 1.0))
            link(pool.affine_select(out=causal[:, :], in_=causal[:, :], compare_op=ALU.is_ge, fill=0.0, base=0,
                                    pattern=[[1, P]], channel_multiplier=-1))
            for e in range(16):
                if e < 8:
                    link(pool.memset(rev8[:, e:e + 1], float(8 - e)))
                link(pool.memset(rev16[:, e:e + 1], float(16 - e)))
            pool.memset(rev16[:, 0:1], 16.0).then_inc(stage("consts"), 1)
            with pool.Fori(0, NBLK - 1) as i:
                mask_convert(i + 1)

        @block.scalar
        def _(act):
            count = [0]

            def link(ins):
                count[0] += 1
                ins.then_inc(act_step, 1)
                act.wait_ge(act_step, count[0])

            def ln_root(tag):
                after(act, tag + ".var")
                act.activation(sd[:, 0:1], sd[:, 1:2], ACT.Sqrt).then_inc(stage(tag + ".sd"), 1)

            def leading(L, place, dst, n, scale=1.0):
                bank, seq = place
                act.wait_ge(L.ring_full[bank], seq)
                src = RING[bank][:, 0:n]
                if len(dst.shape) == 3:
                    src = src.rearrange("p (h d) -> p h d", d=L.dv)
                act.activation(dst, src, ACT.Copy, scale=scale).then_inc(L.high, 1)

            def context(L, places):
                for (_, c, r), at in places:
                    leading(L, at, ctxT[:, 0, c, r * 512:(BLK if r else 512)], 384 if r else 512)

            def naturals(L, half, tiles, at):
                for t in tiles:
                    leading(L, at(("natural", half, t)), natural_group(L, half, t, 0), L.cols // 2, 1.0 / WSCALE)

            def keys(L, x, place):
                bank, seq = place
                act.wait_ge(L.ring_full[bank], seq)
                act.activation(kT[:, x % 4, :], RING[bank].bitcast(FP16)[:, 0:BLK], ACT.Copy)\
                   .then_inc(L.ring_free[bank], 1)

            def mask_order(b, kind):
                act.wait_ge(mask_converted, b + 1)
                if kind != "first":
                    act.wait_ge(L0.negmax, b * HEADS)
                act.activation(mask_add[:, :].rearrange("q (t p) -> q t p", p=P),
                               mask_raw[:, :].bitcast(FP32).rearrange("q (p t) -> q t p", t=TILES),
                               ACT.Copy).then_inc(mask_ready, 1)

            def exps(L, b, h, kind):
                if 0 <= h < HEADS or (h == -1 and kind != "first"):
                    k = h % HEADS
                    act.wait_ge(L.negmax, b * HEADS + (h + 1))
                    if k % 8 == 0 and kind != "first":
                        act.wait_ge(L.sums, b * 2 + (k // 8 - 1))
                    src = masked_s[:, k % 2, :] if L.masked else ps_s[:, 1024 * (k % 2):1024 * (k % 2) + BLK]
                    act.activation(probs[:, k % 2, 0:BLK], src, ACT.Exp, bias=negcur[:, k:k + 1],
                                   scale=-1.0 if L.masked else 1.0,
                                   accum_out=rowsum[:, k:k + 1]).then_inc(L.probs, 1)

            def period(L, b, h, kind):
                groups = L.period(h, kind)
                if L.masked and h == 0:
                    mask_order(b, kind)
                exps(L, b, h - 1, kind)
                for g in groups:
                    if g[0] == "keys" and g[1] % 2 == 0:
                        keys(L, g[1], L.at(b, g))
                    if g[0] == "probs":
                        _, k, r = g
                        leading(L, L.at(b, g), probsT[:, k % L.slots, 0, r * 512:(BLK if r else 512)],
                                384 if r else 512)
                    if g[0] == "natural":
                        naturals(L, g[1], (g[2],), lambda g: L.at(b, g))
                if h % 8 == 1 and not (kind == "first" and h == 1):
                    q = (h // 8 + 1) % 2
                    act.wait_ge(L.shift, b * 2 + h // 8)
                    act.activation(by_row(L)[:, 8 * q:8 * q + 8, :],
                                   shift[:, 8 * q:8 * q + 8].unsqueeze(2).broadcast_to([P, 8, L.width]),
                                   ACT.Exp).then_inc(L.corr, 1)
                context(L, [(g, L.at(b, g)) for g in groups if g[0] == "context"])

            def cross(L):
                context(L, [(g, L.at_first(g)) for g in L.context_groups()])
                naturals(L, 0, range(TILES), L.at_first)
                keys(L, 0, L.at_first(("keys", 0)))
                for h in range(HEADS):
                    period(L, 0, h, "first")
                with act.Fori(0, NBLK - 2) as i:
                    for h in range(HEADS):
                        period(L, i + 1, h, "body")
                for h in range(HEADS + 4):
                    period(L, NBLK - 1, h, "final")

            def softmax_exps(tag, src):
                after(act, tag + ".shifted")
                act.activation(src, src, ACT.Exp).then_inc(stage(tag + ".exps"), 1)

            def experts(E, func, bias_cols, base):
                def round_of_experts(i):
                    for j in range(SLOTS):
                        for half in range(2):
                            act.wait_ge(hid_full, i * (2 * SLOTS) + ((base + j) * 2 + half + 1))
                            bank = (j % 2) * 2 + half
                            for t in range(4):
                                m = half * 4 + t
                                ins = act.activation(
                                    hT[:, j % 2, m, :], ps_s[:, bank * 512 + t * P:bank * 512 + (t + 1) * P], func,
                                    bias=bias_cols[:, bass.ds(i * (SLOTS * HT) + (j * HT + m), 1)])
                            ins.then_inc(hid_ready, 1)

                expert_rounds(act, E, round_of_experts)

            ln_root("x0")
            cross(L0)
            ln_root("la")
            softmax_exps("la.local", wide_a)
            softmax_exps("la.lat", lat_s)
            after(act, "la.gates")
            act.activation(gates[:, :], gates[:, :], ACT.Exp, scale=-1.0).then_inc(stage("la.gexp"), 1)
            ln_root("f0")
            after(act, "f0.top")
            act.activation(gate[:, 6, 0:8], gate[:, 5, 0:8], ACT.Exp).then_inc(stage("f0.exp"), 1)
            experts(8, ACT.Gelu, bin_cols, 0)
            ln_root("x1")
            ln_root("xm")
            after(act, "x1.qkT")
            act.activation(k_self, ps_s[:, 1024:2048].rearrange("p (t n) -> p t n", t=8),
                           ACT.Copy).then_inc(stage("x1.k_self"), 1)
            after(act, "x1.proj")
            act.activation(v_self[:, :], ps_o[:, :], ACT.Copy).then_inc(stage("x1.v_self"), 1)
            softmax_exps("x1.self", wide_a)
            cross(L1)
            ln_root("l1")
            after(act, "l1.abs")
            act.activation(sp_u, sp_a, ACT.Exp, scale=-1.0).then_inc(stage("l1.u"), 1)
            after(act, "l1.w")
            act.activation(sp_a, sp_w, ACT.Ln).then_inc(stage("l1.ln"), 1)
            ln_root("f1")
            after(act, "f1.top")
            act.activation(gate[:, 6, 0:16], gate[:, 5, 0:16], ACT.Exp).then_inc(stage("f1.exp"), 1)
            experts(16, ACT.Relu, b1_cols, 8)

        @block.vector
        def _(dve):
            count = [0]

            def link(ins):
                count[0] += 1
                ins.then_inc(dve_step, 1)
                dve.wait_ge(dve_step, count[0])

            def layernorm(tag, src, dst, eps=1e-5):
                link(dve.bn_stats(stats[:, :], src))
                link(dve.bn_aggr(meanvar[:, :], stats[:, :]))
                dve.tensor_scalar(sd[:, 1:2], meanvar[:, 1:2], eps, None, ALU.add).then_inc(stage(tag + ".var"), 1)
                after(dve, tag + ".sd")
                link(dve.reciprocal(sd[:, 1:2], sd[:, 0:1]))
                dve.tensor_scalar(dst, src, meanvar[:, 0:1], sd[:, 1:2], ALU.subtract,
                                  ALU.mult).then_inc(stage(tag + ".xn"), 1)

            def take(tag, dst, src):
                after(dve, tag)
                dve.tensor_copy(dst, src).then_inc(stage(tag + ".sb"), 1)

            def trailing(L, place, high, dst, lead, n, scale=1.0):
                bank, _ = place
                dve.wait_ge(L.high, high)
                src = RING[bank][:, 0:n]
                if len(dst.shape) == 3:
                    src = src.rearrange("p (h d) -> p h d", d=L.dv)
                dve.scalar_tensor_tensor(out=dst, in0=src, scalar=scale, in1=lead, op0=ALU.mult,
                                         op1=ALU.subtract).then_inc(L.ring_free[bank], 1)

            def context(L, places):
                for (_, c, r), at, high in places:
                    cut = slice(r * 512, BLK if r else 512)
                    trailing(L, at, high, ctxT[:, 1, c, cut], ctxT[:, 0, c, cut], 384 if r else 512)

            def naturals(L, half, tiles, at, high):
                for t in tiles:
                    g = ("natural", half, t)
                    trailing(L, at(g), high(g), natural_group(L, half, t, 1), natural_group(L, half, t, 0),
                             L.cols // 2, 1.0 / WSCALE)

            def keys(L, x, place):
                bank, seq = place
                dve.wait_ge(L.ring_full[bank], seq)
                dve.tensor_copy(kT[:, x % 4, :], RING[bank].bitcast(FP16)[:, 0:BLK]).then_inc(L.ring_free[bank], 1)

            def maximum(L, b, h, kind):
                n = h % 2
                dve.wait_ge(L.scores, b * HEADS + (h + 1))
                s = ps_s[:, 1024 * n:1024 * n + BLK]
                if L.masked:
                    if h >= 2 or kind != "first":
                        dve.wait_ge(L.probs, b * HEADS + (h - 1))
                    if h == 0:
                        dve.wait_ge(mask_ready, b + 1)
                    dve.memset(carrier[:, h:h + 1], 0.0)
                    dve.tensor_tensor_reduce(masked_s[:, n, :], s, mask_add[:, :], 1.0, negprev[:, h:h + 1], ALU.add,
                                             ALU.min, negcur[:, h:h + 1]).then_inc(L.negmax, 1)
                    return
                dve.tensor_reduce(blkmax[:, h:h + 1], s, AX.X, ALU.max).then_inc(L.blkmax, 1)
                dve.wait_ge(L.blkmax, b * HEADS + (h + 1))
                dve.scalar_tensor_tensor(out=negcur[:, h:h + 1], in0=blkmax[:, h:h + 1], scalar=-1.0,
                                         in1=negprev[:, h:h + 1], op0=ALU.mult, op1=ALU.min).then_inc(L.negmax, 1)

            def rescale(L, b, h):
                halves = b * 2 + h // 8
                q = (h // 8 + 1) % 2
                heads = slice(8 * q, 8 * q + 8)
                outputs = O[:, q * L.used // 2:(q + 1) * L.used // 2]
                dve.wait_ge(L.corr, halves)
                dve.wait_ge(L.probs, b * HEADS + h // 8 * 8)
                dve.tensor_copy(negprev[:, heads], negcur[:, heads])
                dve.tensor_tensor(den[:, heads], den[:, heads], by_row(L)[:, heads, 0], ALU.mult)\
                   .then_inc(L.scaled, 1)
                bank, seq = L.at(b, ("factors", h // 8 - 1))
                dve.wait_ge(L.ring_full[bank], seq)
                dve.tensor_tensor(outputs, outputs, RING[bank][:, 0:L.used // 2], ALU.mult)\
                   .then_inc(L.ring_free[bank], 1)
                dve.wait_ge(L.scaled, halves)
                dve.tensor_tensor(den[:, heads], den[:, heads], rowsum[:, heads], ALU.add).then_inc(L.sums, 1)

            def period(L, b, h, kind):
                groups = L.period(h, kind)
                halves = b * 2 + h // 8
                last_half = not (kind == "first" and h < 8)
                q = (h // 8 + 1) % 2
                heads = slice(8 * q, 8 * q + 8)
                outputs = O[:, q * L.used // 2:(q + 1) * L.used // 2]
                for g in groups:
                    if g[0] == "keys" and g[1] % 2 == 1:
                        keys(L, g[1], L.at(b, g))
                if h < HEADS:
                    maximum(L, b, h, kind)
                if h % 8 == 0 and last_half:
                    dve.wait_ge(L.negmax, b * HEADS + h)
                    dve.tensor_tensor(shift[:, heads], negcur[:, heads], negprev[:, heads],
                                      ALU.subtract).then_inc(L.shift, 1)
                for g in groups:
                    if g[0] == "probs":
                        _, k, r = g
                        cut = slice(r * 512, BLK if r else 512)
                        trailing(L, L.at(b, g), L.high_at(b, g), probsT[:, k % L.slots, 1, cut],
                                 probsT[:, k % L.slots, 0, cut], 384 if r else 512)
                    if g[0] == "factors":
                        rescale(L, b, h)
                    if g[0] == "natural":
                        naturals(L, g[1], (g[2],), lambda g: L.at(b, g), lambda g: L.high_at(b, g))
                if h % 8 == 3 and last_half:
                    bank, seq = L.at(b, ("factors", h // 8 - 1))
                    dve.wait_ge(L.ring_free[bank], seq)
                    dve.wait_ge(L.sums, halves)
                    dve.wait_ge(L.pv, halves)
                    start = q * L.used // 2 % 512
                    dve.tensor_tensor(outputs, outputs, ps_o[:, start:start + L.used // 2], ALU.add)\
                       .then_inc(L.acc, 1)
                    dve.wait_ge(L.acc, halves)
                context(L, [(g, L.at(b, g), L.high_at(b, g)) for g in groups if g[0] == "context"])

            def cross(L):
                context(L, [(g, L.at_first(g), i + 1) for i, g in enumerate(L.context_groups())])
                naturals(L, 0, range(TILES), L.at_first, lambda g: L.before.index(g) + 1)
                if L is L1:
                    keys(L, 1, L.at_first(("keys", 1)))
                for h in range(HEADS):
                    period(L, 0, h, "first")
                with dve.Fori(0, NBLK - 2) as i:
                    for h in range(HEADS):
                        period(L, i + 1, h, "body")
                for h in range(HEADS + 4):
                    period(L, NBLK - 1, h, "final")

            def split_weights(parts):
                for src, lo, n in parts:
                    link(dve.tensor_scalar(w16[:, :, 0, lo:lo + n], src, WSCALE, None, ALU.mult))
                    ins = dve.scalar_tensor_tensor(out=w16[:, :, 1, lo:lo + n], in0=src, scalar=WSCALE,
                                                   in1=w16[:, :, 0, lo:lo + n], op0=ALU.mult, op1=ALU.subtract)
                return ins

            def divide(L, tag):
                used = L.used
                link(dve.reciprocal(den[:, :], den[:, :]))
                dve.tensor_copy(by_row(L), den[:, :].unsqueeze(2).broadcast_to([P, HEADS, L.width]))\
                   .then_inc(stage(tag + ".rden"), 1)
                after(dve, tag + ".rden_rows")
                return dve.tensor_tensor(O[:, 0:used], O[:, 0:used], ps_s[:, 0:used], ALU.mult)

            def head_queries(src, e, dst):
                return dve.tensor_tensor(dst, src.unsqueeze(1).broadcast_to([P, 8, P]),
                                         headmask[:, :].unsqueeze(2).broadcast_to([P, 8, P]), ALU.mult)

            def softmax_head(tag, s, heads, keys, negmax, sums):
                s3 = s.rearrange("p (h k) -> p h k", h=heads)
                link(dve.tensor_reduce(negmax, s3, AX.X, ALU.max, negate=True))
                dve.tensor_tensor(s3, s3, negmax.unsqueeze(2).broadcast_to([P, heads, keys]),
                                  ALU.add).then_inc(stage(tag + ".shifted"), 1)
                after(dve, tag + ".exps")
                link(dve.tensor_reduce(sums, s3, AX.X, ALU.add))

            def route(tag, E, logits, rev, renormalise):
                g = [gate[:, i, 0:E] for i in range(8)]
                m = gatecol
                link(dve.tensor_reduce(m[:, 0:1], logits, AX.X, ALU.max))
                dve.tensor_scalar(g[5], logits, m[:, 0:1], None, ALU.subtract).then_inc(stage(tag + ".top"), 1)
                after(dve, tag + ".exp")
                if renormalise:
                    score = logits
                else:
                    link(dve.tensor_reduce(m[:, 1:2], g[6], AX.X, ALU.add))
                    link(dve.reciprocal(m[:, 2:3], m[:, 1:2]))
                    link(dve.tensor_scalar(g[6], g[6], m[:, 2:3], None, ALU.mult))
                    score = g[6]
                    link(dve.tensor_reduce(m[:, 0:1], score, AX.X, ALU.max))
                link(dve.scalar_tensor_tensor(out=g[0], in0=score, scalar=m[:, 0:1], in1=rev[:, :],
                                              op0=ALU.is_equal, op1=ALU.mult))
                link(dve.tensor_reduce(m[:, 3:4], g[0], AX.X, ALU.max))
                link(dve.tensor_scalar(g[1], g[0], m[:, 3:4], None, ALU.is_equal))
                link(dve.scalar_tensor_tensor(out=g[2], in0=g[1], scalar=-HUGE, in1=score,
                                              op0=ALU.mult, op1=ALU.add))
                link(dve.tensor_reduce(m[:, 4:5], g[2], AX.X, ALU.max))
                link(dve.scalar_tensor_tensor(out=g[0], in0=g[2], scalar=m[:, 4:5], in1=rev[:, :],
                                              op0=ALU.is_equal, op1=ALU.mult))
                link(dve.tensor_reduce(m[:, 5:6], g[0], AX.X, ALU.max))
                link(dve.tensor_scalar(g[3], g[0], m[:, 5:6], None, ALU.is_equal))
                link(dve.tensor_tensor(g[1], g[1], g[3], ALU.add))
                if renormalise:
                    link(dve.tensor_tensor(g[2], g[1], g[6], ALU.mult))
                    link(dve.tensor_reduce(m[:, 1:2], g[2], AX.X, ALU.add))
                    link(dve.reciprocal(m[:, 2:3], m[:, 1:2]))
                    dve.tensor_scalar(comb[:, 0:E], g[2], m[:, 2:3], None, ALU.mult).then_inc(stage(tag + ".comb"), 1)
                else:
                    dve.tensor_tensor(comb[:, 0:E], g[1], g[6], ALU.mult).then_inc(stage(tag + ".comb"), 1)

            def experts(tag, E, base):
                take(tag + ".combT", combT[0:E, :], ps_o[0:E, 0:P])
                after(dve, tag + ".bias_ps")
                dve.tensor_tensor(X[:, :], X[:, :], ps_o[:, 512:512 + D], ALU.add).then_inc(stage(tag + ".bias_used"), 1)
                after(dve, tag + ".bias_used")
                if base == 0:
                    arrived(dve, "x1big")
                    split_weights([(wm1, 0, 1024)]).then_inc(stage("x1.w16"), 1)

                def round_of_experts(i):
                    for j in range(SLOTS):
                        e = i * SLOTS + (base + j)
                        dve.wait_ge(y_full, e + 1)
                        dve.scalar_tensor_tensor(out=X[:, :], in0=ps_o[:, (j % 2) * 512:(j % 2) * 512 + D],
                                                 scalar=comb[:, bass.ds(i * SLOTS + j, 1)], in1=X[:, :],
                                                 op0=ALU.mult, op1=ALU.add).then_inc(y_added, 1)
                        dve.wait_ge(y_added, e + 1)

                expert_rounds(dve, E, round_of_experts)

            def add_projection(tag, src, bias_row=None):
                after(dve, tag)
                if bias_row is not None:
                    link(dve.tensor_tensor(X[:, :], X[:, :], rows[:, bias_row, :], ALU.add))
                link(dve.tensor_tensor(X[:, :], X[:, :], src, ALU.add))

            arrived(dve, "x")
            layernorm("x0", X[:, :], xn[:, :])
            take("x0.xT", xT[:, :, :], ps_ring[:, 0:D].rearrange("p (c n) -> p c n", c=DC))
            arrived(dve, "x0")
            after(dve, "x0.q")
            split_weights([(w[:, :, q * P:(q + 1) * P], q * D + v * P, P)
                           for q in range(2) for v, w in enumerate((wk0, wv0))]).then_inc(stage("x0.w16"), 1)
            after(dve, "ident")
            link(dve.tensor_scalar(bk16[:, :], bkf[:, 0:D], WSCALE, None, ALU.mult))
            link(dve.scalar_tensor_tensor(out=bkf[:, D:2 * D], in0=bkf[:, 0:D], scalar=WSCALE, in1=bk16[:, :],
                                          op0=ALU.mult, op1=ALU.subtract))
            link(dve.tensor_scalar(bkf[:, 2 * D:3 * D], bk16[:, :], ident[0:2, 0:1], None, ALU.mult))
            dve.scalar_tensor_tensor(out=bk16[:, :], in0=bkf[:, D:2 * D], scalar=ident[0:2, 1:2],
                                     in1=bkf[:, 2 * D:3 * D], op0=ALU.mult, op1=ALU.add).then_inc(stage("x0.bk"), 1)
            link(dve.tensor_tensor(qn[:, 0:D], ps_o[:, 0:D], rows[:, BQ0, :], ALU.add))
            link(dve.tensor_scalar(qn[:, 0:D], qn[:, 0:D], -0.25, None, ALU.mult))
            link(dve.tensor_copy(qhi[:, 0:D], qn[:, 0:D]))
            link(dve.tensor_tensor(qlo[:, 0:D], qn[:, 0:D], qhi[:, 0:D], ALU.subtract))
            link(dve.memset(qx[:, 0:2048], 0.0))
            view = qx[:, 0:2048].rearrange("p (pair s copy s2 part d) -> p pair s copy s2 part d",
                                           pair=8, s=2, copy=2, s2=2, part=2)
            for i, part_of_q in enumerate((qhi, qlo)):
                q4 = part_of_q[:, 0:D].rearrange("p (pair s d) -> p pair s d", pair=8, s=2)
                for s_ in range(2):
                    for part in range(2):
                        ins = dve.tensor_copy(view[:, :, s_, i, s_, part, :], q4[:, :, s_, :])
            link(ins)
            dve.memset(O[:, :], 0.0).then_inc(stage("x0.qx"), 1)
            after(dve, "x0.qxT")
            dve.tensor_copy(q16[:, :, 0, :], ps_s16[:, 0:2048].rearrange("p (h q) -> p h q", h=HEADS))\
               .then_inc(stage("x0.q16"), 1)
            link(dve.memset(den[:, :], 0.0))
            link(dve.memset(negprev[:, :], HUGE))
            cross(L0)
            link(divide(L0, "x0"))
            arrived(dve, "x0b")
            after(dve, "bvcol")
            dve.tensor_tensor(O[:, 0:512].rearrange("p (g q) -> p g q", g=4), O[:, 0:512].rearrange("p (g q) -> p g q", g=4),
                              bvcol[:, :].unsqueeze(2).broadcast_to([P, 4, P]), ALU.add).then_inc(stage("x0.done"), 1)
            add_projection("x0.out", ps_o[:, 0:D], BO0)

            layernorm("la", X[:, :], xn[:, :])
            after(dve, "la.xT")
            link(dve.tensor_copy(xT[:, :, :], ps_ring[:, 0:D].rearrange("p (c n) -> p c n", c=DC)))
            pair = xT[:, :, :].rearrange("p c (n two) -> p c n two", two=2)
            link(dve.tensor_tensor(xpool, pair[:, :, :, 0], pair[:, :, :, 1], ALU.add))
            dve.tensor_scalar(xpool, xpool, 0.5, None, ALU.mult).then_inc(stage("la.xT.sb"), 1)
            after(dve, "la.proj")
            link(dve.tensor_scalar(qT[:, 0:2, :], ps_s[:, 0:D].rearrange("p (c n) -> p c n", c=2), 0.25, None, ALU.mult))
            link(dve.tensor_copy(qT[:, 2:4, :], ps_s[:, D:2 * D].rearrange("p (c n) -> p c n", c=2)))
            link(dve.tensor_copy(v_nat, ps_s[:, 512:512 + D]))
            link(dve.tensor_copy(q_nat, ps_s[:, 512 + D:1024]))
            link(dve.tensor_scalar(qT[:, 4, :], ps_s[:, 1024:1024 + P], 0.25, None, ALU.mult))
            link(dve.tensor_copy(qT[:, 5, 0:64], ps_s[:, 1024 + P:1024 + P + 64]))
            link(dve.tensor_copy(gv_nat, ps_s[0:64, 1536:1536 + P]))
            after(dve, "headmask")
            link(head_queries(qT[:, 2, :], 0, kz[:, 0, :, :]))
            link(head_queries(qT[:, 3, :], 1, kz[:, 1, :, :]))
            dve.tensor_tensor(gkz, qT[:, 5, 0:64].unsqueeze(1).broadcast_to([P, 8, 64]),
                              headmask[:, :].unsqueeze(2).broadcast_to([P, 8, 64]), ALU.mult).then_inc(stage("la.kz"), 1)
            after(dve, "consts")
            after(dve, "la.scores")
            link(dve.tensor_tensor(wide_a.rearrange("p (h k) -> p h k", h=HEADS),
                                   ps_s[:, :].rearrange("p (h k) -> p h k", h=HEADS),
                                   window[:, :].unsqueeze(1).broadcast_to([P, HEADS, P]), ALU.add))
            link(dve.tensor_tensor(lat_s.rearrange("p (h k) -> p h k", h=8),
                                   ps_ring[:, 0:512].rearrange("p (h k) -> p h k", h=8),
                                   latmask[:, :].unsqueeze(1).broadcast_to([P, 8, 64]), ALU.add))
            softmax_head("la.local", wide_a, HEADS, P, negprev[:, :], den[:, :])
            softmax_head("la.lat", lat_s, 8, 64, negcur[:, 0:8], rowsum[:, 0:8])
            arrived(dve, "la")
            for i, r in ((0, GL), (1, GR)):
                link(dve.tensor_tensor(xn[:, :], q_nat, rows[:, r, :], ALU.mult))
                link(dve.tensor_reduce(gates[:, 16 * i:16 * i + 16], xn[:, :].rearrange("p (h d) -> p h d", h=HEADS),
                                       AX.X, ALU.add))
            dve.tensor_scalar(gates[:, :], gates[:, :], 1.0, None, ALU.mult).then_inc(stage("la.gates"), 1)
            after(dve, "la.gexp")
            link(dve.tensor_scalar(gates[:, :], gates[:, :], 1.0, None, ALU.add))
            link(dve.reciprocal(gates[:, :], gates[:, :]))
            link(dve.reciprocal(den[:, :], den[:, :]))
            link(dve.reciprocal(rowsum[:, 0:8], rowsum[:, 0:8]))
            link(dve.tensor_tensor(gates[:, 0:16], gates[:, 0:16], den[:, :], ALU.mult))
            take("la.turned", wide_b, ps_s[:, :])
            after(dve, "la.pv")
            link(dve.tensor_tensor(attn.rearrange("p (h d) -> p h d", h=HEADS),
                                   ps_o[:, 0:D].rearrange("p (h d) -> p h d", h=HEADS),
                                   gates[:, 0:16].unsqueeze(2).broadcast_to([P, HEADS, 16]), ALU.mult))
            take("la.lturned", wide_a[0:64, 0:1024], ps_s[0:64, 0:1024])
            after(dve, "la.lpv")
            dve.tensor_tensor(rem.rearrange("p (h d) -> p h d", h=8),
                              ps_o[:, 512:512 + P].rearrange("p (h d) -> p h d", h=8),
                              rowsum[:, 0:8].unsqueeze(2).broadcast_to([P, 8, 16]), ALU.mult).then_inc(stage("la.rem"), 1)
            take("la.remT", qT[:, 0, :], ps_ring[:, 0:P])
            after(dve, "la.rproj")
            link(dve.tensor_tensor(xn[:, :].rearrange("p (h d) -> p h d", h=HEADS),
                                   ps_ring[:, 512:512 + D].rearrange("p (h d) -> p h d", h=HEADS),
                                   gates[:, 16:32].unsqueeze(2).broadcast_to([P, HEADS, 16]), ALU.mult))
            dve.tensor_tensor(xn[:, :], xn[:, :], attn, ALU.add).then_inc(stage("la.attn"), 1)
            take("la.attnT", xT[:, :, :], ps_ring[:, 0:D].rearrange("p (c n) -> p c n", c=DC))
            add_projection("la.out_ps", ps_o[:, 0:D])

            layernorm("f0", X[:, :], xn[:, :])
            take("f0.xT", xT[:, :, :], ps_ring[:, 0:D].rearrange("p (c n) -> p c n", c=DC))
            take("f0.bias", bin_cols[:, :], ps_ring[:, 512:512 + 8 * HT])
            after(dve, "f0.logits")
            link(dve.tensor_copy(gate[:, 4, 0:8], ps_o[:, 0:8]))
            route("f0", 8, gate[:, 4, 0:8], rev8, True)
            experts("f0", 8, 0)

            layernorm("x1", X[:, :], xn[:, :])
            after(dve, "x1.xn")
            layernorm("xm", xn[:, :], xm[:, :])
            arrived(dve, "x1")
            after(dve, "xm.xn")
            link(dve.tensor_tensor(xm[:, :], xm[:, :], rows[:, LNG, :], ALU.mult))
            dve.tensor_tensor(xm[:, :], xm[:, :], rows[:, LNB, :], ALU.add).then_inc(stage("xm.affine"), 1)
            take("xm.xT", xT[:, :, :], ps_ring[:, 0:D].rearrange("p (c n) -> p c n", c=DC))
            arrived(dve, "x1big")
            after(dve, "x1.qkT")
            dve.tensor_scalar(qT[:, :, :], ps_s[:, 0:1024].rearrange("p (t n) -> p t n", t=8), 0.125, None,
                              ALU.mult).then_inc(stage("x1.qT"), 1)
            after(dve, "x1.proj")
            link(dve.tensor_scalar(qn, ps_ring[:, :], 0.125, None, ALU.mult))
            link(dve.tensor_copy(qhi, qn))
            link(dve.tensor_tensor(qlo, qn, qhi, ALU.subtract))
            after(dve, "x1.self_scores")
            link(dve.tensor_copy(wide_a.rearrange("p (t c k) -> p c t k", t=8, c=2),
                                 ps_s[:, :].rearrange("p (c t k) -> p c t k", t=8, c=2)))
            softmax_head("x1.self", wide_a, HEADS, P, negprev[:, :], den[:, :])
            view = qx.rearrange("p (h turn half d) -> p h turn half d", h=HEADS, turn=2, half=2)
            for i, part_of_q in enumerate((qhi, qlo)):
                for half in range(2):
                    ins = dve.tensor_copy(view[:, :, i, half, :], part_of_q.rearrange("p (h d) -> p h d", h=HEADS))
            ins.then_inc(stage("x1.qx"), 1)
            take("x1.turned", wide_b, ps_s[:, :])
            after(dve, "x1.self_pv")
            dve.tensor_copy(O[:, :], ps_o[:, :]).then_inc(stage("x1.start"), 1)
            after(dve, "x1.qxT")
            dve.tensor_copy(q16[:, :, :, :].rearrange("p h t q -> p (h t q)"), ps_s16[:, :]).then_inc(stage("x1.q16"), 1)
            after(dve, "x1.start")
            cross(L1)
            divide(L1, "x1").then_inc(stage("x1.done"), 1)
            add_projection("x1.out", ps_o[:, 0:D], BO1)

            layernorm("l1", X[:, :], xn[:, :])
            take("l1.wT", wide_b, ps_s[:, :])
            take("l1.xT", xT[:, :, :], ps_ring[:, 0:D].rearrange("p (c n) -> p c n", c=DC))
            after(dve, "l1.proj")
            link(dve.tensor_copy(sp_z, ps_s[:, 0:512]))
            link(dve.memset(v_ext, 1.0))
            link(dve.tensor_copy(v_ext[:, :, 0:16], ps_s[:, 512:512 + D].rearrange("p (h d) -> p h d", h=HEADS)))
            link(dve.tensor_scalar(sp_w, sp_z, -1.0, None, ALU.mult))
            dve.tensor_tensor(sp_a, sp_z, sp_w, ALU.max).then_inc(stage("l1.abs"), 1)
            after(dve, "l1.u")
            dve.tensor_scalar(sp_w, sp_u, 1.0, None, ALU.add).then_inc(stage("l1.w"), 1)
            after(dve, "l1.w")
            link(dve.scalar_tensor_tensor(out=sp_u, in0=sp_w, scalar=-1.0, in1=sp_u, op0=ALU.add, op1=ALU.subtract))
            after(dve, "l1.ln")
            link(dve.reciprocal(sp_w, sp_w))
            link(dve.tensor_tensor(sp_u, sp_u, sp_w, ALU.mult))
            link(dve.tensor_tensor(sp_a, sp_a, sp_u, ALU.subtract))
            link(dve.tensor_scalar(sp_z, sp_z, 0.0, None, ALU.max))
            link(dve.tensor_tensor(sp_z, sp_z, sp_a, ALU.add))
            link(dve.tensor_scalar(sp_z, sp_z, 1e-6, None, ALU.add))
            link(head_queries(sp_z[:, 0:P], 0, kz[:, 0, :, :]))
            head_queries(sp_z[:, P:2 * P], 1, kz[:, 1, :, :]).then_inc(stage("l1.qz"), 1)
            after(dve, "l1.scores")
            dve.tensor_tensor(wide_a.rearrange("p (h k) -> p h k", h=HEADS),
                              ps_s[:, :].rearrange("p (h k) -> p h k", h=HEADS),
                              causal[:, :].unsqueeze(1).broadcast_to([P, HEADS, P]), ALU.mult).then_inc(stage("l1.causal"), 1)
            after(dve, "l1.pv")
            pv = ps_o[:, 0:HEADS * 17].rearrange("p (h d) -> p h d", h=HEADS)
            link(dve.tensor_scalar(den[:, :], pv[:, :, 16], 1e-6, None, ALU.add))
            link(dve.reciprocal(den[:, :], den[:, :]))
            dve.tensor_tensor(xn[:, :].rearrange("p (h d) -> p h d", h=HEADS), pv[:, :, 0:16],
                              den[:, :].unsqueeze(2).broadcast_to([P, HEADS, 16]), ALU.mult).then_inc(stage("l1.attn"), 1)
            take("l1.attnT", xT[:, :, :], ps_ring[:, 0:D].rearrange("p (c n) -> p c n", c=DC))
            add_projection("l1.out", ps_o[:, 512:512 + D])

            layernorm("f1", X[:, :], xn[:, :])
            take("f1.xT", xT[:, :, :], ps_ring[:, 0:D].rearrange("p (c n) -> p c n", c=DC))
            take("f1.bias", b1_cols[:, :], ps_ring[:, 512:512 + P])
            after(dve, "f1.logits")
            arrived(dve, "f1")
            link(dve.tensor_tensor(gate[:, 4, 0:16], ps_o[:, 0:16], br1[:, :], ALU.add))
            route("f1", 16, gate[:, 4, 0:16], rev16, False)
            experts("f1", 16, 8)
            dve.tensor_copy(gate[:, 0, 0:1], X[:, 0:1]).then_inc(stage("f1.done"), 1)

        @block.tensor
        def _(pe):
            def turn(src, dst, n):
                for t in range(n):
                    ins = pe.transpose(dst[:, t * P:(t + 1) * P], src[:, t * P:(t + 1) * P], ident[:, :])
                return ins

            def project(dst, lhs, rhs, chunks=DC):
                for c in range(chunks):
                    ins = pe.matmul(dst, lhs(c), rhs(c), start=c == 0, stop=c == chunks - 1)
                return ins

            def turn_norm(tag, ready, src):
                after(pe, ready)
                turn(src, ps_ring[:, 0:D], DC).then_inc(stage(tag), 1)

            RANGES = ((0, SPLIT), (SPLIT, TILES))

            def claim(L, place):
                bank, seq = place
                if not (isinstance(seq, int) and seq == 1):
                    pe.wait_ge(L.ring_free[bank], seq - 1)
                return RING[bank]

            def filled(L, place, ins):
                ins.then_inc(L.ring_full[place[0]], 1)

            def out_of_ring(L, places):
                for bank, seq in places:
                    pe.wait_ge(L.ring_free[bank], seq)

            def context(L, g, at):
                _, c, r = g
                dst = claim(L, at)
                t0, t1 = RANGES[r]
                for t in range(t0, t1):
                    ins = pe.transpose(dst[:, (t - t0) * P:(t - t0 + 1) * P], ctx_nat[:, t, c * P:(c + 1) * P],
                                       ident[:, :])
                filled(L, at, ins)

            def project_keys(L, half, t, at):
                w = L.cols // 2
                dst = claim(L, at)[:, 0:w]
                bias = L is L0
                passes = [(c, x, y) for c in range(DC) for x, y in ((0, 0), (0, 1), (1, 0))]
                for i, (c, x, y) in enumerate(passes):
                    ins = pe.matmul(dst, ctxT[:, x, c, t * P:(t + 1) * P], w16[:, c, y, half * w:(half + 1) * w],
                                    start=i == 0, stop=i == len(passes) - 1 and not bias)
                if bias:
                    ins = pe.matmul(dst[:, 0:P], ones16[:, :], bk16[:, half * P:(half + 1) * P], start=False, stop=True)
                filled(L, at, ins)

            def turn_keys(L, x, at, block):
                dst = claim(L, at).bitcast(FP16)
                if x * L.heads_per_turn % 8 == 0:
                    half = x * L.heads_per_turn // 8
                    tiles = L.last_in_banks([("natural", half, t) for t in range(TILES)])
                    out_of_ring(L, [block(g) for g in tiles if L.banks[g] != at[0]])
                if L is L0:
                    first_col = x // 4 * 512 + x % 4 * 64
                    pe.transpose(dst[:, 0:P], vals[:, first_col:first_col + P], ident16[:, :])
                else:
                    first_col = x * P
                for t in range(TILES):
                    o = t * 2 * L.cols + first_col
                    if L is L0:
                        for copy in range(2):
                            ins = pe.transpose(dst[64 * copy:64 * copy + 64, t * P:(t + 1) * P], vals[:, o:o + 64],
                                               ident16[:, :])
                    else:
                        ins = pe.transpose(dst[:, t * P:(t + 1) * P], vals[:, o:o + P], ident16[:, :])
                filled(L, at, ins)

            def scores(L, b, h, kind):
                n = h % 2
                x = h // L.heads_per_turn
                if h >= 2:
                    if h % L.heads_per_turn == 0:
                        out_of_ring(L, [L.at(b, ("keys", x))])
                elif kind == "first":
                    out_of_ring(L, [L.at_first(("keys", x))])
                else:
                    out_of_ring(L, [L.at(b - 1, ("keys", x))])
                if h >= 2 or kind != "first":
                    pe.wait_ge(L.negmax if L.masked else L.probs, b * HEADS + (h - 1))
                passes = 1 if L is L0 else 2
                for t0, t1 in RANGES:
                    for i in range(passes):
                        ins = pe.matmul(ps_s[:, 1024 * n + t0 * P:1024 * n + t1 * P], q16[:, h, i, :],
                                        kT[:, x % 4, t0 * P:t1 * P], start=i == 0, stop=i == passes - 1)
                ins.then_inc(L.scores, 1)

            def weighted(L, b, h, g):
                if h > 0:
                    out_of_ring(L, [L.at(b, ("probs", h - 3, r)) for r in range(2)])
                else:
                    out_of_ring(L, [L.at(b - 1, ("probs", HEADS - 3, r)) for r in range(2)])
                groups = HEADS // L.together
                in_half = g % (groups // 2)
                halves = b * 2 + (h - L.together - 2) // 8
                if in_half == 0 and not (isinstance(halves, int) and halves == 0):
                    pe.wait_ge(L.acc, halves)
                both = slice(0, 2)
                passes = ((both, 0), (both, 1)) if L is L0 else ((slice(0, 1), 0), (slice(0, 1), 1), (slice(1, 2), 0))
                start = g % groups * P % 512
                for t in range(TILES):
                    for i, (v, p) in enumerate(passes):
                        for k in range(L.together):
                            head = (g * L.together + k) % HEADS
                            ins = pe.matmul(ps_o[k * L.width:(k + 1) * L.width, start:start + P],
                                            stationary(L, t, head, v),
                                            probsT[:, head % L.slots, p, t * P:(t + 1) * P],
                                            start=t == 0 and i == 0,
                                            stop=t == TILES - 1 and i == len(passes) - 1)
                if in_half == groups // 2 - 1:
                    ins.then_inc(L.pv, 1)

            def period(L, b, h, kind):
                groups = L.period(h, kind)
                last_half = not (kind == "first" and h < 8)
                if h < HEADS:
                    scores(L, b, h, kind)
                group = L.weighted_at(h)
                if kind == "first" and group is not None and group < 0:
                    group = None
                for g in groups:
                    at = L.at(b, g)
                    if g[0] == "keys":
                        turn_keys(L, g[1], at, lambda g: L.at(b, g))
                    if g[0] == "probs":
                        _, k, r = g
                        t0, t1 = RANGES[r]
                        if r == 0:
                            pe.wait_ge(L.probs, b * HEADS + (h - 1))
                        filled(L, at, turn(probs[:, k % 2, t0 * P:t1 * P], claim(L, at), t1 - t0))
                    if g[0] == "factors":
                        half_groups = HEADS // L.together // 2
                        q = (h // 8 + 1) % 2
                        pe.wait_ge(L.corr, b * 2 + h // 8)
                        filled(L, at, per_row(range(q * half_groups, (q + 1) * half_groups), claim(L, at)))
                        weighted(L, b, h, group)
                    if g[0] == "natural":
                        if g[1:] == (0, 0):
                            out_of_ring(L, [L.at(b, c) for c in L.last_in_banks(L.context_groups())
                                            if L.banks[c] != L.banks[g]])
                        project_keys(L, g[1], g[2], at)
                    if g[0] == "context":
                        if g[1:] == (0, 0):
                            pe.wait_ge(L.ctx_in, b * 16 + 32)
                        context(L, g, at)
                if group is not None and h % 8 != 2:
                    weighted(L, b, h, group)

            def per_row(groups, dst):
                for i, g in enumerate(groups):
                    ins = pe.transpose(dst[:, i * P:(i + 1) * P], factors[:, g * P:(g + 1) * P], ident[:, :])
                return ins

            def cross(L):
                pe.wait_ge(L.ctx_in, 16)
                for g in L.context_groups():
                    context(L, g, L.at_first(g))
                out_of_ring(L, [L.at_first(c) for c in L.last_in_banks(L.context_groups())])
                for t in range(TILES):
                    project_keys(L, 0, t, L.at_first(("natural", 0, t)))
                for x in L.keys_at(-1):
                    turn_keys(L, x, L.at_first(("keys", x)), L.at_first)
                for h in range(HEADS):
                    period(L, 0, h, "first")
                with pe.Fori(0, NBLK - 2) as i:
                    for h in range(HEADS):
                        period(L, i + 1, h, "body")
                for h in range(HEADS + 4):
                    period(L, NBLK - 1, h, "final")

            def experts(tag, E, base):
                after(pe, tag + ".comb")
                pe.transpose(ps_o[0:E, 0:P], comb[:, 0:E], ident[:, :]).then_inc(stage(tag + ".combT"), 1)
                after(pe, tag + ".combT.sb")
                b_out = bout0 if base == 0 else b2_1
                pe.matmul(ps_o[:, 512:512 + D], combT[0:E, :], b_out[0:E, :], start=True,
                          stop=True).then_inc(stage(tag + ".bias_ps"), 1)
                after(pe, tag + ".bias.sb")
                after(pe, tag + ".bias_used")

                def round_of_experts(i):
                    for j in range(SLOTS):
                        e = i * SLOTS + (base + j)
                        fresh = isinstance(e, int) and e < 2
                        pe.wait_ge(expert_in[j], (i + (base // SLOTS + 1)) * 32)
                        for half in range(2):
                            if not fresh:
                                pe.wait_ge(hid_ready, e * 2 + (half - 3))
                            for t in range(4):
                                m = half * 4 + t
                                col = ((j % 2) * 2 + half) * 512 + t * P
                                ins = project(ps_s[:, col:col + P], lambda c: win[:, j, c, m * P:(m + 1) * P],
                                              lambda c: xT[:, c, :])
                            ins.then_inc(hid_full, 1)
                        if not fresh:
                            pe.wait_ge(y_added, e - 1)
                        for half in range(2):
                            pe.wait_ge(hid_ready, e * 2 + (half + 1))
                            for t in range(4):
                                m = half * 4 + t
                                ins = pe.matmul(ps_o[:, (j % 2) * 512:(j % 2) * 512 + D], hT[:, j % 2, m, :],
                                                wout[:, j, m, :], start=m == 0, stop=m == HT - 1)
                        ins.then_inc(y_full, 1)

                expert_rounds(pe, E, round_of_experts)

            after(pe, "ident")
            turn_norm("x0.xT", "x0.xn", xn)
            arrived(pe, "x0")
            after(pe, "x0.xT.sb")
            project(ps_o[:, 0:D], lambda c: xT[:, c, :], lambda c: wq0[:, c, :]).then_inc(stage("x0.q"), 1)
            after(pe, "x0.qx")
            after(pe, "ident16")
            for h in range(HEADS):
                ins = pe.transpose(ps_s16[:, h * P:(h + 1) * P], qx[:, h * P:(h + 1) * P], ident16[:, :])
            ins.then_inc(stage("x0.qxT"), 1)
            after(pe, "x0.q16")
            after(pe, "x0.w16")
            after(pe, "x0.bk")
            after(pe, "ones16")
            cross(L0)
            after(pe, "x0.rden")
            per_row(range(4), ps_s).then_inc(stage("x0.rden_rows"), 1)
            arrived(pe, "x0b")
            after(pe, "x0.done")
            project(ps_o[:, 0:D], lambda g: O[:, g * P:(g + 1) * P], lambda g: wox[:, g, :],
                    4).then_inc(stage("x0.out"), 1)

            turn_norm("la.xT", "la.xn", xn)
            arrived(pe, "la")
            after(pe, "la.xT.sb")
            for e in range(DC):
                cut = slice(e * P, (e + 1) * P)
                project(ps_s[:, e * P:(e + 1) * P], lambda c: la_wq[:, c, cut], lambda c: xT[:, c, :])
                project(ps_s[:, D + e * P:D + (e + 1) * P], lambda c: la_wk[:, c, cut], lambda c: xT[:, c, :])
            project(ps_s[:, 512:512 + D], lambda c: xT[:, c, :], lambda c: la_wv[:, c, :])
            project(ps_s[:, 512 + D:1024], lambda c: xT[:, c, :], lambda c: la_wq[:, c, :])
            project(ps_s[:, 1024:1024 + P], lambda c: la_wgq[:, c, :], lambda c: xT[:, c, :])
            project(ps_s[:, 1024 + P:1024 + P + 64], lambda c: la_wgk[:, c, :], lambda c: xpool[:, c, :])
            project(ps_s[0:64, 1536:1536 + P], lambda c: xpool[:, c, :],
                    lambda c: la_wgv[:, c, :]).then_inc(stage("la.proj"), 1)
            after(pe, "la.kz")
            for g in range(4):
                pe.matmul(ps_s[:, g * 512:(g + 1) * 512], qT[:, g // 2, :], kflat[:, g * 512:(g + 1) * 512],
                          start=True, stop=True)
            pe.matmul(ps_ring[:, 0:512], qT[:, 4, :], kflat[:, 2048:2560], start=True,
                      stop=True).then_inc(stage("la.scores"), 1)
            after(pe, "la.local.exps")
            turn(wide_a, ps_s, HEADS).then_inc(stage("la.turned"), 1)
            after(pe, "la.turned.sb")
            for h in range(HEADS):
                ins = pe.matmul(ps_o[:, h * 16:(h + 1) * 16], wide_b[:, h * P:(h + 1) * P],
                                v_nat[:, h * 16:(h + 1) * 16], start=True, stop=True)
            ins.then_inc(stage("la.pv"), 1)
            after(pe, "la.lat.exps")
            for h in range(8):
                ins = pe.transpose(ps_s[0:64, h * P:(h + 1) * P], lat_s[:, h * 64:(h + 1) * 64], ident[:, :])
            ins.then_inc(stage("la.lturned"), 1)
            after(pe, "la.lturned.sb")
            for h in range(8):
                ins = pe.matmul(ps_o[:, 512 + h * 16:512 + (h + 1) * 16], wide_a[0:64, h * P:(h + 1) * P],
                                gv_nat[:, h * 16:(h + 1) * 16], start=True, stop=True)
            ins.then_inc(stage("la.lpv"), 1)
            after(pe, "la.rem")
            turn(rem, ps_ring[:, 0:P], 1).then_inc(stage("la.remT"), 1)
            after(pe, "la.remT.sb")
            pe.matmul(ps_ring[:, 512:512 + D], qT[:, 0, :], la_rout[:, :], start=True,
                      stop=True).then_inc(stage("la.rproj"), 1)
            turn_norm("la.attnT", "la.attn", xn)
            after(pe, "la.attnT.sb")
            project(ps_o[:, 0:D], lambda c: xT[:, c, :], lambda c: la_wout[:, c, :]).then_inc(stage("la.out_ps"), 1)

            arrived(pe, "f0")
            pe.transpose(ps_ring[:, 512:512 + 8 * HT], bin_rows[0:8 * HT, :],
                         ident[0:8 * HT, 0:8 * HT]).then_inc(stage("f0.bias"), 1)
            turn_norm("f0.xT", "f0.xn", xn)
            after(pe, "f0.xT.sb")
            project(ps_o[:, 0:8], lambda c: xT[:, c, :], lambda c: wgate0[:, c, :]).then_inc(stage("f0.logits"), 1)
            experts("f0", 8, 0)

            turn_norm("xm.xT", "xm.affine", xm)
            arrived(pe, "x1big")
            arrived(pe, "x1")
            after(pe, "xm.xT.sb")
            for t in range(8):
                cut = slice(t * P, (t + 1) * P)
                project(ps_s[:, t * P:(t + 1) * P], lambda c: WQ1[:, c, cut], lambda c: xT[:, c, :])
                ins = project(ps_s[:, 1024 + t * P:1024 + (t + 1) * P], lambda c: WKV1[:, c, cut],
                              lambda c: xT[:, c, :])
            ins.then_inc(stage("x1.qkT"), 1)
            for g in range(2):
                ins = project(ps_o[:, g * 512:(g + 1) * 512], lambda c: xT[:, c, :],
                              lambda c: WKV1[:, c, 1024 + g * 512:1024 + (g + 1) * 512])
            for g in range(2):
                ins = project(ps_ring[:, g * 512:(g + 1) * 512], lambda c: xT[:, c, :],
                              lambda c: WQ1[:, c, g * 512:(g + 1) * 512])
            ins.then_inc(stage("x1.proj"), 1)
            after(pe, "x1.qT")
            after(pe, "x1.k_self")
            for t in range(8):
                for c in range(2):
                    n = c * 8 + t
                    ins = pe.matmul(ps_s[:, n * P:(n + 1) * P], qT[64 * c:64 * c + 64, t, :],
                                    k_self[64 * c:64 * c + 64, t, :], start=True, stop=True)
            ins.then_inc(stage("x1.self_scores"), 1)
            after(pe, "x1.self.exps")
            turn(wide_a, ps_s, HEADS).then_inc(stage("x1.turned"), 1)
            after(pe, "x1.turned.sb")
            after(pe, "x1.v_self")
            for h in range(HEADS):
                row0 = 64 * (h % 2)
                ins = pe.matmul(ps_o[row0:row0 + 64, (h // 2) * P:(h // 2 + 1) * P], v_self[:, h * 64:(h + 1) * 64],
                                wide_b[:, h * P:(h + 1) * P], start=True, stop=True)
            ins.then_inc(stage("x1.self_pv"), 1)
            after(pe, "x1.qx")
            for i in range(2 * HEADS):
                ins = pe.transpose(ps_s16[:, i * P:(i + 1) * P], qx[:, i * P:(i + 1) * P], ident16[:, :])
            ins.then_inc(stage("x1.qxT"), 1)
            after(pe, "x1.start")
            after(pe, "x1.q16")
            after(pe, "x1.w16")
            cross(L1)
            after(pe, "x1.rden")
            per_row(range(8), ps_s).then_inc(stage("x1.rden_rows"), 1)
            after(pe, "x1.done")
            project(ps_o[:, 0:D], lambda t: O[:, t * P:(t + 1) * P], lambda t: wo1[:, t, :],
                    8).then_inc(stage("x1.out"), 1)

            arrived(pe, "la1")
            for i, w in enumerate((la_wq, la_wk, la_wv, la_wout)):
                for c in range(DC):
                    for e in range(DC):
                        col = i * 512 + c * D + e * P
                        ins = pe.transpose(ps_s[:, col:col + P], w[:, e, c * P:(c + 1) * P], ident[:, :])
            ins.then_inc(stage("l1.wT"), 1)
            turn_norm("l1.xT", "l1.xn", xn)
            after(pe, "l1.wT.sb")
            after(pe, "l1.xT.sb")
            for e in range(DC):
                for i in range(2):
                    col = i * D + e * P
                    project(ps_s[:, col:col + P], lambda c: wT[:, i, c, e * P:(e + 1) * P], lambda c: xT[:, c, :])
            project(ps_s[:, 512:512 + D], lambda c: xT[:, c, :], lambda c: wT[:, 2, c, :]).then_inc(stage("l1.proj"), 1)
            after(pe, "l1.qz")
            for g in range(4):
                e = g // 2
                ins = pe.matmul(ps_s[:, g * 512:(g + 1) * 512], sp_z[:, D + e * P:D + (e + 1) * P],
                                kflat[:, g * 512:(g + 1) * 512], start=True, stop=True)
            ins.then_inc(stage("l1.scores"), 1)
            after(pe, "l1.causal")
            for h in range(HEADS):
                ins = pe.matmul(ps_o[:, h * 17:(h + 1) * 17], wide_a[:, h * P:(h + 1) * P], v_ext[:, h, :],
                                start=True, stop=True)
            ins.then_inc(stage("l1.pv"), 1)
            turn_norm("l1.attnT", "l1.attn", xn)
            after(pe, "l1.attnT.sb")
            project(ps_o[:, 512:512 + D], lambda c: xT[:, c, :], lambda c: wT[:, 3, c, :]).then_inc(stage("l1.out"), 1)

            arrived(pe, "f1")
            pe.transpose(ps_ring[:, 512:512 + P], b1_rows[:, :], ident[:, :]).then_inc(stage("f1.bias"), 1)
            turn_norm("f1.xT", "f1.xn", xn)
            after(pe, "f1.xT.sb")
            project(ps_o[:, 0:16], lambda c: xT[:, c, :], lambda c: wr1[:, c, :]).then_inc(stage("f1.logits"), 1)
            experts("f1", 16, 8)


_OUT_SHAPE = (1, P, D)


def kernel(**inputs):
    import concourse.bacc as _bacc
    from concourse.bass_utils import run_bass_kernel_spmd as _run

    nc = _bacc.Bacc("TRN2", target_bir_lowering=False, num_devices=1)
    arrays, args = {}, {}
    for name, value in inputs.items():
        v = np.ascontiguousarray(value)
        arrays[f"in_{name}_dram"] = v
        args[name] = nc.dram_tensor(f"in_{name}_dram", v.shape, mybir.dt.from_np(v.dtype), kind="ExternalInput").ap()
    out = nc.dram_tensor("out_0_dram", _OUT_SHAPE, FP32, kind="ExternalOutput").ap()
    perceiver(nc, args, out)
    r = _run(nc, [arrays], core_ids=[0])
    return r.results[0]["out_0_dram"]
```
